# Optimizing a Trainium2 kernel written in Bass

```python
import numpy as np
import jax
import jax.numpy as jnp

def _softmax(x, axis=-1):
    return jax.nn.softmax(x, axis=axis)

def _gelu(x):
    return jax.nn.gelu(x, approximate=True)

def _silu(x):
    return jax.nn.silu(x)

def _sigmoid(x):
    return jax.nn.sigmoid(x)

def _layernorm(x, axis=-1, eps=1e-05):
    m = jnp.mean(x, axis=axis, keepdims=True)
    v = jnp.var(x, axis=axis, keepdims=True)
    return (x - m) / jnp.sqrt(v + eps)

def _scatter_add(tgt, idx, src, axis=0):
    return tgt.at[idx].add(src)

def _segment_sum(src, seg, n):
    return jax.ops.segment_sum(src, seg, n)
kernel_name = 'mk_xattn_ffn_d2_seqx_r4_c04e23'

def setup_inputs(seed: int=0):
    np.random.seed(seed)
    _w = jnp.asarray

    def _rec_inputs():
        import jax
        import jax.numpy as jnp
        _rk = jax.random.key(seed)
        x = -0.0003929 + 0.9999 * jax.random.normal(jax.random.fold_in(_rk, 1), (1, 2048, 256), jnp.float32)
        _lenS = 2048 - jax.random.randint(jax.random.fold_in(_rk, 7), (1,), 0, max(1, 2048 // 4) + 1, jnp.int32)
        _lenS2 = 1601 - jax.random.randint(jax.random.fold_in(_rk, 8), (1,), 0, max(1, 1601 // 4) + 1, jnp.int32)
        _ctx_512P = jax.random.normal(jax.random.fold_in(_rk, 11), (1, 16, 128), jnp.float32)
        _ctx_512c = jax.random.dirichlet(jax.random.fold_in(_rk, 511), 0.3 * jnp.ones((16,), jnp.float32), (1, 1601))
        _ctx_512t = jnp.einsum('bsk,bkd->bsd', _ctx_512c, _ctx_512P)
        _ctx_512t = _ctx_512t * jax.lax.rsqrt(jnp.mean(jnp.square(_ctx_512t)) + 1e-12) * 0.953939
        ctx_512 = -1.39393e-06 + 0.999914 * (_ctx_512t + 0.3 * jax.random.normal(jax.random.fold_in(_rk, 611), (1, 1601, 128), jnp.float32))
        return (x, ctx_512)
    x, ctx_512 = _rec_inputs()

    def _L0_xattn_setup():
        import jax, jax.numpy as jnp
        import numpy as np
        HEADS = 16
        D_MODEL = 256
        IMG_MODEL = 128
        D_K = D_MODEL // HEADS
        key = jax.random.key(seed)
        ks = jax.random.split(key, 12)
        B, LQ, LKV = (8, 512, 256)
        s_dm = 1.0 / np.sqrt(D_MODEL)
        s_im = 1.0 / np.sqrt(IMG_MODEL)
        return {'q': jax.random.normal(ks[0], (B, LQ, D_MODEL), jnp.float32), 'k': jax.random.normal(ks[1], (B, LKV, IMG_MODEL), jnp.float32), 'v': jax.random.normal(ks[2], (B, LKV, IMG_MODEL), jnp.float32), 'Wq': jax.random.normal(ks[3], (D_MODEL, D_MODEL), jnp.float32) * s_dm, 'bq': jnp.zeros((D_MODEL,), jnp.float32), 'Wk': jax.random.normal(ks[4], (IMG_MODEL, D_MODEL), jnp.float32) * s_im, 'bk': jnp.zeros((D_MODEL,), jnp.float32), 'Wv': jax.random.normal(ks[5], (IMG_MODEL, D_MODEL), jnp.float32) * s_im, 'bv': jnp.zeros((D_MODEL,), jnp.float32), 'Wo': jax.random.normal(ks[6], (D_MODEL, D_MODEL), jnp.float32) * s_dm, 'bo': jnp.zeros((D_MODEL,), jnp.float32)}
    _L0_xattn_all = _L0_xattn_setup()
    _L0_xattn_in = {k: v for k, v in _L0_xattn_all.items() if k in ('Wq', 'bq', 'Wk', 'bk', 'Wv', 'bv', 'Wo', 'bo')}
    del _L0_xattn_all

    def _L0_ffn_setup():
        import jax, jax.numpy as jnp
        import numpy as np
        E, G, TOPK = (32, 16, 2)
        HID, INTER, A_INTER = (256, 512, 128)
        CAP_FACTOR = 1.25
        SCALE = 0.05

        def _stats(x):
            mean = x.mean(-1, keepdims=True)
            std = jnp.std(x, axis=-1, keepdims=True, ddof=1)
            mn = x.min(-1, keepdims=True)
            mx = x.max(-1, keepdims=True)
            l2 = jnp.linalg.norm(x, axis=-1, keepdims=True)
            sp = (jnp.abs(x) < 1e-06).astype(x.dtype).mean(-1, keepdims=True)
            return jnp.concatenate([mean, std, mn, mx, l2, sp], -1)
        key = jax.random.key(seed)
        ks = jax.random.split(key, 8)
        B, N = (4, 256)
        s = lambda k, shape, sc: jax.random.normal(k, shape, jnp.float32) * sc
        return {'x': jax.random.normal(ks[0], (B, N, HID), jnp.float32), 'r1_w': s(ks[1], (HID // 2, HID + 6), 0.02), 'r1_b': jnp.zeros((HID // 2,), jnp.float32), 'r2_w': s(ks[2], (E, HID // 2), 0.02), 'w_up': s(ks[3], (E, 2 * INTER, HID), 0.02), 'w_down': s(ks[4], (E, HID, INTER), 0.02), 'a_up': s(ks[5], (G, 2 * A_INTER, HID), 0.02), 'a_down': s(ks[6], (G, HID, A_INTER), 0.02)}
    _L0_ffn_all = _L0_ffn_setup()
    _L0_ffn_in = {k: v for k, v in _L0_ffn_all.items() if k in ('r1_w', 'r1_b', 'r2_w', 'w_up', 'w_down', 'a_up', 'a_down')}
    del _L0_ffn_all

    def _L1_xattn_setup():
        import jax, jax.numpy as jnp
        import numpy as np
        H, D, C1, C2, S, M, B, W = (16, 32, 256, 128, 512, 128, 2, 4)

        def _ln(x, g, b):
            m = jnp.mean(x, -1, keepdims=True)
            v = jnp.var(x, -1, keepdims=True)
            return (x - m) * jax.lax.rsqrt(v + 1e-05) * g + b

        def _mha(x, y, wq, wk, wv, li1_w, li1_b, lnx_g, lnx_b, lny_g, lny_b, ln3_g, ln3_b, li2_w, li2_b, li3_w, li3_b, causal):
            xn = _ln(x, lnx_g, lnx_b)
            yn = _ln(y, lny_g, lny_b)
            q = jnp.einsum('bsc,hcd->bhsd', xn, wq)
            k = jnp.einsum('btc,hcd->bhtd', yn, wk)
            v = jnp.einsum('btc,hcd->bhtd', yn, wv)
            a = jax.nn.softmax(jnp.einsum('bhsd,bhtd->bhst', q, k) * D ** (-0.5), axis=-1)
            if causal:
                s, t = (a.shape[-2], a.shape[-1])
                mask = (jnp.arange(t)[None, :] > jnp.arange(s)[:, None]).astype(a.dtype)
                a = a * mask
            o = jnp.einsum('bhst,bhtd->bhsd', a, v)
            o = o.transpose(0, 2, 1, 3).reshape(x.shape[0], x.shape[1], H * D)
            x_out = x + o @ li1_w + li1_b
            h = jax.nn.gelu(_ln(x_out, ln3_g, ln3_b) @ li2_w + li2_b, approximate=False)
            return x_out + h @ li3_w + li3_b
        key = jax.random.key(seed)
        ks = iter(jax.random.split(key, 64))

        def w(shape, scale=0.02):
            return jax.random.normal(next(ks), shape, jnp.float32) * scale
        inp = {'xx': jax.random.normal(next(ks), (B, S, C1), jnp.float32), 'ee': jax.random.normal(next(ks), (B, M, C2), jnp.float32), 'ln1_g': jnp.ones(C1, jnp.float32), 'ln1_b': jnp.zeros(C1, jnp.float32), 'ln2_g': jnp.ones(C1, jnp.float32), 'ln2_b': jnp.zeros(C1, jnp.float32)}
        for pfx, cy in (('a1', C1), ('a2', C2)):
            inp[pfx + '_wq'] = w((H, C1, D))
            inp[pfx + '_wk'] = w((H, cy, D))
            inp[pfx + '_wv'] = w((H, cy, D))
            inp[pfx + '_li1_w'] = w((H * D, C1))
            inp[pfx + '_li1_b'] = jnp.zeros(C1, jnp.float32)
            inp[pfx + '_lnx_g'] = jnp.ones(C1, jnp.float32)
            inp[pfx + '_lnx_b'] = jnp.zeros(C1, jnp.float32)
            inp[pfx + '_lny_g'] = jnp.ones(cy, jnp.float32)
            inp[pfx + '_lny_b'] = jnp.zeros(cy, jnp.float32)
            inp[pfx + '_ln3_g'] = jnp.ones(C1, jnp.float32)
            inp[pfx + '_ln3_b'] = jnp.zeros(C1, jnp.float32)
            inp[pfx + '_li2_w'] = w((C1, C1 * W))
            inp[pfx + '_li2_b'] = jnp.zeros(C1 * W, jnp.float32)
            inp[pfx + '_li3_w'] = w((C1 * W, C1))
            inp[pfx + '_li3_b'] = jnp.zeros(C1, jnp.float32)
        inp['training'] = 0
        return inp
    _L1_xattn_all = _L1_xattn_setup()
    _L1_xattn_in = {k: v for k, v in _L1_xattn_all.items() if k in ('ln1_g', 'ln1_b', 'ln2_g', 'ln2_b', 'a1_wq', 'a1_wk', 'a1_wv', 'a1_li1_w', 'a1_li1_b', 'a1_lnx_g', 'a1_lnx_b', 'a1_lny_g', 'a1_lny_b', 'a1_ln3_g', 'a1_ln3_b', 'a1_li2_w', 'a1_li2_b', 'a1_li3_w', 'a1_li3_b', 'a2_wq', 'a2_wk', 'a2_wv', 'a2_li1_w', 'a2_li1_b', 'a2_lnx_g', 'a2_lnx_b', 'a2_lny_g', 'a2_lny_b', 'a2_ln3_g', 'a2_ln3_b', 'a2_li2_w', 'a2_li2_b', 'a2_li3_w', 'a2_li3_b')}
    del _L1_xattn_all

    def _L1_ffn_setup():
        import jax, jax.numpy as jnp
        import numpy as np
        E = 16
        K = 4
        G = 4
        TG = 2
        NS = 2
        H = 256
        I = 352
        SCALE = 1.0

        def _gate(x2d, gate_w, gate_bias):
            T = x2d.shape[0]
            logits = x2d.astype(jnp.float32) @ gate_w.astype(jnp.float32).T
            scores = jax.nn.sigmoid(logits)
            sfc = scores + gate_bias[None, :]
            grp = sfc.reshape(T, G, E // G)
            top2, _ = jax.lax.top_k(grp, 2)
            group_scores = top2.sum(-1)
            _, gidx = jax.lax.top_k(group_scores, TG)
            gmask = jnp.zeros((T, G), sfc.dtype).at[jnp.arange(T)[:, None], gidx].set(1.0)
            smask = jnp.repeat(gmask, E // G, axis=1) > 0
            tmp = jnp.where(smask, sfc, 0.0)
            _, topk_idx = jax.lax.top_k(tmp, K)
            topk_w = jnp.take_along_axis(scores, topk_idx, axis=1)
            topk_w = topk_w / (topk_w.sum(-1, keepdims=True) + 1e-20)
            return (topk_idx, topk_w * SCALE)
        key = jax.random.key(seed)
        ks = jax.random.split(key, 8)
        bound = 1.0 / np.sqrt(H)
        return {'hidden_states': jax.random.normal(ks[0], (1, 256, H), jnp.float32), 'gate_w': jax.random.uniform(ks[1], (E, H), jnp.float32, -bound, bound), 'gate_bias': jnp.zeros((E,), jnp.float32), 'gate_proj': jax.random.normal(ks[2], (E, I, H), jnp.float32) * 0.02, 'up_proj': jax.random.normal(ks[3], (E, I, H), jnp.float32) * 0.02, 'down_proj': jax.random.normal(ks[4], (E, H, I), jnp.float32) * 0.02, 'shared_gate_w': jax.random.normal(ks[5], (I * NS, H), jnp.float32) * 0.02, 'shared_up_w': jax.random.normal(ks[6], (I * NS, H), jnp.float32) * 0.02, 'shared_down_w': jax.random.normal(ks[7], (H, I * NS), jnp.float32) * 0.02}
    _L1_ffn_all = _L1_ffn_setup()
    _L1_ffn_in = {k: v for k, v in _L1_ffn_all.items() if k in ('gate_w', 'gate_bias', 'gate_proj', 'up_proj', 'down_proj', 'shared_gate_w', 'shared_up_w', 'shared_down_w')}
    del _L1_ffn_all
    return {'x': x, 'ctx_512': ctx_512, 'L0_xattn_Wq': _L0_xattn_in['Wq'], 'L0_xattn_bq': _L0_xattn_in['bq'], 'L0_xattn_Wk': _L0_xattn_in['Wk'], 'L0_xattn_bk': _L0_xattn_in['bk'], 'L0_xattn_Wv': _L0_xattn_in['Wv'], 'L0_xattn_bv': _L0_xattn_in['bv'], 'L0_xattn_Wo': _L0_xattn_in['Wo'], 'L0_xattn_bo': _L0_xattn_in['bo'], 'L0_ffn_r1_w': _L0_ffn_in['r1_w'], 'L0_ffn_r1_b': _L0_ffn_in['r1_b'], 'L0_ffn_r2_w': _L0_ffn_in['r2_w'], 'L0_ffn_w_up': _L0_ffn_in['w_up'], 'L0_ffn_w_down': _L0_ffn_in['w_down'], 'L0_ffn_a_up': _L0_ffn_in['a_up'], 'L0_ffn_a_down': _L0_ffn_in['a_down'], 'L1_xattn_ln1_g': _L1_xattn_in['ln1_g'], 'L1_xattn_ln1_b': _L1_xattn_in['ln1_b'], 'L1_xattn_ln2_g': _L1_xattn_in['ln2_g'], 'L1_xattn_ln2_b': _L1_xattn_in['ln2_b'], 'L1_xattn_a1_wq': _L1_xattn_in['a1_wq'], 'L1_xattn_a1_wk': _L1_xattn_in['a1_wk'], 'L1_xattn_a1_wv': _L1_xattn_in['a1_wv'], 'L1_xattn_a1_li1_w': _L1_xattn_in['a1_li1_w'], 'L1_xattn_a1_li1_b': _L1_xattn_in['a1_li1_b'], 'L1_xattn_a1_lnx_g': _L1_xattn_in['a1_lnx_g'], 'L1_xattn_a1_lnx_b': _L1_xattn_in['a1_lnx_b'], 'L1_xattn_a1_lny_g': _L1_xattn_in['a1_lny_g'], 'L1_xattn_a1_lny_b': _L1_xattn_in['a1_lny_b'], 'L1_xattn_a1_ln3_g': _L1_xattn_in['a1_ln3_g'], 'L1_xattn_a1_ln3_b': _L1_xattn_in['a1_ln3_b'], 'L1_xattn_a1_li2_w': _L1_xattn_in['a1_li2_w'], 'L1_xattn_a1_li2_b': _L1_xattn_in['a1_li2_b'], 'L1_xattn_a1_li3_w': _L1_xattn_in['a1_li3_w'], 'L1_xattn_a1_li3_b': _L1_xattn_in['a1_li3_b'], 'L1_xattn_a2_wq': _L1_xattn_in['a2_wq'], 'L1_xattn_a2_wk': _L1_xattn_in['a2_wk'], 'L1_xattn_a2_wv': _L1_xattn_in['a2_wv'], 'L1_xattn_a2_li1_w': _L1_xattn_in['a2_li1_w'], 'L1_xattn_a2_li1_b': _L1_xattn_in['a2_li1_b'], 'L1_xattn_a2_lnx_g': _L1_xattn_in['a2_lnx_g'], 'L1_xattn_a2_lnx_b': _L1_xattn_in['a2_lnx_b'], 'L1_xattn_a2_lny_g': _L1_xattn_in['a2_lny_g'], 'L1_xattn_a2_lny_b': _L1_xattn_in['a2_lny_b'], 'L1_xattn_a2_ln3_g': _L1_xattn_in['a2_ln3_g'], 'L1_xattn_a2_ln3_b': _L1_xattn_in['a2_ln3_b'], 'L1_xattn_a2_li2_w': _L1_xattn_in['a2_li2_w'], 'L1_xattn_a2_li2_b': _L1_xattn_in['a2_li2_b'], 'L1_xattn_a2_li3_w': _L1_xattn_in['a2_li3_w'], 'L1_xattn_a2_li3_b': _L1_xattn_in['a2_li3_b'], 'L1_ffn_gate_w': _L1_ffn_in['gate_w'], 'L1_ffn_gate_bias': _L1_ffn_in['gate_bias'], 'L1_ffn_gate_proj': _L1_ffn_in['gate_proj'], 'L1_ffn_up_proj': _L1_ffn_in['up_proj'], 'L1_ffn_down_proj': _L1_ffn_in['down_proj'], 'L1_ffn_shared_gate_w': _L1_ffn_in['shared_gate_w'], 'L1_ffn_shared_up_w': _L1_ffn_in['shared_up_w'], 'L1_ffn_shared_down_w': _L1_ffn_in['shared_down_w']}

def reference(x, ctx_512, L0_xattn_Wq, L0_xattn_bq, L0_xattn_Wk, L0_xattn_bk, L0_xattn_Wv, L0_xattn_bv, L0_xattn_Wo, L0_xattn_bo, L0_ffn_r1_w, L0_ffn_r1_b, L0_ffn_r2_w, L0_ffn_w_up, L0_ffn_w_down, L0_ffn_a_up, L0_ffn_a_down, L1_xattn_ln1_g, L1_xattn_ln1_b, L1_xattn_ln2_g, L1_xattn_ln2_b, L1_xattn_a1_wq, L1_xattn_a1_wk, L1_xattn_a1_wv, L1_xattn_a1_li1_w, L1_xattn_a1_li1_b, L1_xattn_a1_lnx_g, L1_xattn_a1_lnx_b, L1_xattn_a1_lny_g, L1_xattn_a1_lny_b, L1_xattn_a1_ln3_g, L1_xattn_a1_ln3_b, L1_xattn_a1_li2_w, L1_xattn_a1_li2_b, L1_xattn_a1_li3_w, L1_xattn_a1_li3_b, L1_xattn_a2_wq, L1_xattn_a2_wk, L1_xattn_a2_wv, L1_xattn_a2_li1_w, L1_xattn_a2_li1_b, L1_xattn_a2_lnx_g, L1_xattn_a2_lnx_b, L1_xattn_a2_lny_g, L1_xattn_a2_lny_b, L1_xattn_a2_ln3_g, L1_xattn_a2_ln3_b, L1_xattn_a2_li2_w, L1_xattn_a2_li2_b, L1_xattn_a2_li3_w, L1_xattn_a2_li3_b, L1_ffn_gate_w, L1_ffn_gate_bias, L1_ffn_gate_proj, L1_ffn_up_proj, L1_ffn_down_proj, L1_ffn_shared_gate_w, L1_ffn_shared_up_w, L1_ffn_shared_down_w):
    import jax
    import jax.numpy as jnp

    def _L0_xattn_ref(q, k, v, Wq, bq, Wk, bk, Wv, bv, Wo, bo):
        import jax, jax.numpy as jnp
        import numpy as np
        HEADS = 16
        D_MODEL = 256
        IMG_MODEL = 128
        D_K = D_MODEL // HEADS
        B, LQ, _ = q.shape
        LKV = k.shape[1]
        qh = (q @ Wq + bq).reshape(B, LQ, HEADS, D_K).transpose(0, 2, 1, 3)
        kh = (k @ Wk + bk).reshape(B, LKV, HEADS, D_K).transpose(0, 2, 1, 3)
        vh = (v @ Wv + bv).reshape(B, LKV, HEADS, D_K).transpose(0, 2, 1, 3)
        scale = 1.0 / np.sqrt(D_K)
        scores = jnp.einsum('bhqd,bhkd->bhqk', qh, kh) * scale
        attn = jax.nn.softmax(scores, axis=-1)
        out = jnp.einsum('bhqk,bhkd->bhqd', attn, vh)
        concat = out.transpose(0, 2, 1, 3).reshape(B, LQ, D_MODEL)
        return concat @ Wo + bo

    def _L0_ffn_ref(x, r1_w, r1_b, r2_w, w_up, w_down, a_up, a_down):
        import jax, jax.numpy as jnp
        import numpy as np
        E, G, TOPK = (32, 16, 2)
        HID, INTER, A_INTER = (256, 512, 128)
        CAP_FACTOR = 1.25
        SCALE = 0.05

        def _stats(x):
            mean = x.mean(-1, keepdims=True)
            std = jnp.std(x, axis=-1, keepdims=True, ddof=1)
            mn = x.min(-1, keepdims=True)
            mx = x.max(-1, keepdims=True)
            l2 = jnp.linalg.norm(x, axis=-1, keepdims=True)
            sp = (jnp.abs(x) < 1e-06).astype(x.dtype).mean(-1, keepdims=True)
            return jnp.concatenate([mean, std, mn, mx, l2, sp], -1)
        B, N, C = x.shape
        xf = x.reshape(-1, C)
        T = xf.shape[0]
        cap = int(CAP_FACTOR * T / E)
        ri = jnp.concatenate([xf, _stats(xf)], -1)
        h = jax.nn.gelu(ri @ r1_w.T + r1_b, approximate=False)
        probs = jax.nn.softmax(h @ r2_w.T, -1)
        topp, topi = jax.lax.top_k(probs, TOPK)
        wnorm = topp / topp.sum(-1, keepdims=True)
        eids = jnp.arange(E)
        hit = topi[..., None] == eids
        routed = hit.any(1)
        Wc = jnp.where(hit, wnorm[..., None], 0.0).sum(1)
        score = jnp.where(routed, probs, -jnp.inf)
        idx = jnp.argsort(-score, axis=0)[:cap].T
        valid = jnp.take_along_axis(routed.T, idx, 1)
        w = jnp.take_along_axis(Wc.T, idx, 1) * valid
        xe = xf[idx]
        up = jnp.einsum('eci,eji->ecj', xe, w_up)
        gate, upv = jnp.split(up, 2, axis=-1)
        hact = jax.nn.silu(gate) * upv
        ye = jnp.einsum('ecj,eoj->eco', hact, w_down)
        out = jnp.zeros((T, C), xf.dtype).at[idx.reshape(-1)].add((w[..., None] * ye).reshape(-1, C))
        Wmask = jnp.zeros((T, E), xf.dtype).at[idx, eids[:, None]].add(w)
        gw = SCALE * Wmask.reshape(T, G, E // G).sum(-1)
        aup = jnp.einsum('tc,gjc->tgj', xf, a_up)
        ag, av = jnp.split(aup, 2, axis=-1)
        ah = jax.nn.silu(ag) * av
        ay = jnp.einsum('tgj,goj->tgo', ah, a_down)
        out = out + jnp.einsum('tg,tgo->to', gw, ay)
        return out.reshape(B, N, C)

    def _L1_xattn_ref(xx, ee, ln1_g, ln1_b, ln2_g, ln2_b, a1_wq, a1_wk, a1_wv, a1_li1_w, a1_li1_b, a1_lnx_g, a1_lnx_b, a1_lny_g, a1_lny_b, a1_ln3_g, a1_ln3_b, a1_li2_w, a1_li2_b, a1_li3_w, a1_li3_b, a2_wq, a2_wk, a2_wv, a2_li1_w, a2_li1_b, a2_lnx_g, a2_lnx_b, a2_lny_g, a2_lny_b, a2_ln3_g, a2_ln3_b, a2_li2_w, a2_li2_b, a2_li3_w, a2_li3_b, training):
        import jax, jax.numpy as jnp
        import numpy as np
        H, D, C1, C2, S, M, B, W = (16, 32, 256, 128, 512, 128, 2, 4)

        def _ln(x, g, b):
            m = jnp.mean(x, -1, keepdims=True)
            v = jnp.var(x, -1, keepdims=True)
            return (x - m) * jax.lax.rsqrt(v + 1e-05) * g + b

        def _mha(x, y, wq, wk, wv, li1_w, li1_b, lnx_g, lnx_b, lny_g, lny_b, ln3_g, ln3_b, li2_w, li2_b, li3_w, li3_b, causal):
            xn = _ln(x, lnx_g, lnx_b)
            yn = _ln(y, lny_g, lny_b)
            q = jnp.einsum('bsc,hcd->bhsd', xn, wq)
            k = jnp.einsum('btc,hcd->bhtd', yn, wk)
            v = jnp.einsum('btc,hcd->bhtd', yn, wv)
            a = jax.nn.softmax(jnp.einsum('bhsd,bhtd->bhst', q, k) * D ** (-0.5), axis=-1)
            if causal:
                s, t = (a.shape[-2], a.shape[-1])
                mask = (jnp.arange(t)[None, :] > jnp.arange(s)[:, None]).astype(a.dtype)
                a = a * mask
            o = jnp.einsum('bhst,bhtd->bhsd', a, v)
            o = o.transpose(0, 2, 1, 3).reshape(x.shape[0], x.shape[1], H * D)
            x_out = x + o @ li1_w + li1_b
            h = jax.nn.gelu(_ln(x_out, ln3_g, ln3_b) @ li2_w + li2_b, approximate=False)
            return x_out + h @ li3_w + li3_b
        x = _ln(xx, ln1_g, ln1_b)
        x = x + _mha(x, x, a1_wq, a1_wk, a1_wv, a1_li1_w, a1_li1_b, a1_lnx_g, a1_lnx_b, a1_lny_g, a1_lny_b, a1_ln3_g, a1_ln3_b, a1_li2_w, a1_li2_b, a1_li3_w, a1_li3_b, causal=True)
        x = _ln(x, ln2_g, ln2_b)
        return x + _mha(x, ee, a2_wq, a2_wk, a2_wv, a2_li1_w, a2_li1_b, a2_lnx_g, a2_lnx_b, a2_lny_g, a2_lny_b, a2_ln3_g, a2_ln3_b, a2_li2_w, a2_li2_b, a2_li3_w, a2_li3_b, causal=False)

    def _L1_ffn_ref(hidden_states, gate_w, gate_bias, gate_proj, up_proj, down_proj, shared_gate_w, shared_up_w, shared_down_w):
        import jax, jax.numpy as jnp
        import numpy as np
        E = 16
        K = 4
        G = 4
        TG = 2
        NS = 2
        H = 256
        I = 352
        SCALE = 1.0

        def _gate(x2d, gate_w, gate_bias):
            T = x2d.shape[0]
            logits = x2d.astype(jnp.float32) @ gate_w.astype(jnp.float32).T
            scores = jax.nn.sigmoid(logits)
            sfc = scores + gate_bias[None, :]
            grp = sfc.reshape(T, G, E // G)
            top2, _ = jax.lax.top_k(grp, 2)
            group_scores = top2.sum(-1)
            _, gidx = jax.lax.top_k(group_scores, TG)
            gmask = jnp.zeros((T, G), sfc.dtype).at[jnp.arange(T)[:, None], gidx].set(1.0)
            smask = jnp.repeat(gmask, E // G, axis=1) > 0
            tmp = jnp.where(smask, sfc, 0.0)
            _, topk_idx = jax.lax.top_k(tmp, K)
            topk_w = jnp.take_along_axis(scores, topk_idx, axis=1)
            topk_w = topk_w / (topk_w.sum(-1, keepdims=True) + 1e-20)
            return (topk_idx, topk_w * SCALE)
        orig_shape = hidden_states.shape
        x = hidden_states.reshape(-1, H)
        topk_idx, topk_w = _gate(x, gate_w, gate_bias)
        combine_w = (jax.nn.one_hot(topk_idx, E, dtype=x.dtype) * topk_w[..., None]).sum(1)
        g = jnp.einsum('th,eih->tei', x, gate_proj)
        u = jnp.einsum('th,eih->tei', x, up_proj)
        act = jax.nn.silu(g) * u
        y = jnp.einsum('tei,ehi,te->th', act, down_proj, combine_w)
        sg = x @ shared_gate_w.T
        su = x @ shared_up_w.T
        y = y + jax.nn.silu(sg) * su @ shared_down_w.T
        return y.reshape(orig_shape)
    x = x + _L0_xattn_ref(_layernorm(x, axis=-1), ctx_512, ctx_512, L0_xattn_Wq, L0_xattn_bq, L0_xattn_Wk, L0_xattn_bk, L0_xattn_Wv, L0_xattn_bv, L0_xattn_Wo, L0_xattn_bo)
    x = x + _L0_ffn_ref(_layernorm(x, axis=-1), L0_ffn_r1_w, L0_ffn_r1_b, L0_ffn_r2_w, L0_ffn_w_up, L0_ffn_w_down, L0_ffn_a_up, L0_ffn_a_down)
    x = x + _L1_xattn_ref(_layernorm(x, axis=-1), ctx_512, L1_xattn_ln1_g, L1_xattn_ln1_b, L1_xattn_ln2_g, L1_xattn_ln2_b, L1_xattn_a1_wq, L1_xattn_a1_wk, L1_xattn_a1_wv, L1_xattn_a1_li1_w, L1_xattn_a1_li1_b, L1_xattn_a1_lnx_g, L1_xattn_a1_lnx_b, L1_xattn_a1_lny_g, L1_xattn_a1_lny_b, L1_xattn_a1_ln3_g, L1_xattn_a1_ln3_b, L1_xattn_a1_li2_w, L1_xattn_a1_li2_b, L1_xattn_a1_li3_w, L1_xattn_a1_li3_b, L1_xattn_a2_wq, L1_xattn_a2_wk, L1_xattn_a2_wv, L1_xattn_a2_li1_w, L1_xattn_a2_li1_b, L1_xattn_a2_lnx_g, L1_xattn_a2_lnx_b, L1_xattn_a2_lny_g, L1_xattn_a2_lny_b, L1_xattn_a2_ln3_g, L1_xattn_a2_ln3_b, L1_xattn_a2_li2_w, L1_xattn_a2_li2_b, L1_xattn_a2_li3_w, L1_xattn_a2_li3_b, 0)
    x = x + _L1_ffn_ref(_layernorm(x, axis=-1), L1_ffn_gate_w, L1_ffn_gate_bias, L1_ffn_gate_proj, L1_ffn_up_proj, L1_ffn_down_proj, L1_ffn_shared_gate_w, L1_ffn_shared_up_w, L1_ffn_shared_down_w)
    return x

_drawn_inputs = setup_inputs


def setup_inputs(seed=0):
    import zlib

    import numpy as np

    out = dict(_drawn_inputs(seed))
    spreads = {'L0_xattn_bq': (0.0, 0.347),
     'L0_xattn_bk': (0.0, 0.8),
     'L0_xattn_bv': (0.0, 0.1),
     'L0_xattn_bo': (0.0, 0.1),
     'L0_ffn_r1_b': (0.0, 0.8),
     'L1_xattn_ln1_g': (1.0, 0.2),
     'L1_xattn_ln1_b': (0.0, 0.1),
     'L1_xattn_ln2_g': (1.0, 0.2),
     'L1_xattn_ln2_b': (0.0, 0.1),
     'L1_xattn_a1_li1_b': (0.0, 0.278),
     'L1_xattn_a1_lnx_g': (1.0, 0.6),
     'L1_xattn_a1_lnx_b': (0.0, 0.8),
     'L1_xattn_a1_lny_g': (1.0, 0.6),
     'L1_xattn_a1_lny_b': (0.0, 0.8),
     'L1_xattn_a1_ln3_g': (1.0, 0.6),
     'L1_xattn_a1_ln3_b': (0.0, 0.8),
     'L1_xattn_a1_li2_b': (0.0, 0.707),
     'L1_xattn_a1_li3_b': (0.0, 0.1),
     'L1_xattn_a2_li1_b': (0.0, 0.1),
     'L1_xattn_a2_lnx_g': (1.0, 0.6),
     'L1_xattn_a2_lnx_b': (0.0, 0.8),
     'L1_xattn_a2_lny_g': (1.0, 0.6),
     'L1_xattn_a2_lny_b': (0.0, 0.8),
     'L1_xattn_a2_ln3_g': (1.0, 0.6),
     'L1_xattn_a2_ln3_b': (0.0, 0.8),
     'L1_xattn_a2_li2_b': (0.0, 0.708),
     'L1_xattn_a2_li3_b': (0.0, 0.1),
     'L1_ffn_gate_bias': (0.0, 0.8)}
    factors = {'L0_ffn_r1_w': 7.559,
     'L0_ffn_r2_w': 7.333,
     'L0_ffn_w_up': 7.859,
     'L0_ffn_w_down': 7.834,
     'L0_ffn_a_up': 8.0,
     'L0_ffn_a_down': 8.0,
     'L1_xattn_a1_wq': 8.0,
     'L1_xattn_a1_wk': 8.0,
     'L1_xattn_a1_wv': 4.711,
     'L1_xattn_a1_li1_w': 4.766,
     'L1_xattn_a2_wq': 8.0,
     'L1_xattn_a2_wk': 8.0,
     'L1_xattn_a2_wv': 3.162,
     'L1_xattn_a2_li1_w': 3.333,
     'L1_ffn_gate_w': 8.0,
     'L1_ffn_gate_proj': 8.0,
     'L1_ffn_up_proj': 8.0,
     'L1_ffn_down_proj': 8.0,
     'L1_ffn_shared_gate_w': 6.363,
     'L1_ffn_shared_up_w': 6.409,
     'L1_ffn_shared_down_w': 6.317}
    for name, (base, spread) in spreads.items():
        noise = np.random.default_rng([zlib.crc32(name.encode()), seed]).standard_normal(out[name].shape)
        drawn = base * np.exp(spread * noise) if base else spread * noise
        out[name] = jnp.asarray(drawn.astype(out[name].dtype))
    for name, factor in factors.items():
        out[name] = (out[name] * factor).astype(out[name].dtype)
    return out
```

```python
from collections import deque
from contextlib import ExitStack

import numpy as np
import concourse.bass as bass
from concourse import mybir

F32 = mybir.dt.float32
F16 = mybir.dt.float16
U32 = mybir.dt.uint32
ALU = mybir.AluOpType
ACT = mybir.ActivationFunctionType
AX = mybir.AxisListType

P = 128
T = 2048
D = 256
S = 1601
C = 128
NT = T // P
KC = D // P
CH = 512
NCH = T // CH
TPC = CH // P
HEADS = 16
HG = 4
NG = HEADS // HG
SLOT = 32
STACK = 3 * SLOT
EPS = 1e-5

E0, CAP, INTER, AG, AI = 32, 80, 512, 16, 128
NSTAT = 6
ROW = D + E0
E1, EI, SH, TOPK1, G1, TG1 = 16, 352, 2, 4, 4, 2
FF = 1024

COLS, ROWS = {}, {}
_at = 0
for _n, _k in (("bq0", NG), ("bk0", NG), ("r1b", 1),
               ("a1_lnx_g", 2), ("a1_lnx_b", 2), ("a1_lny_g", 2), ("a1_lny_b", 2), ("a1_ln3_g", 2), ("a1_ln3_b", 2),
               ("a1_li2_b", 8),
               ("a2_lnx_g", 2), ("a2_lnx_b", 2), ("a2_lny_g", 1), ("a2_lny_b", 1), ("a2_ln3_g", 2), ("a2_ln3_b", 2),
               ("a2_li2_b", 8)):
    COLS[_n] = (_at, _k)
    _at += _k
NCOLS = _at
_at = 0
for _n, _k in (("bo0", D), ("ln1_g", D), ("ln1_b", D), ("ln2_g", D), ("ln2_b", D), ("a1_li1_b", D), ("a1_li3_b", D),
               ("a2_li1_b", D), ("a2_li3_b", D), ("gate_bias", E1), ("bv0", NG * P)):
    ROWS[_n] = (_at, _k)
    _at += _k
NROWS = _at


def tiles_of(n):
    return [min(P, n - P * t) for t in range((n + P - 1) // P)]


def chunks_of(n):
    return [(CH * c, min(CH, n - CH * c)) for c in range((n + CH - 1) // CH)]


FREE_SEMS = deque()


def phase(nc, name):
    ctx = ExitStack()
    sems = []

    def clear():
        nc.clear_and_free_semaphores(sems)
        FREE_SEMS.extend(s.num for s in sems)

    ctx.callback(clear)

    def sb(n, shape, dt=F32):
        return ctx.enter_context(nc.sbuf_tensor(f"{name}_{n}", shape, dt))

    def ps(n, shape, dt=F32):
        return ctx.enter_context(nc.psum_tensor(f"{name}_{n}", shape, dt))

    def sem(n):
        sems.append(nc.alloc_semaphore(f"{name}_{n}", FREE_SEMS.popleft()))
        return sems[-1]

    return ctx, sb, ps, sem


def load_constants(nc, a, cols, rows, ident, ones, x_sb):
    ctx, sb, ps, sem = phase(nc, "init")
    with ctx:
        loaded, zeroed, made = sem("loaded"), sem("zeroed"), sem("made")
        block = ctx.enter_context(nc.Block())

        @block.sync
        def _(sp):
            sp.dma_start(cols[:, :], a["cols"]).then_inc(loaded, 16)
            sp.dma_start(rows[:, :], a["rows"].partition_broadcast(P).rearrange("p o n -> p (o n)")).then_inc(loaded, 16)
            sp.dma_start(x_sb[:, :, :], a["x"].rearrange("o (t p) d -> p (o t) d", p=P)).then_inc(loaded, 16)
            sp.wait_ge(loaded, 48)

        @block.gpsimd
        def _(pool):
            pool.memset(ident[:, :], 0.0).then_inc(zeroed, 1)
            pool.memset(ones[:, :], 1.0)
            pool.wait_ge(zeroed, 1)
            pool.affine_select(out=ident[:, :], in_=ident[:, :], compare_op=ALU.not_equal, fill=1.0, base=0,
                               pattern=[[-1, P]], channel_multiplier=1).then_inc(made, 1)
            pool.wait_ge(made, 1)


def layernorm(nc, name, src, dst, rows, width, affine=None, outs=(), ident=None):
    ctx, sb, ps, sem = phase(nc, name)
    n = len(rows)
    nk = width // P
    with ctx:
        stats = sb("stats", [P, n, 6])
        mv = sb("mv", [P, n, 2])
        std = sb("std", [P, n])
        rstd = sb("rstd", [P, n])
        eps = sb("eps", [P, 1])
        tp = ps("tp", [P, 4, CH]) if outs else None
        eps_set, stats_done, var_ready = sem("eps_set"), sem("stats_done"), sem("var_ready")
        std_ready, rstd_ready, normed, scaled = sem("std_ready"), sem("rstd_ready"), sem("normed"), sem("scaled")
        ready, turned, taken = sem("ready"), sem("turned"), sem("taken")
        block = ctx.enter_context(nc.Block())
        full = [t for t in range(n) if rows[t] == P]
        spans = [(0, len(full), P)] + [(t, t + 1, rows[t]) for t in range(n) if rows[t] < P]
        groups = [(k, t0, min(t0 + TPC, n)) for t0 in range(0, n, TPC) for k in range(nk)]

        @block.vector
        def _(dve):
            dve.memset(eps[:, :], EPS).then_inc(eps_set, 1)
            for t in range(n):
                r = rows[t]
                dve.bn_stats(stats[:r, t, :], src[:r, t, :]).then_inc(stats_done, 1)
            for t in range(n):
                r = rows[t]
                dve.wait_ge(stats_done, t + 1)
                dve.bn_aggr(mv[:r, t, :], stats[:r, t, :]).then_inc(var_ready, 1)
            for i, (t0, t1, r) in enumerate(spans):
                dve.wait_ge(std_ready, i + 1)
                dve.reciprocal(rstd[:r, t0:t1], std[:r, t0:t1]).then_inc(rstd_ready, 1)
            dve.wait_ge(rstd_ready, len(spans))
            for t in range(n):
                r = rows[t]
                i = dve.tensor_scalar(dst[:r, t, :], src[:r, t, :], mv[:r, t, 0:1], rstd[:r, t:t + 1],
                                      ALU.subtract, ALU.mult)
                if affine is None:
                    i.then_inc(ready, 1)
                    continue
                i.then_inc(normed, 1)
            if affine is not None:
                for t in range(n):
                    dve.wait_ge(normed, t + 1)
                    dve.tensor_tensor(dst[:, t, :], dst[:, t, :], affine[0], ALU.mult).then_inc(scaled, 1)
                for t in range(n):
                    dve.wait_ge(scaled, t + 1)
                    dve.tensor_tensor(dst[:, t, :], dst[:, t, :], affine[1], ALU.add).then_inc(ready, 1)

        @block.scalar
        def _(act):
            act.wait_ge(eps_set, 1)
            act.wait_ge(var_ready, n)
            for t0, t1, r in spans:
                act.activation(std[:r, t0:t1], mv[:r, t0:t1, 1], ACT.Sqrt, bias=eps[:r, 0:1]).then_inc(std_ready, 1)
            for i, (k, t0, t1) in enumerate(groups if outs else ()):
                w = sum(rows[t0:t1])
                act.wait_ge(turned, i + 1)
                for target, g, b in outs:
                    o = target[:, k, P * t0:P * t0 + w]
                    if g is None:
                        last = act.activation(o, tp[:, i % 4, :w], ACT.Copy)
                    else:
                        last = act.activation(o, tp[:, i % 4, :w], ACT.Identity, bias=b[:, k:k + 1], scale=g[:, k:k + 1])
                last.then_inc(taken, 1)

        if outs:
            @block.tensor
            def _(pe):
                for i, (k, t0, t1) in enumerate(groups):
                    pe.wait_ge(ready, t1)
                    if i >= 4:
                        pe.wait_ge(taken, i - 3)
                    for t in range(t0, t1):
                        r = rows[t]
                        o = P * (t - t0)
                        last = pe.transpose(tp[:, i % 4, o:o + r], dst[:r, t, P * k:P * k + P], ident[:r, :r])
                    last.then_inc(turned, 1)


def attention(nc, a, name, wq, wk, wv, xq, nkq, xk, nkk, nkeys, scale, causal, ot, ones, bq=None, bk=None, bv=None, ering=4):
    ctx, sb, ps, sem = phase(nc, name)
    kt_rows = tiles_of(nkeys)
    nkt = len(kt_rows)
    kch = chunks_of(nkeys)
    nmx = 4
    mxw = (nkeys + nmx - 1) // nmx
    mxs = [min(mxw * i, nkeys - mxw) for i in range(nmx)]
    nunit = TPC * HG * nmx
    nproj = len(kch) + NCH
    nvb = (nkt + 3) // 4
    with ctx:
        wqg = sb("wqg", [P, nkq, P])
        wkg = sb("wkg", [P, nkk, P])
        wvg = sb("wvg", [P, nkk, P])
        stage = sb("stage", [P, 2, T], F16)
        qs = sb("qs", [P, HG, T], F16)
        ks = sb("ks", [P, HG, T], F16)
        v = sb("v", [P, nkt, P])
        e = sb("e", [P, ering, HG, CH])
        em = sb("em", [P, 2, HG, CH]) if causal else None
        later = sb("later", [P, TPC, CH], F16) if causal else None
        part_max = sb("part_max", [P, HG, TPC, nmx])
        row_max = sb("row_max", [P, HG, TPC])
        neg_max = sb("neg_max", [HG * TPC, P], F16)
        rden = sb("rden", [P, CH])
        mx = [ps(f"mx{i}", [P, CH]) for i in range(2)]
        sc = [ps(f"sc{i}", [P, 2, CH]) for i in range(2)]
        po = ps("po", [P, CH])
        pd = ps("pd", [P, CH])
        identm = a["ident"]

        w_loaded = sem("w_loaded")
        ones_set, mask_filled = sem("ones_set"), sem("mask_filled")
        proj_ready, high_ready, proj_taken = sem("proj_ready"), sem("high_ready"), sem("proj_taken")
        v_ready, v_taken = sem("v_ready"), sem("v_taken")
        k_stacked, q_stacked = sem("k_stacked"), sem("q_stacked")
        mx_ready, mx_taken = sem("mx_ready"), sem("mx_taken")
        rowmax_ready, maxT_ready, negmax_ready, negmax_loaded = sem("rowmax_ready"), sem("maxT_ready"), sem("negmax_ready"), sem("negmax_loaded")
        sc_ready, exp_done, masked, pv_done = sem("sc_ready"), sem("exp_done"), sem("masked"), sem("pv_done")
        rden_ready, o_taken = sem("rden_ready"), sem("o_taken")
        block = ctx.enter_context(nc.Block())

        @block.sync
        def _(sp):
            with sp.Fori(0, NG) as g:
                sp.wait_ge(v_ready, nvb * g)
                sp.dma_start(wkg[:, :, :], wk[bass.ds(g, 1)].rearrange("o p k n -> (o p) k n")).then_inc(w_loaded, 16)
                sp.dma_start(wvg[:, :, :], wv[bass.ds(g, 1)].rearrange("o p k n -> (o p) k n")).then_inc(w_loaded, 16)
                sp.dma_start(wqg[:, :, :], wq[bass.ds(g, 1)].rearrange("o p k n -> (o p) k n")).then_inc(w_loaded, 16)
                sp.wait_ge(proj_taken, nproj * g + len(kch))
                for j in range(HG):
                    h = SLOT * j
                    for s, part in enumerate((0, 1, 0)):
                        sp.dma_start(ks[SLOT * s:SLOT * s + SLOT, j, :nkeys],
                                     stage[h:h + SLOT, part, :nkeys]).then_inc(k_stacked, 16)
                sp.wait_ge(proj_taken, nproj * g + nproj)
                for j in range(HG):
                    h = SLOT * j
                    for s, part in enumerate((0, 0, 1)):
                        sp.dma_start(qs[SLOT * s:SLOT * s + SLOT, j, :],
                                     stage[h:h + SLOT, part, :]).then_inc(q_stacked, 16)
                for qc in range(NCH):
                    sp.wait_ge(negmax_ready, NCH * g + qc + 1)
                    for j in range(HG):
                        sp.dma_start(qs[STACK:STACK + 1, j, CH * qc:CH * qc + CH].rearrange("o (t q) -> o t q", t=TPC),
                                     neg_max[TPC * j:TPC * j + TPC, :]).then_inc(negmax_loaded, 16)

        @block.gpsimd
        def _(pool):
            if causal:
                pool.memset(later[:, :, :], 1.0).then_inc(mask_filled, 1)
                pool.wait_ge(mask_filled, 1)
                pool.affine_select(out=later[:, :, :], in_=later[:, :, :], compare_op=ALU.is_gt, fill=0.0, base=0,
                                   pattern=[[P, TPC], [-1, CH]], channel_multiplier=1).then_inc(mask_filled, 1)
                pool.wait_ge(mask_filled, 2)
                with pool.Fori(0, NG) as g:
                    for qc in range(NCH):
                        for i in range(TPC):
                            kt = TPC * qc + i
                            n = TPC * qc + i
                            pool.wait_ge(exp_done, 2 * nkt * NCH * g + 2 * (nkt * qc + kt + 1))
                            if n >= 2:
                                m = nkt * (qc if i >= 2 else qc - 1) + (kt - 2) + 1
                                pool.wait_ge(pv_done, nkt * NCH * g + m)
                            else:
                                pool.wait_ge(pv_done, nkt * NCH * g)
                            pool.tensor_tensor(em[:, n % 2, :, :], e[:, (nkt * qc + kt) % ering, :, :],
                                               later[:, i, :].unsqueeze(1).to_broadcast([P, HG, CH]),
                                               ALU.mult).then_inc(masked, 1)

        @block.scalar
        def _(act):
            with act.Fori(0, NG) as g:
                for b in range(nvb):
                    act.wait_ge(v_ready, nvb * g + b + 1)
                    ts = range(4 * b, min(4 * b + 4, nkt))
                    r = [t for t in ts if kt_rows[t] == P]
                    src = sc[b % 2][:, b // 2 % 2, :].rearrange("p (t n) -> p t n", n=P)
                    if r:
                        last = act.activation(v[:, r[0]:r[-1] + 1, :], src[:, 0:len(r), :], ACT.Copy)
                    for t in ts:
                        if kt_rows[t] < P:
                            last = act.activation(v[:kt_rows[t], t, :], src[:kt_rows[t], t - 4 * b, :], ACT.Copy)
                    last.then_inc(v_taken, 1)
                for qc in range(NCH):
                    for kt in range(nkt):
                        n = nkt * qc + kt
                        r = kt_rows[kt]
                        for half in range(2):
                            act.wait_ge(sc_ready, 2 * nkt * NCH * g + 2 * n + half + 1)
                            if n >= ering:
                                act.wait_ge(pv_done, nkt * NCH * g + n - ering + 1)
                            act.activation(e[:r, n % ering, 2 * half:2 * half + 2, :], sc[half][:r, :, :], ACT.Exp,
                                           scale=scale).then_inc(exp_done, 1)

        @block.vector
        def _(dve):
            dve.memset(ks[STACK:STACK + 1, :, :], 1.0).then_inc(ones_set, 1)

            def max_units(g, qc, u0, u1):
                for u in range(u0, u1):
                    j, t, i = u // nmx % HG, u // nmx // HG, u % nmx
                    dve.wait_ge(mx_ready, nunit * NCH * g + nunit * qc + u + 1)
                    dve.tensor_reduce(part_max[:, j, t, i:i + 1], mx[u % 2][:, :mxw], AX.X, ALU.max).then_inc(mx_taken, 1)

            def row_maxima(g, qc):
                n = NCH * g + qc
                dve.wait_ge(mx_taken, nunit * n + nunit)
                dve.tensor_reduce(row_max[:, :, :], part_max[:, :, :, :], AX.X, ALU.max).then_inc(rowmax_ready, 1)
                dve.wait_ge(maxT_ready, n + 1)
                dve.wait_ge(negmax_loaded, 16 * HG * n)
                dve.tensor_scalar(neg_max[:, :], mx[0][:HG * TPC, :P], -1.0, None, ALU.mult).then_inc(negmax_ready, 1)

            with dve.Fori(0, NG) as g:
                for c in range(nproj):
                    isk = c < len(kch)
                    o, w = kch[c] if isk else (CH * (c - len(kch)), CH)
                    src = (po if c % 2 == 0 else pd)[:, :w]
                    bias = bk if isk else bq
                    bias = bias[:, bass.ds(g, 1)] if bias is not None else 0.0
                    dve.wait_ge(proj_ready, nproj * g + c + 1)
                    if c == 0:
                        dve.wait_ge(q_stacked, 16 * 12 * g)
                    if c == len(kch):
                        dve.wait_ge(k_stacked, 16 * 12 * g + 16 * 12)
                    dve.tensor_scalar(stage[:, 0, o:o + w], src, bias, None, ALU.add).then_inc(high_ready, 1)
                    dve.wait_ge(high_ready, nproj * g + c + 1)
                    dve.scalar_tensor_tensor(out=stage[:, 1, o:o + w], in0=src, scalar=bias, in1=stage[:, 0, o:o + w],
                                             op0=ALU.add, op1=ALU.subtract).then_inc(proj_taken, 1)
                max_units(g, 0, 0, nunit)
                row_maxima(g, 0)
                for qc in range(NCH):
                    if qc + 1 < NCH:
                        max_units(g, qc + 1, 0, nunit)
                        row_maxima(g, qc + 1)
                    dve.wait_ge(pv_done, nkt * NCH * g + nkt * (qc + 1))
                    dve.reciprocal(rden[:, :], pd[:, :]).then_inc(rden_ready, 1)
                    dve.wait_ge(rden_ready, NCH * g + qc + 1)
                    dve.tensor_tensor(ot[:, bass.ds(g, 1), CH * qc:CH * qc + CH].rearrange("p o n -> p (o n)"),
                                      po[:, :], rden[:, :], ALU.mult).then_inc(o_taken, 1)

        @block.tensor
        def _(pe):
            def project_keys_queries(g):
                for c in range(nproj):
                    isk = c < len(kch)
                    o, w = kch[c] if isk else (CH * (c - len(kch)), CH)
                    dst = (po if c % 2 == 0 else pd)[:, :w]
                    if c >= 2:
                        pe.wait_ge(proj_taken, nproj * g + c - 1)
                    else:
                        pe.wait_ge(o_taken, NCH * g)
                    W, X, nk = (wkg, xk, nkk) if isk else (wqg, xq, nkq)
                    for k in range(nk):
                        last = pe.matmul(dst, W[:, k, :], X[:, k, o:o + w], start=(k == 0), stop=(k == nk - 1))
                    last.then_inc(proj_ready, 1)

            def project_values(g):
                for b in range(nvb):
                    dst = sc[b % 2][:, b // 2 % 2, :]
                    if b == 0:
                        pe.wait_ge(exp_done, 2 * nkt * NCH * g)
                    for t in range(4 * b, min(4 * b + 4, nkt)):
                        r = kt_rows[t]
                        o = dst[:r, P * (t - 4 * b):P * (t - 4 * b) + P]
                        for k in range(nkk):
                            last = pe.matmul(o, xk[:, k, P * t:P * t + r], wvg[:, k, :], start=(k == 0),
                                             stop=(k == nkk - 1 and bv is None))
                        if bv is not None:
                            last = pe.matmul(o, ones[0:1, :r], bv[0:1, bass.ds(g, 1), :].rearrange("p o n -> p (o n)"),
                                             start=False, stop=True)
                    last.then_inc(v_ready, 1)

            def max_unit(g, qc, u):
                j, t, i = u // nmx % HG, u // nmx // HG, u % nmx
                n = nunit * qc + u
                if n >= 2:
                    pe.wait_ge(mx_taken, nunit * NCH * g + n - 1)
                if u < 2:
                    pe.wait_ge(negmax_ready, NCH * g + qc)
                q = CH * qc + P * t
                pe.matmul(mx[u % 2][:, :mxw], qs[:STACK, j, q:q + P], ks[:STACK, j, mxs[i]:mxs[i] + mxw],
                          start=True, stop=True).then_inc(mx_ready, 1)

            def turn_maxima(g, qc):
                pe.wait_ge(rowmax_ready, NCH * g + qc + 1)
                pe.transpose(mx[0][:HG * TPC, :P], row_max[:, :, :].rearrange("p j t -> p (j t)"),
                             identm[:, :]).then_inc(maxT_ready, 1)

            def score(g, qc, kt):
                n = nkt * qc + kt
                r = kt_rows[kt]
                for half in range(2):
                    if n >= 1:
                        pe.wait_ge(exp_done, 2 * nkt * NCH * g + 2 * (n - 1) + half + 1)
                    elif half == 0:
                        pe.wait_ge(v_taken, nvb * g + nvb)
                    for i in range(2):
                        j = 2 * half + i
                        last = pe.matmul(sc[half][:r, i, :], ks[:STACK + 1, j, P * kt:P * kt + r],
                                         qs[:STACK + 1, j, CH * qc:CH * qc + CH], start=True, stop=True)
                    last.then_inc(sc_ready, 1)

            def sum_values(g, qc, kt):
                n = nkt * qc + kt
                r = kt_rows[kt]
                pe.wait_ge(exp_done, 2 * nkt * NCH * g + 2 * n + 2)
                if kt == 0:
                    pe.wait_ge(o_taken, NCH * g + qc)
                first = TPC * qc if causal else 0
                if causal and first <= kt < first + TPC:
                    pe.wait_ge(masked, NT * g + kt + 1)
                    weights = em[:, kt % 2, :, :]
                else:
                    weights = e[:, n % ering, :, :]
                if kt >= first:
                    for j in range(HG):
                        h = SLOT * j
                        pe.matmul(po[h:h + SLOT, :], v[:r, kt, h:h + SLOT], weights[:r, j, :],
                                  start=(kt == first), stop=(kt == nkt - 1))
                for j in range(HG):
                    h = SLOT * j
                    last = pe.matmul(pd[h:h + SLOT, :], ones[:r, :SLOT], e[:r, n % ering, j, :],
                                     start=(kt == 0), stop=(kt == nkt - 1))
                last.then_inc(pv_done, 1)

            with pe.Fori(0, NG) as g:
                pe.wait_ge(ones_set, 1)
                pe.wait_ge(w_loaded, 48 * g + 48)
                project_keys_queries(g)
                project_values(g)
                pe.wait_ge(k_stacked, 16 * 12 * g + 16 * 12)
                pe.wait_ge(q_stacked, 16 * 12 * g + 16 * 12)
                for u in range(nunit):
                    max_unit(g, 0, u)
                turn_maxima(g, 0)
                for qc in range(NCH):
                    pe.wait_ge(negmax_loaded, 16 * HG * NCH * g + 16 * HG * (qc + 1))
                    u = 0
                    for kt in range(nkt + 1):
                        if kt < nkt:
                            score(g, qc, kt)
                        if kt >= 1:
                            sum_values(g, qc, kt - 1)
                        while qc + 1 < NCH and u < nunit * (kt + 1) // (nkt + 1):
                            max_unit(g, qc + 1, u)
                            u += 1
                    if qc + 1 < NCH:
                        turn_maxima(g, qc + 1)


def project_out(nc, name, ot, wo_dram, bias, res, dst):
    ctx, sb, ps, sem = phase(nc, name)
    with ctx:
        wo = sb("wo", [P, NG, D])
        y = [ps(f"y{i}", [P, D]) for i in range(4)]
        w_loaded, y_ready, summed, biased = sem("w_loaded"), sem("y_ready"), sem("summed"), sem("biased")
        block = ctx.enter_context(nc.Block())

        @block.sync
        def _(sp):
            sp.dma_start(wo[:, :, :], wo_dram).then_inc(w_loaded, 16)

        @block.tensor
        def _(pe):
            pe.wait_ge(w_loaded, 16)
            for t in range(NT):
                if t >= 4:
                    pe.wait_ge(summed, t - 3)
                for g in range(NG):
                    last = pe.matmul(y[t % 4][:, :], ot[:, g, P * t:P * t + P], wo[:, g, :], start=(g == 0), stop=(g == NG - 1))
                last.then_inc(y_ready, 1)

        @block.vector
        def _(dve):
            for t in range(NT):
                dve.wait_ge(y_ready, t + 1)
                dve.tensor_tensor(dst[:, t, :], y[t % 4][:, :], res[:, t, :], ALU.add).then_inc(summed, 1)

        @block.gpsimd
        def _(pool):
            for t in range(NT):
                pool.wait_ge(summed, t + 1)
                pool.tensor_tensor(dst[:, t, :], dst[:, t, :], bias, ALU.add).then_inc(biased, 1)


def gelu_ffn(nc, name, xt, w2_dram, w3_dram, b2, b3, xo, adds, dst):
    ctx, sb, ps, sem = phase(nc, name)
    nj = FF // P
    with ctx:
        w2 = sb("w2", [P, KC, FF])
        w3 = sb("w3", [P, nj, D])
        h = sb("h", [P, 2, nj, CH])
        hp = [ps(f"hp{i}", [P, CH]) for i in range(4)]
        y = [ps(f"y{i}", [P, D]) for i in range(4)]
        w_loaded, based = sem("w_loaded"), sem("based")
        h_ready, h_done, y_ready, summed = sem("h_ready"), sem("h_done"), sem("y_ready"), sem("summed")
        block = ctx.enter_context(nc.Block())

        @block.sync
        def _(sp):
            sp.dma_start(w2[:, :, :], w2_dram).then_inc(w_loaded, 16)
            sp.dma_start(w3[:, :, :], w3_dram).then_inc(w_loaded, 16)

        @block.gpsimd
        def _(pool):
            for i, add in enumerate(adds):
                if i:
                    pool.wait_ge(based, i)
                pool.tensor_tensor(xo[:, :, :], xo[:, :, :], add[:, :, :], ALU.add).then_inc(based, 1)
            pool.wait_ge(based, len(adds))
            for t in range(NT):
                pool.tensor_tensor(xo[:, t, :], xo[:, t, :], b3, ALU.add).then_inc(based, 1)

        @block.tensor
        def _(pe):
            pe.wait_ge(w_loaded, 32)

            def hidden(c, j):
                n = nj * c + j
                if n >= 4:
                    pe.wait_ge(h_done, n - 3)
                for k in range(KC):
                    last = pe.matmul(hp[n % 4][:, :], w2[:, k, P * j:P * j + P], xt[:, k, CH * c:CH * c + CH],
                                     start=(k == 0), stop=(k == KC - 1))
                last.then_inc(h_ready, 1)

            def out(t):
                pe.wait_ge(h_done, nj * (t // TPC + 1))
                if t >= 4:
                    pe.wait_ge(summed, t - 3)
                q = P * (t % TPC)
                for j in range(nj):
                    last = pe.matmul(y[t % 4][:, :], h[:, t // TPC % 2, j, q:q + P], w3[:, j, :], start=(j == 0), stop=(j == nj - 1))
                last.then_inc(y_ready, 1)

            for c in range(NCH + 1):
                for i in range(nj):
                    if c < NCH:
                        hidden(c, i)
                    if c >= 1 and i % 2 == 1:
                        out(TPC * (c - 1) + i // 2)

        @block.scalar
        def _(act):
            for n in range(nj * NCH):
                c, j = n // nj, n % nj
                act.wait_ge(h_ready, n + 1)
                if c >= 2 and j == 0:
                    act.wait_ge(y_ready, TPC * (c - 1))
                act.activation(h[:, c % 2, j, :], hp[n % 4][:, :], ACT.Gelu, bias=b2[:, j:j + 1]).then_inc(h_done, 1)

        @block.vector
        def _(dve):
            for t in range(NT):
                dve.wait_ge(y_ready, t + 1)
                dve.wait_ge(based, len(adds) + t + 1)
                dve.tensor_tensor(dst[:, t, :], y[t % 4][:, :], xo[:, t, :], ALU.add).then_inc(summed, 1)


class Chain:

    def __init__(self, engine, sem):
        self.engine, self.sem, self.n = engine, sem, 0

    def __call__(self, instruction):
        self.n += 1
        instruction.then_inc(self.sem, 1)
        self.engine.wait_ge(self.sem, self.n)


def over(ap, n):
    return ap.unsqueeze(2).to_broadcast([ap.shape[0], ap.shape[1], n])


def router_stats(nc, z, zst, ident):
    ctx, sb, ps, sem = phase(nc, "stats")
    with ctx:
        st = sb("st", [P, NT, 6])
        mv = sb("mv", [P, NT, 2])
        sq = sb("sq", [P, NT])
        f = sb("f", [P, NT, NSTAT])
        small = sb("small", [P, NT, D])
        tp = [ps(f"tp{i}", [NSTAT, CH]) for i in range(NCH)]
        chain, sums_ready, roots_ready, turned, taken = sem("chain"), sem("sums_ready"), sem("roots_ready"), sem("turned"), sem("taken")
        block = ctx.enter_context(nc.Block())

        @block.vector
        def _(dve):
            link = Chain(dve, chain)
            for t in range(NT):
                last = dve.bn_stats(st[:, t, :], z[:, t, :])
            link(last)
            for t in range(NT):
                last = dve.bn_aggr(mv[:, t, :], st[:, t, :])
            link(last)
            dve.tensor_copy(f[:, :, 0], mv[:, :, 0])
            link(dve.tensor_tensor(sq[:, :], mv[:, :, 0], mv[:, :, 0], ALU.mult))
            dve.tensor_tensor(sq[:, :], sq[:, :], mv[:, :, 1], ALU.add).then_inc(sums_ready, 1)
            dve.tensor_reduce(f[:, :, 2], z[:, :, :], AX.X, ALU.min)
            dve.tensor_reduce(f[:, :, 3], z[:, :, :], AX.X, ALU.max)
            link(dve.tensor_scalar(small[:, :, :], z[:, :, :], 1e-6, None, ALU.is_lt))
            flat_z, flat_small = (v[:, :, :].rearrange("p t d -> p (t d)") for v in (z, small))
            link(dve.scalar_tensor_tensor(out=flat_small, in0=flat_z, scalar=-1e-6, in1=flat_small, op0=ALU.is_gt, op1=ALU.mult))
            link(dve.tensor_reduce(f[:, :, 5], small[:, :, :], AX.X, ALU.add))
            link(dve.tensor_scalar(f[:, :, 5], f[:, :, 5], 1.0 / D, None, ALU.mult))
            for c in range(NCH):
                dve.wait_ge(turned, c + 1)
                dve.tensor_copy(zst[:NSTAT, CH * c:CH * c + CH], tp[c][:, :]).then_inc(taken, 1)

        @block.scalar
        def _(act):
            act.wait_ge(sums_ready, 1)
            act.activation(f[:, :, 4], sq[:, :], ACT.Sqrt, scale=float(D)).then_inc(roots_ready, 1)
            act.activation(f[:, :, 1], mv[:, :, 1], ACT.Sqrt, scale=D / (D - 1.0)).then_inc(roots_ready, 1)

        @block.tensor
        def _(pe):
            pe.wait_ge(roots_ready, 2)
            pe.wait_ge(chain, 7)
            for c in range(NCH):
                for i in range(TPC):
                    last = pe.transpose(tp[c][:, P * i:P * i + P], f[:, TPC * c + i, :], ident[:, :])
                last.then_inc(turned, 1)


def router(nc, a, zt, zst, r1b, wc, picks, ident):
    ctx, sb, ps, sem = phase(nc, "router")
    with ctx:
        r1 = sb("r1", [P, KC, P])
        r1s = sb("r1s", [NSTAT, P])
        r2 = sb("r2", [P, E0])
        h = sb("h", [P, T])
        hp = [ps(f"hp{i}", [P, CH]) for i in range(2)]
        lg = ps("lg", [P, NT, E0])
        tp = [ps(f"tp{i}", [E0, CH]) for i in range(NCH)]
        pr = sb("pr", [P, NT, E0])
        top = sb("top", [P, NT, 8])
        at = sb("at", [P, NT, 8], U32)
        atf = sb("atf", [P, NT, 8])
        iota = sb("iota", [P, NT, E0])
        mask = sb("mask", [P, NT, E0])
        one = sb("one", [P, NT, E0])
        m = sb("m", [P, NT])
        w_loaded, iota_ready, chain = sem("w_loaded"), sem("iota_ready"), sem("chain")
        h_ready, h_done, logits_ready, shifted, exped = sem("h_ready"), sem("h_done"), sem("logits_ready"), sem("shifted"), sem("exped")
        picked, turned, taken = sem("picked"), sem("turned"), sem("taken")
        block = ctx.enter_context(nc.Block())

        @block.sync
        def _(sp):
            sp.dma_start(r1[:, :, :], a["r1"]).then_inc(w_loaded, 16)
            sp.dma_start(r1s[:, :], a["r1s"]).then_inc(w_loaded, 16)
            sp.dma_start(r2[:, :], a["r2"]).then_inc(w_loaded, 16)

        @block.gpsimd
        def _(pool):
            pool.iota(iota[:, :, :], [[0, NT], [1, E0]], base=0, channel_multiplier=0,
                      allow_small_or_imprecise_dtypes=True).then_inc(iota_ready, 1)

        @block.tensor
        def _(pe):
            pe.wait_ge(w_loaded, 48)
            for c in range(NCH):
                if c >= 2:
                    pe.wait_ge(h_done, c - 1)
                o = hp[c % 2][:, :]
                x = slice(CH * c, CH * c + CH)
                for k in range(KC):
                    pe.matmul(o, r1[:, k, :], zt[:, k, x], start=(k == 0), stop=False)
                pe.matmul(o, r1s[:, :], zst[:NSTAT, x], start=False, stop=True).then_inc(h_ready, 1)
            for t in range(NT):
                pe.wait_ge(h_done, t // TPC + 1)
                last = pe.matmul(lg[:, t, :], h[:, P * t:P * t + P], r2[:, :], start=True, stop=True)
            last.then_inc(logits_ready, 1)
            pe.wait_ge(picked, 1)
            for c in range(NCH):
                for i in range(TPC):
                    last = pe.transpose(tp[c][:, P * i:P * i + P], one[:, TPC * c + i, :], ident[:, :])
                last.then_inc(turned, 1)

        @block.scalar
        def _(act):
            for c in range(NCH):
                act.wait_ge(h_ready, c + 1)
                act.activation(h[:, CH * c:CH * c + CH], hp[c % 2][:, :], ACT.Gelu, bias=r1b).then_inc(h_done, 1)
            act.wait_ge(shifted, 1)
            act.activation(pr[:, :, :], pr[:, :, :], ACT.Exp).then_inc(exped, 1)

        @block.vector
        def _(dve):
            link = Chain(dve, chain)
            dve.wait_ge(logits_ready, 1)
            link(dve.tensor_reduce(m[:, :], lg[:, :, :], AX.X, ALU.max))
            dve.tensor_tensor(pr[:, :, :], lg[:, :, :], over(m[:, :], E0), ALU.subtract).then_inc(shifted, 1)
            dve.wait_ge(exped, 1)
            link(dve.tensor_reduce(m[:, :], pr[:, :, :], AX.X, ALU.add))
            link(dve.reciprocal(m[:, :], m[:, :]))
            link(dve.tensor_tensor(pr[:, :, :], pr[:, :, :], over(m[:, :], E0), ALU.mult))
            for t in range(NT):
                last = dve.max(top[:, t, :], pr[:, t, :])
            link(last)
            for t in range(NT):
                last = dve.max_index(at[:, t, :], top[:, t, :], pr[:, t, :])
            link(last)
            link(dve.tensor_copy(atf[:, :, :], at[:, :, :]))
            dve.wait_ge(iota_ready, 1)
            dve.tensor_tensor(mask[:, :, :], iota[:, :, :], over(atf[:, :, 0], E0), ALU.is_equal)
            link(dve.tensor_tensor(one[:, :, :], iota[:, :, :], over(atf[:, :, 1], E0), ALU.is_equal))
            dve.tensor_tensor(m[:, :], top[:, :, 0], top[:, :, 1], ALU.add)
            link(dve.tensor_tensor(mask[:, :, :], mask[:, :, :], one[:, :, :], ALU.add))
            link(dve.reciprocal(m[:, :], m[:, :]))
            link(dve.tensor_tensor(pr[:, :, :], pr[:, :, :], mask[:, :, :], ALU.mult))
            dve.tensor_tensor(wc[:, :, :], pr[:, :, :], over(m[:, :], E0), ALU.mult)
            link(dve.tensor_scalar(mask[:, :, :], mask[:, :, :], 1.0, None, ALU.subtract))
            dve.tensor_tensor(one[:, :, :], pr[:, :, :], mask[:, :, :], ALU.add).then_inc(picked, 1)
            for c in range(NCH):
                dve.wait_ge(turned, c + 1)
                dve.tensor_copy(picks[:, CH * c:CH * c + CH], tp[c][:, :]).then_inc(taken, 1)


def choose(nc, a, picks, z, wc, x_sb, slots, ident):
    ctx, sb, ps, sem = phase(nc, "choose")
    with ctx:
        other = sb("other", [E0, T])
        val = sb("val", [E0, CAP])
        at = sb("at", [E0, CAP], U32)
        atf = sb("atf", [E0, CAP])
        tp = ps("tp", [CAP, E0])
        chain, at_ready, turned, stored = sem("chain"), sem("at_ready"), sem("turned"), sem("stored")
        block = ctx.enter_context(nc.Block())

        @block.sync
        def _(sp):
            rows = a["table"].rearrange("(t p) c -> p t c", p=P)
            sp.dma_start(rows[:, :, :D], z[:, :, :]).then_inc(stored, 16)
            sp.dma_start(rows[:, :, D:], wc[:, :, :]).then_inc(stored, 16)
            sp.dma_start(a["acc"].rearrange("(t p) d -> p t d", p=P), x_sb[:, :, :]).then_inc(stored, 16)
            sp.wait_ge(stored, 48)

        @block.vector
        def _(dve):
            link = Chain(dve, chain)
            buf = [picks, other]
            for r in range(CAP // 8):
                src, dst = buf[r % 2], buf[(r + 1) % 2]
                o = slice(8 * r, 8 * r + 8)
                link(dve.max(val[:, o], src[:, :]))
                link(dve.max_index(at[:, o], val[:, o], src[:, :]))
                if r < CAP // 8 - 1:
                    link(dve.match_replace(dst[:, :], val[:, o], src[:, :], -2.0))
            dve.tensor_copy(atf[:, :], at[:, :]).then_inc(at_ready, 1)
            dve.wait_ge(turned, 1)
            link(dve.tensor_copy(slots[:CAP, :], tp[:, :]))

        @block.tensor
        def _(pe):
            pe.wait_ge(at_ready, 1)
            pe.transpose(tp[:, :], atf[:, :], ident[:E0, :E0]).then_inc(turned, 1)


def experts(nc, a, slots, x_sb, ident):
    ctx, sb, ps, sem = phase(nc, "experts")
    NJ = INTER // P
    UP = KC * 2 * INTER
    with ctx:
        xe = sb("xe", [CAP, E0, ROW])
        xet = sb("xet", [P, KC, E0, CAP])
        we = sb("we", [CAP, E0])
        w = [sb(f"w{i}", [P, UP + NJ * D]) for i in range(2)]
        aw = sb("aw", [P, KC * 2 * AI + D])
        sg = [sb(f"sg{i}", [P, NJ + 1, CAP]) for i in range(2)]
        h = [sb(f"h{i}", [P, NJ + 1, CAP]) for i in range(2)]
        ye = [sb(f"ye{i}", [CAP, D]) for i in range(2)]
        gp = [ps(f"gp{i}", [P, NJ + 1, CAP]) for i in range(2)]
        up = [ps(f"up{i}", [P, NJ + 1, CAP]) for i in range(2)]
        y = [ps(f"y{i}", [CAP, D]) for i in range(2)]
        tp = [ps(f"tp{i}", [P, 4, CAP]) for i in range(2)]
        gathered, turned, taken, we_ready = sem("gathered"), sem("turned"), sem("taken"), sem("we_ready")
        w_loaded = [sem(f"w_loaded{i}") for i in range(2)]
        aw_loaded = sem("aw_loaded")
        g_ready, u_ready, silu_done, h_done = sem("g_ready"), sem("u_ready"), sem("silu_done"), sem("h_done")
        y_ready, ye_ready, added, back = sem("y_ready"), sem("ye_ready"), sem("added"), sem("back")
        block = ctx.enter_context(nc.Block())

        @block.sync
        def _(sp):
            with sp.Fori(0, E0 // 2) as i:
                for s in range(2):
                    sp.wait_ge(y_ready, 2 * i)
                    if s == 0:
                        sp.dma_start(aw[:, :], a["aw"][bass.ds(i, 1)].rearrange("o p n -> (o p) n")).then_inc(aw_loaded, 16)
                    sp.dma_start(w[s][:, :], a["we"][bass.ds(2 * i + s, 1)].rearrange("o p n -> (o p) n")).then_inc(w_loaded[s], 16)
            sp.wait_ge(added, 16 * E0)
            sp.dma_start(x_sb[:, :, :], a["acc"].rearrange("(t p) d -> p t d", p=P)).then_inc(back, 16)
            sp.wait_ge(back, 16)

        @block.gpsimd
        def _(pool):
            for e in range(E0):
                pool.indirect_dma_start(xe[:, e, :], None, a["table"],
                                        bass.IndirectOffsetOnAxis(slots[:CAP, e:e + 1], 0)).then_inc(gathered, 16)
            for e in range(E0):
                pool.wait_ge(ye_ready, e + 1)
                if e >= 1:
                    pool.wait_ge(added, 16 * e)
                pool.indirect_dma_start(a["acc"], bass.IndirectOffsetOnAxis(slots[:CAP, e:e + 1], 0), ye[e % 2][:, :], None,
                                        compute_op=ALU.add).then_inc(added, 16)

        @block.tensor
        def _(pe):
            pe.wait_ge(gathered, 16 * E0)
            n = 0
            for e0 in range(0, E0, 4):
                for k in range(KC):
                    if n >= 2:
                        pe.wait_ge(taken, n - 1)
                    for e in range(e0, e0 + 4):
                        last = pe.transpose(tp[n % 2][:, e - e0, :], xe[:, e, P * k:P * k + P], ident[:CAP, :CAP])
                    last.then_inc(turned, 1)
                    n += 1
            pe.wait_ge(taken, n)
            with pe.Fori(0, E0 // 2) as i:
                for s in range(2):
                    e = 2 * i + s
                    pe.wait_ge(w_loaded[s], 16 * i + 16)
                    pe.wait_ge(aw_loaded, 16 * i + 16)
                    pe.wait_ge(h_done, 2 * i)
                    for dst, off, aoff, ready in ((gp[s], 0, 0, g_ready), (up[s], INTER, AI, u_ready)):
                        for j in range(NJ + 1):
                            for k in range(KC):
                                if j < NJ:
                                    o = 2 * INTER * k + off + P * j
                                    lhs = w[s][:, o:o + P]
                                else:
                                    o = 2 * AI * k + aoff
                                    lhs = aw[:, o:o + AI]
                                last = pe.matmul(dst[:, j, :], lhs, xet[:, k, bass.ds(e, 1), :].rearrange("p o c -> p (o c)"),
                                                 start=(k == 0), stop=(k == KC - 1))
                        last.then_inc(ready, 1)
                for s in range(2):
                    pe.wait_ge(h_done, 2 * i + s + 1)
                    pe.wait_ge(ye_ready, 2 * i)
                    for j in range(NJ + 1):
                        rhs = w[s][:, UP + D * j:UP + D * j + D] if j < NJ else aw[:, KC * 2 * AI:]
                        last = pe.matmul(y[s][:, :], h[s][:, j, :], rhs, start=(j == 0), stop=(j == NJ))
                    last.then_inc(y_ready, 1)

        @block.scalar
        def _(act):
            with act.Fori(0, E0 // 2) as i:
                for s in range(2):
                    act.wait_ge(g_ready, 2 * i + s + 1)
                    act.wait_ge(h_done, 2 * i)
                    act.activation(sg[s][:, :, :], gp[s][:, :, :], ACT.Silu).then_inc(silu_done, 1)

        @block.vector
        def _(dve):
            n = 0
            for e0 in range(0, E0, 4):
                for k in range(KC):
                    dve.wait_ge(turned, n + 1)
                    dve.tensor_copy(xet[:, k, e0:e0 + 4, :], tp[n % 2][:, :, :]).then_inc(taken, 1)
                    n += 1
            flat = xe[:, :, :].rearrange("p e c -> p (e c)")
            dve.tensor_copy(we[:, :], flat[:, D:D + (ROW + 1) * (E0 - 1) + 1:ROW + 1]).then_inc(we_ready, 1)
            dve.wait_ge(we_ready, 1)
            with dve.Fori(0, E0 // 2) as i:
                for s in range(2):
                    dve.wait_ge(silu_done, 2 * i + s + 1)
                    dve.wait_ge(u_ready, 2 * i + s + 1)
                    dve.wait_ge(y_ready, 2 * i)
                    dve.tensor_tensor(h[s][:, :NJ, :], sg[s][:, :NJ, :], up[s][:, :NJ, :], ALU.mult)
                    dve.scalar_tensor_tensor(out=h[s][:, NJ, :], in0=sg[s][:, NJ, :], scalar=0.05, in1=up[s][:, NJ, :],
                                             op0=ALU.mult, op1=ALU.mult).then_inc(h_done, 1)
                for s in range(2):
                    dve.wait_ge(y_ready, 2 * i + s + 1)
                    dve.wait_ge(added, 32 * i)
                    dve.tensor_scalar(ye[s][:, :], y[s][:, :], we[:, bass.ds(2 * i + s, 1)], None, ALU.mult).then_inc(ye_ready, 1)


def gate1(nc, a, xt, gate_bias, cw):
    ctx, sb, ps, sem = phase(nc, "gate1")
    with ctx:
        gw = sb("gw", [P, KC, E1])
        lg = ps("lg", [P, NT, E1])
        sco = sb("sco", [P, NT, E1])
        sfc = sb("sfc", [P, NT, E1])
        hi = sb("hi", [P, NT * G1, 2])
        lo = sb("lo", [P, NT * G1, 2])
        t1 = sb("t1", [P, NT * G1])
        t2 = sb("t2", [P, NT * G1])
        gs = sb("gs", [P, NT, 8])
        top = sb("top", [P, NT, 8])
        at = sb("at", [P, NT, 8], U32)
        atf = sb("atf", [P, NT, 8])
        iota = sb("iota", [P, NT, E1])
        m4 = sb("m4", [P, NT, G1])
        m4b = sb("m4b", [P, NT, G1])
        m16 = [sb(f"m16{i}", [P, NT, E1]) for i in range(4)]
        tot = sb("tot", [P, NT])
        w_loaded, iota_ready, logits_ready, sig_ready, chain = sem("w_loaded"), sem("iota_ready"), sem("logits_ready"), sem("sig_ready"), sem("chain")
        block = ctx.enter_context(nc.Block())

        @block.sync
        def _(sp):
            sp.dma_start(gw[:, :, :], a["gw"]).then_inc(w_loaded, 16)

        @block.gpsimd
        def _(pool):
            pool.iota(iota[:, :, :], [[0, NT], [1, E1]], base=0, channel_multiplier=0,
                      allow_small_or_imprecise_dtypes=True).then_inc(iota_ready, 1)

        @block.tensor
        def _(pe):
            pe.wait_ge(w_loaded, 16)
            for t in range(NT):
                for k in range(KC):
                    last = pe.matmul(lg[:, t, :], xt[:, k, P * t:P * t + P], gw[:, k, :], start=(k == 0), stop=(k == KC - 1))
            last.then_inc(logits_ready, 1)

        @block.scalar
        def _(act):
            act.wait_ge(logits_ready, 1)
            act.activation(sco[:, :, :], lg[:, :, :], ACT.Sigmoid).then_inc(sig_ready, 1)

        @block.vector
        def _(dve):
            link = Chain(dve, chain)
            dve.memset(cw[:, :, E1:], 1.0)
            dve.memset(gs[:, :, :], -3e38)
            dve.wait_ge(sig_ready, 1)
            dve.wait_ge(iota_ready, 1)
            link(dve.tensor_tensor(sfc[:, :, :], sco[:, :, :], gate_bias.unsqueeze(1).to_broadcast([P, NT, E1]), ALU.add))
            four = sfc[:, :, :].rearrange("p t (g i) -> p (t g) i", i=E1 // G1)
            dve.tensor_tensor(hi[:, :, :], four[:, :, 0:2], four[:, :, 2:4], ALU.max)
            link(dve.tensor_tensor(lo[:, :, :], four[:, :, 0:2], four[:, :, 2:4], ALU.min))
            dve.tensor_tensor(t1[:, :], hi[:, :, 0], hi[:, :, 1], ALU.min)
            link(dve.tensor_tensor(t2[:, :], lo[:, :, 0], lo[:, :, 1], ALU.max))
            link(dve.tensor_tensor(t1[:, :], t1[:, :], t2[:, :], ALU.max))
            link(dve.tensor_tensor(t2[:, :], hi[:, :, 0], hi[:, :, 1], ALU.max))
            link(dve.tensor_tensor(gs[:, :, :G1], t1[:, :].rearrange("p (t g) -> p t g", g=G1),
                                   t2[:, :].rearrange("p (t g) -> p t g", g=G1), ALU.add))
            for t in range(NT):
                last = dve.max(top[:, t, :], gs[:, t, :])
            link(last)
            for t in range(NT):
                last = dve.max_index(at[:, t, :], top[:, t, :], gs[:, t, :])
            link(last)
            link(dve.tensor_copy(atf[:, :, :], at[:, :, :]))
            dve.tensor_tensor(m4[:, :, :], iota[:, :, :G1], over(atf[:, :, 0], G1), ALU.is_equal)
            link(dve.tensor_tensor(m4b[:, :, :], iota[:, :, :G1], over(atf[:, :, 1], G1), ALU.is_equal))
            link(dve.tensor_tensor(m4[:, :, :], m4[:, :, :], m4b[:, :, :], ALU.add))
            link(dve.tensor_tensor(four, four, over(m4[:, :, :].rearrange("p t g -> p (t g)"), E1 // G1), ALU.mult))
            link(dve.tensor_scalar(sfc[:, :, :], sfc[:, :, :], 0.0, None, ALU.add))
            for t in range(NT):
                last = dve.max(top[:, t, :], sfc[:, t, :])
            link(last)
            for t in range(NT):
                last = dve.max_index(at[:, t, :], top[:, t, :], sfc[:, t, :])
            link(last)
            link(dve.tensor_copy(atf[:, :, :], at[:, :, :]))
            for i in range(TOPK1):
                last = dve.tensor_tensor(m16[i][:, :, :], iota[:, :, :], over(atf[:, :, i], E1), ALU.is_equal)
            link(last)
            dve.tensor_tensor(m16[0][:, :, :], m16[0][:, :, :], m16[1][:, :, :], ALU.add)
            link(dve.tensor_tensor(m16[2][:, :, :], m16[2][:, :, :], m16[3][:, :, :], ALU.add))
            link(dve.tensor_tensor(m16[0][:, :, :], m16[0][:, :, :], m16[2][:, :, :], ALU.add))
            link(dve.tensor_tensor(sco[:, :, :], sco[:, :, :], m16[0][:, :, :], ALU.mult))
            link(dve.tensor_reduce(tot[:, :], sco[:, :, :], AX.X, ALU.add))
            link(dve.tensor_scalar(tot[:, :], tot[:, :], 1e-20, None, ALU.add))
            link(dve.reciprocal(tot[:, :], tot[:, :]))
            link(dve.tensor_tensor(cw[:, :, :E1], sco[:, :, :], over(tot[:, :], E1), ALU.mult))


def moe(nc, a, xt, cw, x_sb, out):
    ctx, sb, ps, sem = phase(nc, "moe")
    it_rows = tiles_of(EI)
    NI = len(it_rows)
    UP, DN = KC * EI, 2 * KC * EI
    NE = E1 + SH
    NU = 2 * NCH * NI
    NY = 2 * NT
    with ctx:
        w = [sb(f"w{i}", [P, DN + NI * D]) for i in range(2)]
        sg = sb("sg", [P, 2, CH])
        h = sb("h", [P, 2, NI, CH])
        gp = [ps(f"gp{i}", [P, CH]) for i in range(2)]
        up = [ps(f"up{i}", [P, CH]) for i in range(2)]
        y = [ps(f"y{i}", [P, D]) for i in range(4)]
        w_loaded = [sem(f"w_loaded{i}") for i in range(2)]
        gu_ready, silu_done, h_done, y_ready, summed, stored = (sem("gu_ready"), sem("silu_done"), sem("h_done"), sem("y_ready"),
                                                                sem("summed"), sem("stored"))
        block = ctx.enter_context(nc.Block())

        @block.sync
        def _(sp):
            with sp.Fori(0, NE // 2) as i:
                for s in range(2):
                    sp.wait_ge(y_ready, NY * i)
                    sp.dma_start(w[s][:, :], a["wm"][bass.ds(2 * i + s, 1)].rearrange("o p n -> (o p) n")).then_inc(w_loaded[s], 16)
            sp.wait_ge(summed, NY * (NE // 2))
            sp.dma_start(out.rearrange("o (t p) d -> p (o t) d", p=P), x_sb[:, :, :]).then_inc(stored, 16)
            sp.wait_ge(stored, 16)

        @block.tensor
        def _(pe):
            def hidden(i, s, c, it):
                n = NI * (NCH * s + c) + it
                r = it_rows[it]
                if n >= 2:
                    pe.wait_ge(h_done, NU * i + n - 1)
                else:
                    pe.wait_ge(h_done, NU * i)
                for dst, off in ((gp[n % 2], 0), (up[n % 2], UP)):
                    for k in range(KC):
                        o = off + EI * k + P * it
                        last = pe.matmul(dst[:r, :], w[s][:, o:o + r], xt[:, k, CH * c:CH * c + CH], start=(k == 0), stop=(k == KC - 1))
                last.then_inc(gu_ready, 1)

            def out_tile(i, s, t):
                n = NT * s + t
                c = NCH * s + t // TPC
                pe.wait_ge(h_done, NU * i + NI * (c + 1))
                if n >= 4:
                    pe.wait_ge(summed, NY * i + n - 3)
                else:
                    pe.wait_ge(summed, NY * i)
                q = P * (t % TPC)
                for it in range(NI):
                    r = it_rows[it]
                    last = pe.matmul(y[n % 4][:, :], h[:r, c % 2, it, q:q + P], w[s][:r, DN + D * it:DN + D * it + D],
                                     start=(it == 0), stop=(it == NI - 1))
                last.then_inc(y_ready, 1)

            with pe.Fori(0, NE // 2) as i:
                for c in range(2 * NCH + 1):
                    if c % NCH == 0 and c < 2 * NCH:
                        pe.wait_ge(w_loaded[c // NCH], 16 * i + 16)
                    done = 0
                    for it in range(NI):
                        if c < 2 * NCH:
                            hidden(i, c // NCH, c % NCH, it)
                        if c >= 1:
                            for q in range(TPC * it // NI, TPC * (it + 1) // NI):
                                out_tile(i, (c - 1) // NCH, TPC * ((c - 1) % NCH) + q)

        @block.scalar
        def _(act):
            with act.Fori(0, NE // 2) as i:
                for n in range(NU):
                    r = it_rows[n % NI]
                    act.wait_ge(gu_ready, NU * i + n + 1)
                    act.wait_ge(h_done, NU * i + max(n - 1, 0))
                    act.activation(sg[:r, n % 2, :], gp[n % 2][:r, :], ACT.Silu).then_inc(silu_done, 1)

        @block.vector
        def _(dve):
            def product(i, n):
                it, c = n % NI, n // NI
                r = it_rows[it]
                dve.wait_ge(silu_done, NU * i + n + 1)
                if it == 0:
                    dve.wait_ge(y_ready, NY * i + TPC * max(c - 1, 0))
                dve.tensor_tensor(h[:r, c % 2, it, :], sg[:r, n % 2, :], up[n % 2][:r, :], ALU.mult).then_inc(h_done, 1)

            def add(i, n):
                s, t = n // NT, n % NT
                dve.wait_ge(y_ready, NY * i + n + 1)
                dve.scalar_tensor_tensor(out=x_sb[:, t, :], in0=y[n % 4][:, :], scalar=cw[:, t, bass.ds(2 * i + s, 1)],
                                         in1=x_sb[:, t, :], op0=ALU.mult, op1=ALU.add).then_inc(summed, 1)

            with dve.Fori(0, NE // 2) as i:
                dve.wait_ge(summed, NY * i)
                for c in range(2 * NCH + 1):
                    for it in range(NI):
                        if c < 2 * NCH:
                            product(i, NI * c + it)
                        if c >= 1:
                            for q in range(TPC * it // NI, TPC * (it + 1) // NI):
                                if c - 1 == NCH and it == 0 and q == 0:
                                    dve.wait_ge(summed, NY * i + NT)
                                add(i, TPC * (c - 1) + q)


def program(nc, a, out, stop=99, dump=None):
    a = dict(a)
    a["table"] = nc.dram_tensor("token_rows", (T, ROW), F32, kind="Internal").ap()
    a["acc"] = nc.dram_tensor("token_sums", (T, D), F32, kind="Internal").ap()
    rows_t = [P] * NT
    rows_s = tiles_of(S)

    FREE_SEMS.clear()
    FREE_SEMS.extend(sorted(nc.free_semaphores))
    top = ExitStack()
    with top:
        def sb(n, shape, dt=F32):
            return top.enter_context(nc.sbuf_tensor(n, shape, dt))

        def finish(t):
            c, _, _, sem = phase(nc, "finish")
            with c:
                stored = sem("stored")
                block = c.enter_context(nc.Block())

                @block.sync
                def _(sp):
                    sp.dma_start(out.rearrange("o (t p) d -> p (o t) d", p=P), t[:, :, :]).then_inc(stored, 16)
                    sp.wait_ge(stored, 16)

        cols, rows = sb("cols", [P, NCOLS]), sb("rows", [P, NROWS])
        ident, ones = sb("ident", [P, P]), sb("ones", [P, P])
        x = sb("x", [P, NT, D])
        a["ident"] = ident
        load_constants(nc, a, cols, rows, ident, ones, x)

        def col(n):
            o, k = COLS[n]
            return cols[:, o:o + k]

        def row(n):
            o, k = ROWS[n]
            return rows[:, o:o + k]

        def scope():
            c = ExitStack()
            return c, lambda n, shape, dt=F32: c.enter_context(nc.sbuf_tensor(n, shape, dt))

        c, sb1 = scope()
        with c:
            ot = sb1("ot_0", [P, NG, T])
            c2, sb2 = scope()
            with c2:
                ct, xt = sb2("ct_0", [P, 1, S]), sb2("xt_0", [P, KC, T])
                c3, sb3 = scope()
                with c3:
                    ctx_block(nc, a, "ctx_t", ct)
                    xn = sb3("xn_0", [P, NT, D])
                    layernorm(nc, "ln_0", x, xn, rows_t, D, outs=[(xt, None, None)], ident=ident)
                attention(nc, a, "xa0", a["wq0"], a["wk0"], a["wv0"], xt, KC, ct, 1, S, (D // HEADS) ** -0.5, False, ot, ones,
                          bq=col("bq0"), bk=col("bk0"), bv=row("bv0").rearrange("p (g n) -> p g n", n=P))
            project_out(nc, "out0", ot, a["wo0"], row("bo0"), x, x)
        if stop == 0:
            return finish(x)

        c, sb1 = scope()
        with c:
            slots = sb1("slots", [P, E0], U32)
            c2, sb2 = scope()
            with c2:
                z, wc, picks = sb2("z", [P, NT, D]), sb2("wc", [P, NT, E0]), sb2("picks", [E0, T])
                zt, zst = sb2("zt", [P, KC, T]), sb2("zst", [NSTAT, T])
                layernorm(nc, "ln_z", x, z, rows_t, D, outs=[(zt, None, None)], ident=ident)
                router_stats(nc, z, zst, ident)
                router(nc, a, zt, zst, col("r1b"), wc, picks, ident)
                choose(nc, a, picks, z, wc, x, slots, ident)
            experts(nc, a, slots, x, ident)
        if stop == 1:
            return finish(x)

        c, sb1 = scope()
        with c:
            r = sb1("r", [P, NT, D])
            layernorm(nc, "ln_xx", x, r, rows_t, D)
            layernorm(nc, "ln1", r, r, rows_t, D, affine=(row("ln1_g"), row("ln1_b")))
            for n, p in enumerate(("a1", "a2")):
                if n == 1:
                    layernorm(nc, "ln2", r, r, rows_t, D, affine=(row("ln2_g"), row("ln2_b")))
                c2, sb2 = scope()
                with c2:
                    ot = sb2(f"{p}_ot", [P, NG, T])
                    c3, sb3 = scope()
                    with c3:
                        xq = sb3(f"{p}_xq", [P, KC, T])
                        if n == 0:
                            xk, nkk, nkeys = sb3(f"{p}_xk", [P, KC, T]), KC, T
                        else:
                            xk, nkk, nkeys = sb3(f"{p}_xk", [P, 1, S]), 1, S
                        c4, sb4 = scope()
                        with c4:
                            xn = sb4(f"{p}_xn", [P, NT, D])
                            outs = [(xq, col(p + "_lnx_g"), col(p + "_lnx_b"))]
                            if n == 0:
                                outs.append((xk, col(p + "_lny_g"), col(p + "_lny_b")))
                            layernorm(nc, p + "_lnx", r, xn, rows_t, D, outs=outs, ident=ident)
                        if n == 1:
                            c4, sb4 = scope()
                            with c4:
                                cr = sb4("ctx_rows", [P, len(rows_s), C])
                                load_ctx_rows(nc, a, cr)
                                layernorm(nc, p + "_lny", cr, cr, rows_s, C,
                                          outs=[(xk, col(p + "_lny_g"), col(p + "_lny_b"))], ident=ident)
                        attention(nc, a, p, a[p + "_wq"], a[p + "_wk"], a[p + "_wv"], xq, KC, xk, nkk, nkeys, SLOT ** -0.5, n == 0,
                                  ot, ones, ering=2 if n == 0 else 4)
                    xo = sb2(f"{p}_xo", [P, NT, D])
                    project_out(nc, p + "_out", ot, a[p + "_wo"], row(p + "_li1_b"), r, xo)
                    xt = sb2(f"{p}_xt", [P, KC, T])
                    c3, sb3 = scope()
                    with c3:
                        xn = sb3(f"{p}_xn3", [P, NT, D])
                        layernorm(nc, p + "_ln3", xo, xn, rows_t, D, outs=[(xt, col(p + "_ln3_g"), col(p + "_ln3_b"))], ident=ident)
                    gelu_ffn(nc, p + "_ffn", xt, a[p + "_li2"], a[p + "_li3"], col(p + "_li2_b"), row(p + "_li3_b"), xo,
                             [r] if n == 0 else [r, x], r if n == 0 else x)
                if stop == 2 + n:
                    return finish(r if n == 0 else x)

        xt, cw = sb("m_xt", [P, KC, T]), sb("cw", [P, NT, E1 + SH])
        c, sb1 = scope()
        with c:
            xn = sb1("m_xn", [P, NT, D])
            layernorm(nc, "m_ln", x, xn, rows_t, D, outs=[(xt, None, None)], ident=ident)
        gate1(nc, a, xt, row("gate_bias"), cw)
        moe(nc, a, xt, cw, x, out)


def ctx_block(nc, a, name, ct):
    ctx, sb, ps, sem = phase(nc, name)
    with ctx:
        loaded = sem("loaded")
        block = ctx.enter_context(nc.Block())

        @block.sync
        def _(sp):
            sp.dma_start(ct[:, 0, :], a["ctx_t"]).then_inc(loaded, 16)
            sp.wait_ge(loaded, 16)


def load_ctx_rows(nc, a, cr):
    ctx, sb, ps, sem = phase(nc, "ctx_rows_in")
    full = S // P
    with ctx:
        loaded = sem("loaded")
        block = ctx.enter_context(nc.Block())

        @block.sync
        def _(sp):
            sp.dma_start(cr[:, :full, :], a["ctx"][:full * P, :].rearrange("(t p) c -> p t c", p=P)).then_inc(loaded, 16)
            sp.dma_start(cr[:S - full * P, full, :], a["ctx"][full * P:, :]).then_inc(loaded, 16)
            sp.wait_ge(loaded, 32)


def laid_out(i):
    i = {k: np.asarray(v) for k, v in i.items()}

    def blocks(w):
        k, n = w.shape
        return w.reshape(k // P, P, n).transpose(1, 0, 2)

    def slots(w, heads_width):
        k = w.shape[0]
        o = np.zeros((k, HEADS, SLOT), np.float32)
        o[:, :, :heads_width] = w.reshape(k, HEADS, heads_width)
        return o.reshape(k, HEADS * SLOT)

    def grouped(w):
        k = w.shape[0]
        return w.reshape(k // P, P, NG, P).transpose(2, 1, 0, 3)

    dk = D // HEADS
    o = {"x": i["x"], "ctx": i["ctx_512"][0], "ctx_t": i["ctx_512"][0].T}
    o["wq0"] = grouped(slots(i["L0_xattn_Wq"], dk))
    o["wk0"] = grouped(slots(i["L0_xattn_Wk"], dk))
    o["wv0"] = grouped(slots(i["L0_xattn_Wv"], dk))
    o["wo0"] = blocks(slots(i["L0_xattn_Wo"].T, dk).T)
    o["r1"] = blocks(i["L0_ffn_r1_w"][:, :D].T)
    o["r1s"] = i["L0_ffn_r1_w"][:, D:].T
    o["r2"] = i["L0_ffn_r2_w"].T
    up = i["L0_ffn_w_up"].transpose(0, 2, 1).reshape(E0, KC, P, 2 * INTER).transpose(0, 2, 1, 3).reshape(E0, P, -1)
    dn = i["L0_ffn_w_down"].transpose(0, 2, 1).reshape(E0, INTER // P, P, D).transpose(0, 2, 1, 3).reshape(E0, P, -1)
    o["we"] = np.concatenate([up, dn], 2)
    up = i["L0_ffn_a_up"].transpose(0, 2, 1).reshape(AG, KC, P, 2 * AI).transpose(0, 2, 1, 3).reshape(AG, P, -1)
    o["aw"] = np.concatenate([up, i["L0_ffn_a_down"].transpose(0, 2, 1)], 2)
    for p in ("a1", "a2"):
        for n in "qkv":
            w = i[f"L1_xattn_{p}_w{n}"]
            o[f"{p}_w{n}"] = grouped(w.transpose(1, 0, 2).reshape(w.shape[1], HEADS * SLOT))
        o[p + "_wo"] = blocks(i[f"L1_xattn_{p}_li1_w"])
        o[p + "_li2"] = blocks(i[f"L1_xattn_{p}_li2_w"])
        o[p + "_li3"] = blocks(i[f"L1_xattn_{p}_li3_w"])
    o["gw"] = blocks(i["L1_ffn_gate_w"].T)
    gate = np.concatenate([i["L1_ffn_gate_proj"], i["L1_ffn_shared_gate_w"].reshape(SH, EI, D)])
    upw = np.concatenate([i["L1_ffn_up_proj"], i["L1_ffn_shared_up_w"].reshape(SH, EI, D)])
    down = np.concatenate([i["L1_ffn_down_proj"], i["L1_ffn_shared_down_w"].reshape(D, SH, EI).transpose(1, 0, 2)])
    n = E1 + SH
    gu = [w.transpose(0, 2, 1).reshape(n, KC, P, EI).transpose(0, 2, 1, 3).reshape(n, P, -1) for w in (gate, upw)]
    ni = (EI + P - 1) // P
    dn = np.zeros((n, ni * P, D), np.float32)
    dn[:, :EI] = down.transpose(0, 2, 1)
    o["wm"] = np.concatenate([*gu, dn.reshape(n, ni, P, D).transpose(0, 2, 1, 3).reshape(n, P, -1)], 2)
    vec = {"bq0": slots(i["L0_xattn_bq"][None], dk)[0], "bk0": slots(i["L0_xattn_bk"][None], dk)[0], "r1b": i["L0_ffn_r1_b"],
           "bo0": i["L0_xattn_bo"], "bv0": slots(i["L0_xattn_bv"][None], dk)[0], "gate_bias": i["L1_ffn_gate_bias"]}
    for n in ("ln1_g", "ln1_b", "ln2_g", "ln2_b"):
        vec[n] = i["L1_xattn_" + n]
    for n in list(COLS) + list(ROWS):
        if n not in vec:
            vec[n] = i["L1_xattn_" + n]
    o["cols"] = np.concatenate([vec[n].reshape(-1, P).T for n in COLS], 1)
    o["rows"] = np.concatenate([vec[n] for n in ROWS])[None]
    return {k: np.ascontiguousarray(v) for k, v in o.items()}


def kernel(**inputs):
    import concourse.bacc as bacc
    from concourse.bass_utils import run_bass_kernel_spmd

    arrays = {f"in_{k}": v for k, v in laid_out(inputs).items()}
    nc = bacc.Bacc("TRN2", target_bir_lowering=False, num_devices=1)
    a = {k[3:]: nc.dram_tensor(k, v.shape, mybir.dt.from_np(v.dtype), kind="ExternalInput").ap() for k, v in arrays.items()}
    out = nc.dram_tensor("out_x", (1, T, D), F32, kind="ExternalOutput").ap()
    program(nc, a, out)
    r = run_bass_kernel_spmd(nc, [arrays], core_ids=[0])
    return r.results[0]["out_x"]
```

```python
from collections import deque
from contextlib import ExitStack

import numpy as np
import concourse.bass as bass
from concourse import mybir

F32 = mybir.dt.float32
F16 = mybir.dt.float16
U32 = mybir.dt.uint32
ALU = mybir.AluOpType
ACT = mybir.ActivationFunctionType
AX = mybir.AxisListType

P = 128
T = 2048
D = 256
S = 1601
C = 128
NT = T // P
KC = D // P
CH = 512
NCH = T // CH
TPC = CH // P
HEADS = 16
HG = 4
NG = HEADS // HG
SLOT = 32
STACK = 3 * SLOT
EPS = 1e-5

E0, CAP, INTER, AG, AI = 32, 80, 512, 16, 128
NSTAT = 6
ROW = D + E0
E1, EI, SH, TOPK1, G1, TG1 = 16, 352, 2, 4, 4, 2
FF = 1024

COLS, ROWS = {}, {}
_at = 0
for _n, _k in (("bq0", NG), ("bk0", NG), ("r1b", 1),
               ("a1_lnx_g", 2), ("a1_lnx_b", 2), ("a1_lny_g", 2), ("a1_lny_b", 2), ("a1_ln3_g", 2), ("a1_ln3_b", 2),
               ("a1_li2_b", 8),
               ("a2_lnx_g", 2), ("a2_lnx_b", 2), ("a2_lny_g", 1), ("a2_lny_b", 1), ("a2_ln3_g", 2), ("a2_ln3_b", 2),
               ("a2_li2_b", 8)):
    COLS[_n] = (_at, _k)
    _at += _k
NCOLS = _at
_at = 0
for _n, _k in (("bo0", D), ("ln1_g", D), ("ln1_b", D), ("ln2_g", D), ("ln2_b", D), ("a1_li1_b", D), ("a1_li3_b", D),
               ("a2_li1_b", D), ("a2_li3_b", D), ("gate_bias", E1), ("bv0", NG * P)):
    ROWS[_n] = (_at, _k)
    _at += _k
NROWS = _at


def tiles_of(n):
    return [min(P, n - P * t) for t in range((n + P - 1) // P)]


def chunks_of(n):
    return [(CH * c, min(CH, n - CH * c)) for c in range((n + CH - 1) // CH)]


FREE_SEMS = deque()


def phase(nc, name):
    ctx = ExitStack()
    sems = []

    def clear():
        nc.clear_and_free_semaphores(sems)
        FREE_SEMS.extend(s.num for s in sems)

    ctx.callback(clear)

    def sb(n, shape, dt=F32):
        return ctx.enter_context(nc.sbuf_tensor(f"{name}_{n}", shape, dt))

    def ps(n, shape, dt=F32):
        return ctx.enter_context(nc.psum_tensor(f"{name}_{n}", shape, dt))

    def sem(n):
        sems.append(nc.alloc_semaphore(f"{name}_{n}", FREE_SEMS.popleft()))
        return sems[-1]

    return ctx, sb, ps, sem


def load_constants(nc, a, cols, rows, ident, ones, x_sb):
    ctx, sb, ps, sem = phase(nc, "init")
    with ctx:
        loaded, zeroed, made = sem("loaded"), sem("zeroed"), sem("made")
        block = ctx.enter_context(nc.Block())

        @block.sync
        def _(sp):
            sp.dma_start(cols[:, :], a["cols"]).then_inc(loaded, 16)
            sp.dma_start(rows[:, :], a["rows"].partition_broadcast(P).rearrange("p o n -> p (o n)")).then_inc(loaded, 16)
            sp.dma_start(x_sb[:, :, :], a["x"].rearrange("o (t p) d -> p (o t) d", p=P)).then_inc(loaded, 16)
            sp.wait_ge(loaded, 48)

        @block.gpsimd
        def _(pool):
            pool.memset(ident[:, :], 0.0).then_inc(zeroed, 1)
            pool.memset(ones[:, :], 1.0)
            pool.wait_ge(zeroed, 1)
            pool.affine_select(out=ident[:, :], in_=ident[:, :], compare_op=ALU.not_equal, fill=1.0, base=0,
                               pattern=[[-1, P]], channel_multiplier=1).then_inc(made, 1)
            pool.wait_ge(made, 1)


def layernorm(nc, name, src, dst, rows, width, affine=None, outs=(), ident=None):
    ctx, sb, ps, sem = phase(nc, name)
    n = len(rows)
    nk = width // P
    with ctx:
        stats = sb("stats", [P, n, 6])
        mv = sb("mv", [P, n, 2])
        std = sb("std", [P, n])
        rstd = sb("rstd", [P, n])
        eps = sb("eps", [P, 1])
        tp = ps("tp", [P, 4, CH]) if outs else None
        eps_set, stats_done, var_ready = sem("eps_set"), sem("stats_done"), sem("var_ready")
        std_ready, rstd_ready, normed, scaled = sem("std_ready"), sem("rstd_ready"), sem("normed"), sem("scaled")
        ready, turned, taken = sem("ready"), sem("turned"), sem("taken")
        block = ctx.enter_context(nc.Block())
        full = [t for t in range(n) if rows[t] == P]
        spans = [(0, len(full), P)] + [(t, t + 1, rows[t]) for t in range(n) if rows[t] < P]
        groups = [(k, t0, min(t0 + TPC, n)) for t0 in range(0, n, TPC) for k in range(nk)]

        @block.vector
        def _(dve):
            dve.memset(eps[:, :], EPS).then_inc(eps_set, 1)
            for t in range(n):
                r = rows[t]
                dve.bn_stats(stats[:r, t, :], src[:r, t, :]).then_inc(stats_done, 1)
            for t in range(n):
                r = rows[t]
                dve.wait_ge(stats_done, t + 1)
                dve.bn_aggr(mv[:r, t, :], stats[:r, t, :]).then_inc(var_ready, 1)
            for i, (t0, t1, r) in enumerate(spans):
                dve.wait_ge(std_ready, i + 1)
                dve.reciprocal(rstd[:r, t0:t1], std[:r, t0:t1]).then_inc(rstd_ready, 1)
            dve.wait_ge(rstd_ready, len(spans))
            for t in range(n):
                r = rows[t]
                i = dve.tensor_scalar(dst[:r, t, :], src[:r, t, :], mv[:r, t, 0:1], rstd[:r, t:t + 1],
                                      ALU.subtract, ALU.mult)
                if affine is None:
                    i.then_inc(ready, 1)
                    continue
                i.then_inc(normed, 1)
            if affine is not None:
                for t in range(n):
                    dve.wait_ge(normed, t + 1)
                    dve.tensor_tensor(dst[:, t, :], dst[:, t, :], affine[0], ALU.mult).then_inc(scaled, 1)
                for t in range(n):
                    dve.wait_ge(scaled, t + 1)
                    dve.tensor_tensor(dst[:, t, :], dst[:, t, :], affine[1], ALU.add).then_inc(ready, 1)

        @block.scalar
        def _(act):
            act.wait_ge(eps_set, 1)
            act.wait_ge(var_ready, n)
            for t0, t1, r in spans:
                act.activation(std[:r, t0:t1], mv[:r, t0:t1, 1], ACT.Sqrt, bias=eps[:r, 0:1]).then_inc(std_ready, 1)
            for i, (k, t0, t1) in enumerate(groups if outs else ()):
                w = sum(rows[t0:t1])
                act.wait_ge(turned, i + 1)
                for target, g, b in outs:
                    o = target[:, k, P * t0:P * t0 + w]
                    if g is None:
                        last = act.activation(o, tp[:, i % 4, :w], ACT.Copy)
                    else:
                        last = act.activation(o, tp[:, i % 4, :w], ACT.Identity, bias=b[:, k:k + 1], scale=g[:, k:k + 1])
                last.then_inc(taken, 1)

        if outs:
            @block.tensor
            def _(pe):
                for i, (k, t0, t1) in enumerate(groups):
                    pe.wait_ge(ready, t1)
                    if i >= 4:
                        pe.wait_ge(taken, i - 3)
                    for t in range(t0, t1):
                        r = rows[t]
                        o = P * (t - t0)
                        last = pe.transpose(tp[:, i % 4, o:o + r], dst[:r, t, P * k:P * k + P], ident[:r, :r])
                    last.then_inc(turned, 1)


def attention(nc, a, name, wq, wk, wv, xq, nkq, xk, nkk, nkeys, scale, causal, ot, ones, bq=None, bk=None, bv=None, ering=4):
    ctx, sb, ps, sem = phase(nc, name)
    kt_rows = tiles_of(nkeys)
    nkt = len(kt_rows)
    kch = chunks_of(nkeys)
    nmx = 4
    mxw = (nkeys + nmx - 1) // nmx
    mxs = [min(mxw * i, nkeys - mxw) for i in range(nmx)]
    nvb = (nkt + 3) // 4
    NC = NG * NCH
    NST = 3
    MOVES = 16 * 3 * HG

    def maxima(n):
        return [("max", n, t, j, i) for t in range(TPC) for j in range(HG) for i in range(nmx)] + [("turn", n)]

    before = [("k", 0, c) for c in range(len(kch))] + [("q", 0), ("q", 1)] + [("v", 0, b) for b in range(nvb)] + maxima(0)
    during = []
    for n in range(NC):
        g, qc = n // NCH, n % NCH
        work = [("q", n + 2)] if n + 2 < NC else []
        if g + 1 < NG:
            work += {0: [("k", g + 1, c) for c in range(2)], 1: [("k", g + 1, c) for c in range(2, len(kch))],
                     2: [("v", g + 1, b) for b in range(nvb)]}.get(qc, [])
        during.append(work + (maxima(n + 1) if n + 1 < NC else []))
    order = before + [u for work in during for u in work]
    number = {u: i for i, u in enumerate(order)}
    staged = {u: i for i, u in enumerate(u for u in order if u[0] in "kq")}

    with ctx:
        wqs = sb("wqs", [P, NG, nkq, P])
        wks = sb("wks", [P, NG, nkk, P])
        wvs = sb("wvs", [P, NG, nkk, P])
        stage = sb("stage", [P, NST, 2, CH], F16)
        qs = sb("qs", [P, HG, NCH, CH], F16)
        ks = sb("ks", [P, 2, HG, nkeys + nkeys % 2], F16)
        v = sb("v", [P, 2, nkt, P])
        e = sb("e", [P, ering, HG, CH])
        em = sb("em", [P, 2, HG, P]) if causal else None
        later = sb("later", [P, P]) if causal else None
        part_max = sb("part_max", [P, HG, TPC, nmx])
        row_max = sb("row_max", [P, HG, TPC])
        neg_max = sb("neg_max", [HG * TPC, P], F16)
        rden = sb("rden", [P, CH])
        wb = [ps(f"wb{i}", [P, CH]) for i in range(2)]
        sc = [ps(f"sc{i}", [P, 2, CH]) for i in range(2)]
        po = ps("po", [P, CH])
        pd = ps("pd", [P, CH])

        w_loaded, ones_set, mask_filled = sem("w_loaded"), sem("ones_set"), sem("mask_filled")
        unit_ready, unit_taken, high_ready = sem("unit_ready"), sem("unit_taken"), sem("high_ready")
        split_ready = sem("split_ready")
        stacked = [sem(f"stacked{i}") for i in range(NST)]
        rowmax_ready, negmax_ready, negmax_loaded = sem("rowmax_ready"), sem("negmax_ready"), sem("negmax_loaded")
        sc_ready, exp_done, masked, pv_done = sem("sc_ready"), sem("exp_done"), sem("masked"), sem("pv_done")
        rden_ready, o_taken = sem("rden_ready"), sem("o_taken")
        block = ctx.enter_context(nc.Block())

        def wait_stacked(eng, unit):
            i = staged[unit]
            eng.wait_ge(stacked[i % NST], MOVES * (i // NST + 1))

        @block.sync
        def _(sp):
            sp.dma_start(wks[:, :, :, :], wk.rearrange("g p k n -> p g k n")).then_inc(w_loaded, 16)
            sp.dma_start(wqs[:, :, :, :], wq.rearrange("g p k n -> p g k n")).then_inc(w_loaded, 16)
            sp.dma_start(wvs[:, :, :, :], wv.rearrange("g p k n -> p g k n")).then_inc(w_loaded, 16)
            for u in order:
                if u[0] in "kq":
                    i = staged[u]
                    sp.wait_ge(split_ready, i + 1)
                    if u[0] == "k":
                        g, (o, w) = u[1], kch[u[2]]
                        if g >= 2:
                            sp.wait_ge(pv_done, nkt * NCH * (g - 1))
                        dst = [ks[SLOT * s:SLOT * s + SLOT, g % 2, j, o:o + w] for s in range(3) for j in range(HG)]
                        parts = (0, 1, 0)
                    else:
                        n, w = u[1], CH
                        if n >= NCH:
                            sp.wait_ge(pv_done, nkt * (n - NCH + 1))
                        dst = [qs[SLOT * s:SLOT * s + SLOT, j, n % NCH, :] for s in range(3) for j in range(HG)]
                        parts = (0, 0, 1)
                    for m, d in enumerate(dst):
                        h = SLOT * (m % HG)
                        sp.dma_start(d, stage[h:h + SLOT, i % NST, parts[m // HG], :w]).then_inc(stacked[i % NST], 16)
                if u[0] == "turn":
                    n = u[1]
                    sp.wait_ge(negmax_ready, n + 1)
                    for j in range(HG):
                        sp.dma_start(qs[STACK:STACK + 1, j, n % NCH, :].rearrange("o (t q) -> o t q", t=TPC),
                                     neg_max[TPC * j:TPC * j + TPC, :]).then_inc(negmax_loaded, 16)

        if causal:
            @block.gpsimd
            def _(pool):
                pool.memset(later[:, :], 1.0).then_inc(mask_filled, 1)
                pool.wait_ge(mask_filled, 1)
                pool.affine_select(out=later[:, :], in_=later[:, :], compare_op=ALU.is_gt, fill=0.0, base=0,
                                   pattern=[[-1, P]], channel_multiplier=1).then_inc(mask_filled, 1)
                pool.wait_ge(mask_filled, 2)
                for n in range(NC):
                    for i in range(TPC):
                        kt = TPC * (n % NCH) + i
                        pool.wait_ge(exp_done, 2 * (nkt * n + kt + 1))
                        if TPC * n + i >= 2:
                            before_n, before_kt = (n, kt - 2) if i >= 2 else (n - 1, TPC * ((n - 1) % NCH) + i + 2)
                            pool.wait_ge(pv_done, nkt * before_n + before_kt + 1)
                        pool.tensor_tensor(em[:, kt % 2, :, :], e[:, (nkt * n + kt) % ering, :, P * i:P * i + P],
                                           later[:, :].unsqueeze(1).to_broadcast([P, HG, P]), ALU.mult).then_inc(masked, 1)

        @block.scalar
        def _(act):
            for m in range(nkt * NC):
                r = kt_rows[m % nkt]
                for half in range(2):
                    act.wait_ge(sc_ready, 2 * m + half + 1)
                    if m >= ering:
                        act.wait_ge(pv_done, m - ering + 1)
                    act.activation(e[:r, m % ering, 2 * half:2 * half + 2, :], sc[half][:r, :, :], ACT.Exp,
                                   scale=scale).then_inc(exp_done, 1)

        @block.vector
        def _(dve):
            dve.memset(ks[STACK:STACK + 1, :, :, :], 1.0).then_inc(ones_set, 1)

            def take(u):
                i = number[u]
                src = wb[i % 2]
                if u[0] in "kq":
                    m = staged[u]
                    g = u[1] if u[0] == "k" else u[1] // NCH
                    w = kch[u[2]][1] if u[0] == "k" else CH
                    bias = bk if u[0] == "k" else bq
                    bias = bias[:, g:g + 1] if bias is not None else 0.0
                    high, low = (stage[:, m % NST, k, :w] for k in range(2))
                    dve.wait_ge(unit_ready, i + 1)
                    if m >= NST:
                        dve.wait_ge(stacked[m % NST], MOVES * (m // NST))
                    dve.tensor_scalar(high, src[:, :w], bias, None, ALU.add).then_inc(high_ready, 1)
                    dve.wait_ge(high_ready, m + 1)
                    last = dve.scalar_tensor_tensor(out=low, in0=src[:, :w], scalar=bias, in1=high, op0=ALU.add, op1=ALU.subtract)
                    last.then_inc(split_ready, 1)
                    dve.wait_ge(split_ready, m + 1)
                    dve.sem_inc(unit_taken, 1)
                elif u[0] == "v":
                    g, b = u[1:]
                    dve.wait_ge(unit_ready, i + 1)
                    if g >= 2:
                        dve.wait_ge(pv_done, nkt * NCH * (g - 1))
                    ts = range(4 * b, min(4 * b + 4, nkt))
                    whole = [t for t in ts if kt_rows[t] == P]
                    src = src[:, :].rearrange("p (t n) -> p t n", n=P)
                    if whole:
                        last = dve.tensor_copy(v[:, g % 2, whole[0]:whole[-1] + 1, :], src[:, :len(whole), :])
                    for t in ts:
                        r = kt_rows[t]
                        if r < P:
                            last = dve.tensor_copy(v[:r, g % 2, t, :], src[:r, t - 4 * b, :])
                    last.then_inc(unit_taken, 1)
                elif u[0] == "max":
                    n, t, j, k = u[1:]
                    dve.wait_ge(unit_ready, i + 1)
                    dve.tensor_reduce(part_max[:, j, t, k:k + 1], src[:, :mxw], AX.X, ALU.max).then_inc(unit_taken, 1)
                else:
                    n = u[1]
                    dve.wait_ge(unit_taken, i)
                    dve.tensor_reduce(row_max[:, :, :], part_max[:, :, :, :], AX.X, ALU.max).then_inc(rowmax_ready, 1)
                    dve.wait_ge(unit_ready, i + 1)
                    if n:
                        dve.wait_ge(negmax_loaded, 16 * HG * n)
                    dve.tensor_scalar(neg_max[:, :], src[:HG * TPC, :P], -1.0, None, ALU.mult).then_inc(negmax_ready, 1)
                    dve.wait_ge(negmax_ready, n + 1)
                    dve.sem_inc(unit_taken, 1)

            for u in before:
                take(u)
            for n in range(NC):
                g, qc = n // NCH, n % NCH
                for u in during[n]:
                    take(u)
                dve.wait_ge(pv_done, nkt * (n + 1))
                dve.reciprocal(rden[:, :], pd[:, :]).then_inc(rden_ready, 1)
                dve.wait_ge(rden_ready, n + 1)
                dve.tensor_tensor(ot[:, g, CH * qc:CH * qc + CH], po[:, :], rden[:, :], ALU.mult).then_inc(o_taken, 1)

        @block.tensor
        def _(pe):
            def unit(u):
                i = number[u]
                dst = wb[i % 2]
                if i >= 2:
                    pe.wait_ge(unit_taken, i - 1)
                if u[0] == "k":
                    g, (o, w) = u[1], kch[u[2]]
                    for k in range(nkk):
                        last = pe.matmul(dst[:, :w], wks[:, g, k, :], xk[:, k, o:o + w], start=(k == 0), stop=(k == nkk - 1))
                elif u[0] == "q":
                    g, o = u[1] // NCH, CH * (u[1] % NCH)
                    for k in range(nkq):
                        last = pe.matmul(dst[:, :], wqs[:, g, k, :], xq[:, k, o:o + CH], start=(k == 0), stop=(k == nkq - 1))
                elif u[0] == "v":
                    g, b = u[1:]
                    for t in range(4 * b, min(4 * b + 4, nkt)):
                        r = kt_rows[t]
                        o = dst[:r, P * (t - 4 * b):P * (t - 4 * b) + P]
                        for k in range(nkk):
                            last = pe.matmul(o, xk[:, k, P * t:P * t + r], wvs[:, g, k, :], start=(k == 0),
                                             stop=(k == nkk - 1 and bv is None))
                        if bv is not None:
                            last = pe.matmul(o, ones[0:1, :r], bv[0:1, g, :], start=False, stop=True)
                elif u[0] == "max":
                    n, t, j, k = u[1:]
                    g = n // NCH
                    if (t, j, k) == (0, 0, 0):
                        wait_stacked(pe, ("q", n))
                        if n % NCH == 0:
                            for c in range(len(kch)):
                                wait_stacked(pe, ("k", g, c))
                    last = pe.matmul(dst[:, :mxw], qs[:STACK, j, n % NCH, P * t:P * t + P],
                                     ks[:STACK, g % 2, j, mxs[k]:mxs[k] + mxw], start=True, stop=True)
                else:
                    pe.wait_ge(rowmax_ready, u[1] + 1)
                    last = pe.transpose(dst[:HG * TPC, :P], row_max[:, :, :].rearrange("p j t -> p (j t)"), a["ident"][:, :])
                last.then_inc(unit_ready, 1)

            def score(n, kt, half):
                m = nkt * n + kt
                r = kt_rows[kt]
                if m >= 1:
                    pe.wait_ge(exp_done, 2 * (m - 1) + half + 1)
                for i in range(2):
                    j = 2 * half + i
                    last = pe.matmul(sc[half][:r, i, :], ks[:STACK + 1, n // NCH % 2, j, P * kt:P * kt + r],
                                     qs[:STACK + 1, j, n % NCH, :], start=True, stop=True)
                last.then_inc(sc_ready, 1)

            def sum_values(n, kt):
                m = nkt * n + kt
                r = kt_rows[kt]
                first = TPC * (n % NCH) if causal else 0
                pe.wait_ge(exp_done, 2 * m + 2)
                if kt == 0 and n:
                    pe.wait_ge(o_taken, n)
                if kt < first:
                    return
                i = kt - first
                diagonal = causal and i < TPC
                if diagonal:
                    pe.wait_ge(masked, TPC * n + i + 1)
                for j in range(HG):
                    h = SLOT * j
                    w = v[:r, n // NCH % 2, kt, h:h + SLOT]
                    stop = kt == nkt - 1
                    if not diagonal:
                        pe.matmul(po[h:h + SLOT, :], w, e[:r, m % ering, j, :], start=(kt == first), stop=stop)
                        continue
                    if i:
                        pe.matmul(po[h:h + SLOT, :P * i], w, e[:r, m % ering, j, :P * i], start=False, stop=False)
                    pe.matmul(po[h:h + SLOT, P * i:P * i + P], w, em[:r, kt % 2, j, :], start=(i == 0), stop=stop)

            def sum_weights(n, kt):
                m = nkt * n + kt
                r = kt_rows[kt]
                for j in range(HG):
                    h = SLOT * j
                    last = pe.matmul(pd[h:h + SLOT, :], ones[:r, :SLOT], e[:r, m % ering, j, :],
                                     start=(kt == 0), stop=(kt == nkt - 1))
                last.then_inc(pv_done, 1)

            pe.wait_ge(ones_set, 1)
            pe.wait_ge(w_loaded, 48)
            for u in before:
                unit(u)
            for n in range(NC):
                work = iter(during[n])
                steps = 4 * (nkt - 1)
                sent, step = 0, 0

                def some_work():
                    nonlocal sent, step
                    step += 1
                    while sent < min(len(during[n]), -(-len(during[n]) * step // steps)):
                        unit(next(work))
                        sent += 1

                pe.wait_ge(negmax_loaded, 16 * HG * (n + 1))
                for kt in range(nkt + 1):
                    if kt < nkt:
                        score(n, kt, 0)
                        some_work()
                    if kt >= 1:
                        sum_values(n, kt - 1)
                        some_work()
                    if kt < nkt:
                        score(n, kt, 1)
                        some_work()
                    if kt >= 1:
                        sum_weights(n, kt - 1)
                        some_work()
                for u in work:
                    unit(u)


def project_out(nc, name, ot, wo_dram, bias, res, dst):
    ctx, sb, ps, sem = phase(nc, name)
    with ctx:
        wo = sb("wo", [P, NG, D])
        y = [ps(f"y{i}", [P, D]) for i in range(4)]
        w_loaded, y_ready, summed, biased = sem("w_loaded"), sem("y_ready"), sem("summed"), sem("biased")
        block = ctx.enter_context(nc.Block())

        @block.sync
        def _(sp):
            sp.dma_start(wo[:, :, :], wo_dram).then_inc(w_loaded, 16)

        @block.tensor
        def _(pe):
            pe.wait_ge(w_loaded, 16)
            for t in range(NT):
                if t >= 4:
                    pe.wait_ge(summed, t - 3)
                for g in range(NG):
                    last = pe.matmul(y[t % 4][:, :], ot[:, g, P * t:P * t + P], wo[:, g, :], start=(g == 0), stop=(g == NG - 1))
                last.then_inc(y_ready, 1)

        @block.vector
        def _(dve):
            for t in range(NT):
                dve.wait_ge(y_ready, t + 1)
                dve.tensor_tensor(dst[:, t, :], y[t % 4][:, :], res[:, t, :], ALU.add).then_inc(summed, 1)

        @block.gpsimd
        def _(pool):
            for t in range(NT):
                pool.wait_ge(summed, t + 1)
                pool.tensor_tensor(dst[:, t, :], dst[:, t, :], bias, ALU.add).then_inc(biased, 1)


def gelu_ffn(nc, name, xt, w2_dram, w3_dram, b2, b3, xo, adds, dst):
    ctx, sb, ps, sem = phase(nc, name)
    nj = FF // P
    with ctx:
        w2 = sb("w2", [P, KC, FF])
        w3 = sb("w3", [P, nj, D])
        h = sb("h", [P, 2, nj, CH])
        hp = [ps(f"hp{i}", [P, CH]) for i in range(4)]
        y = [ps(f"y{i}", [P, D]) for i in range(4)]
        w_loaded, based = sem("w_loaded"), sem("based")
        h_ready, h_done, y_ready, summed = sem("h_ready"), sem("h_done"), sem("y_ready"), sem("summed")
        block = ctx.enter_context(nc.Block())

        @block.sync
        def _(sp):
            sp.dma_start(w2[:, :, :], w2_dram).then_inc(w_loaded, 16)
            sp.dma_start(w3[:, :, :], w3_dram).then_inc(w_loaded, 16)

        @block.gpsimd
        def _(pool):
            for i, add in enumerate(adds):
                if i:
                    pool.wait_ge(based, i)
                pool.tensor_tensor(xo[:, :, :], xo[:, :, :], add[:, :, :], ALU.add).then_inc(based, 1)
            pool.wait_ge(based, len(adds))
            for t in range(NT):
                pool.tensor_tensor(xo[:, t, :], xo[:, t, :], b3, ALU.add).then_inc(based, 1)

        @block.tensor
        def _(pe):
            pe.wait_ge(w_loaded, 32)

            def hidden(c, j):
                n = nj * c + j
                if n >= 4:
                    pe.wait_ge(h_done, n - 3)
                for k in range(KC):
                    last = pe.matmul(hp[n % 4][:, :], w2[:, k, P * j:P * j + P], xt[:, k, CH * c:CH * c + CH],
                                     start=(k == 0), stop=(k == KC - 1))
                last.then_inc(h_ready, 1)

            def out(t):
                pe.wait_ge(h_done, nj * (t // TPC + 1))
                if t >= 4:
                    pe.wait_ge(summed, t - 3)
                q = P * (t % TPC)
                for j in range(nj):
                    last = pe.matmul(y[t % 4][:, :], h[:, t // TPC % 2, j, q:q + P], w3[:, j, :], start=(j == 0), stop=(j == nj - 1))
                last.then_inc(y_ready, 1)

            for c in range(NCH + 1):
                for i in range(nj):
                    if c < NCH:
                        hidden(c, i)
                    if c >= 1 and i % 2 == 1:
                        out(TPC * (c - 1) + i // 2)

        @block.scalar
        def _(act):
            for n in range(nj * NCH):
                c, j = n // nj, n % nj
                act.wait_ge(h_ready, n + 1)
                if c >= 2 and j == 0:
                    act.wait_ge(y_ready, TPC * (c - 1))
                act.activation(h[:, c % 2, j, :], hp[n % 4][:, :], ACT.Gelu, bias=b2[:, j:j + 1]).then_inc(h_done, 1)

        @block.vector
        def _(dve):
            for t in range(NT):
                dve.wait_ge(y_ready, t + 1)
                dve.wait_ge(based, len(adds) + t + 1)
                dve.tensor_tensor(dst[:, t, :], y[t % 4][:, :], xo[:, t, :], ALU.add).then_inc(summed, 1)


class Chain:

    def __init__(self, engine, sem):
        self.engine, self.sem, self.n = engine, sem, 0

    def __call__(self, instruction):
        self.n += 1
        instruction.then_inc(self.sem, 1)
        self.engine.wait_ge(self.sem, self.n)


def over(ap, n):
    return ap.unsqueeze(2).to_broadcast([ap.shape[0], ap.shape[1], n])


def router_stats(nc, z, zst, ident):
    ctx, sb, ps, sem = phase(nc, "stats")
    with ctx:
        st = sb("st", [P, NT, 6])
        mv = sb("mv", [P, NT, 2])
        sq = sb("sq", [P, NT])
        f = sb("f", [P, NT, NSTAT])
        small = sb("small", [P, NT, D])
        tp = [ps(f"tp{i}", [NSTAT, CH]) for i in range(NCH)]
        chain, sums_ready, roots_ready, turned, taken = sem("chain"), sem("sums_ready"), sem("roots_ready"), sem("turned"), sem("taken")
        block = ctx.enter_context(nc.Block())

        @block.vector
        def _(dve):
            link = Chain(dve, chain)
            for t in range(NT):
                last = dve.bn_stats(st[:, t, :], z[:, t, :])
            link(last)
            for t in range(NT):
                last = dve.bn_aggr(mv[:, t, :], st[:, t, :])
            link(last)
            dve.tensor_copy(f[:, :, 0], mv[:, :, 0])
            link(dve.tensor_tensor(sq[:, :], mv[:, :, 0], mv[:, :, 0], ALU.mult))
            dve.tensor_tensor(sq[:, :], sq[:, :], mv[:, :, 1], ALU.add).then_inc(sums_ready, 1)
            dve.tensor_reduce(f[:, :, 2], z[:, :, :], AX.X, ALU.min)
            dve.tensor_reduce(f[:, :, 3], z[:, :, :], AX.X, ALU.max)
            link(dve.tensor_scalar(small[:, :, :], z[:, :, :], 1e-6, None, ALU.is_lt))
            flat_z, flat_small = (v[:, :, :].rearrange("p t d -> p (t d)") for v in (z, small))
            link(dve.scalar_tensor_tensor(out=flat_small, in0=flat_z, scalar=-1e-6, in1=flat_small, op0=ALU.is_gt, op1=ALU.mult))
            link(dve.tensor_reduce(f[:, :, 5], small[:, :, :], AX.X, ALU.add))
            link(dve.tensor_scalar(f[:, :, 5], f[:, :, 5], 1.0 / D, None, ALU.mult))
            for c in range(NCH):
                dve.wait_ge(turned, c + 1)
                dve.tensor_copy(zst[:NSTAT, CH * c:CH * c + CH], tp[c][:, :]).then_inc(taken, 1)

        @block.scalar
        def _(act):
            act.wait_ge(sums_ready, 1)
            act.activation(f[:, :, 4], sq[:, :], ACT.Sqrt, scale=float(D)).then_inc(roots_ready, 1)
            act.activation(f[:, :, 1], mv[:, :, 1], ACT.Sqrt, scale=D / (D - 1.0)).then_inc(roots_ready, 1)

        @block.tensor
        def _(pe):
            pe.wait_ge(roots_ready, 2)
            pe.wait_ge(chain, 7)
            for c in range(NCH):
                for i in range(TPC):
                    last = pe.transpose(tp[c][:, P * i:P * i + P], f[:, TPC * c + i, :], ident[:, :])
                last.then_inc(turned, 1)


def router(nc, a, zt, zst, r1b, wc, picks, ident):
    ctx, sb, ps, sem = phase(nc, "router")
    with ctx:
        r1 = sb("r1", [P, KC, P])
        r1s = sb("r1s", [NSTAT, P])
        r2 = sb("r2", [P, E0])
        h = sb("h", [P, T])
        hp = [ps(f"hp{i}", [P, CH]) for i in range(2)]
        lg = ps("lg", [P, NT, E0])
        tp = [ps(f"tp{i}", [E0, CH]) for i in range(NCH)]
        pr = sb("pr", [P, NT, E0])
        top = sb("top", [P, NT, 8])
        at = sb("at", [P, NT, 8], U32)
        atf = sb("atf", [P, NT, 8])
        iota = sb("iota", [P, NT, E0])
        mask = sb("mask", [P, NT, E0])
        one = sb("one", [P, NT, E0])
        m = sb("m", [P, NT])
        w_loaded, iota_ready, chain = sem("w_loaded"), sem("iota_ready"), sem("chain")
        h_ready, h_done, logits_ready, shifted, exped = sem("h_ready"), sem("h_done"), sem("logits_ready"), sem("shifted"), sem("exped")
        picked, turned, taken = sem("picked"), sem("turned"), sem("taken")
        block = ctx.enter_context(nc.Block())

        @block.sync
        def _(sp):
            sp.dma_start(r1[:, :, :], a["r1"]).then_inc(w_loaded, 16)
            sp.dma_start(r1s[:, :], a["r1s"]).then_inc(w_loaded, 16)
            sp.dma_start(r2[:, :], a["r2"]).then_inc(w_loaded, 16)

        @block.gpsimd
        def _(pool):
            pool.iota(iota[:, :, :], [[0, NT], [1, E0]], base=0, channel_multiplier=0,
                      allow_small_or_imprecise_dtypes=True).then_inc(iota_ready, 1)

        @block.tensor
        def _(pe):
            pe.wait_ge(w_loaded, 48)
            for c in range(NCH):
                if c >= 2:
                    pe.wait_ge(h_done, c - 1)
                o = hp[c % 2][:, :]
                x = slice(CH * c, CH * c + CH)
                for k in range(KC):
                    pe.matmul(o, r1[:, k, :], zt[:, k, x], start=(k == 0), stop=False)
                pe.matmul(o, r1s[:, :], zst[:NSTAT, x], start=False, stop=True).then_inc(h_ready, 1)
            for t in range(NT):
                pe.wait_ge(h_done, t // TPC + 1)
                last = pe.matmul(lg[:, t, :], h[:, P * t:P * t + P], r2[:, :], start=True, stop=True)
            last.then_inc(logits_ready, 1)
            pe.wait_ge(picked, 1)
            for c in range(NCH):
                for i in range(TPC):
                    last = pe.transpose(tp[c][:, P * i:P * i + P], one[:, TPC * c + i, :], ident[:, :])
                last.then_inc(turned, 1)

        @block.scalar
        def _(act):
            for c in range(NCH):
                act.wait_ge(h_ready, c + 1)
                act.activation(h[:, CH * c:CH * c + CH], hp[c % 2][:, :], ACT.Gelu, bias=r1b).then_inc(h_done, 1)
            act.wait_ge(shifted, 1)
            act.activation(pr[:, :, :], pr[:, :, :], ACT.Exp).then_inc(exped, 1)

        @block.vector
        def _(dve):
            link = Chain(dve, chain)
            dve.wait_ge(logits_ready, 1)
            link(dve.tensor_reduce(m[:, :], lg[:, :, :], AX.X, ALU.max))
            dve.tensor_tensor(pr[:, :, :], lg[:, :, :], over(m[:, :], E0), ALU.subtract).then_inc(shifted, 1)
            dve.wait_ge(exped, 1)
            link(dve.tensor_reduce(m[:, :], pr[:, :, :], AX.X, ALU.add))
            link(dve.reciprocal(m[:, :], m[:, :]))
            link(dve.tensor_tensor(pr[:, :, :], pr[:, :, :], over(m[:, :], E0), ALU.mult))
            for t in range(NT):
                last = dve.max(top[:, t, :], pr[:, t, :])
            link(last)
            for t in range(NT):
                last = dve.max_index(at[:, t, :], top[:, t, :], pr[:, t, :])
            link(last)
            link(dve.tensor_copy(atf[:, :, :], at[:, :, :]))
            dve.wait_ge(iota_ready, 1)
            dve.tensor_tensor(mask[:, :, :], iota[:, :, :], over(atf[:, :, 0], E0), ALU.is_equal)
            link(dve.tensor_tensor(one[:, :, :], iota[:, :, :], over(atf[:, :, 1], E0), ALU.is_equal))
            dve.tensor_tensor(m[:, :], top[:, :, 0], top[:, :, 1], ALU.add)
            link(dve.tensor_tensor(mask[:, :, :], mask[:, :, :], one[:, :, :], ALU.add))
            link(dve.reciprocal(m[:, :], m[:, :]))
            link(dve.tensor_tensor(pr[:, :, :], pr[:, :, :], mask[:, :, :], ALU.mult))
            dve.tensor_tensor(wc[:, :, :], pr[:, :, :], over(m[:, :], E0), ALU.mult)
            link(dve.tensor_scalar(mask[:, :, :], mask[:, :, :], 1.0, None, ALU.subtract))
            dve.tensor_tensor(one[:, :, :], pr[:, :, :], mask[:, :, :], ALU.add).then_inc(picked, 1)
            for c in range(NCH):
                dve.wait_ge(turned, c + 1)
                dve.tensor_copy(picks[:, CH * c:CH * c + CH], tp[c][:, :]).then_inc(taken, 1)


def choose(nc, a, picks, z, wc, x_sb, slots, ident):
    ctx, sb, ps, sem = phase(nc, "choose")
    with ctx:
        other = sb("other", [E0, T])
        val = sb("val", [E0, CAP])
        at = sb("at", [E0, CAP], U32)
        atf = sb("atf", [E0, CAP])
        tp = ps("tp", [CAP, E0])
        chain, at_ready, turned, stored = sem("chain"), sem("at_ready"), sem("turned"), sem("stored")
        block = ctx.enter_context(nc.Block())

        @block.sync
        def _(sp):
            rows = a["table"].rearrange("(t p) c -> p t c", p=P)
            sp.dma_start(rows[:, :, :D], z[:, :, :]).then_inc(stored, 16)
            sp.dma_start(rows[:, :, D:], wc[:, :, :]).then_inc(stored, 16)
            sp.dma_start(a["acc"].rearrange("(t p) d -> p t d", p=P), x_sb[:, :, :]).then_inc(stored, 16)
            sp.wait_ge(stored, 48)

        @block.vector
        def _(dve):
            link = Chain(dve, chain)
            buf = [picks, other]
            for r in range(CAP // 8):
                src, dst = buf[r % 2], buf[(r + 1) % 2]
                o = slice(8 * r, 8 * r + 8)
                link(dve.max(val[:, o], src[:, :]))
                link(dve.max_index(at[:, o], val[:, o], src[:, :]))
                if r < CAP // 8 - 1:
                    link(dve.match_replace(dst[:, :], val[:, o], src[:, :], -2.0))
            dve.tensor_copy(atf[:, :], at[:, :]).then_inc(at_ready, 1)
            dve.wait_ge(turned, 1)
            link(dve.tensor_copy(slots[:CAP, :], tp[:, :]))

        @block.tensor
        def _(pe):
            pe.wait_ge(at_ready, 1)
            pe.transpose(tp[:, :], atf[:, :], ident[:E0, :E0]).then_inc(turned, 1)


def experts(nc, a, slots, x_sb, ident):
    ctx, sb, ps, sem = phase(nc, "experts")
    NJ = INTER // P
    UP = KC * 2 * INTER
    with ctx:
        xe = sb("xe", [CAP, E0, ROW])
        xet = sb("xet", [P, KC, E0, CAP])
        we = sb("we", [CAP, E0])
        w = [sb(f"w{i}", [P, UP + NJ * D]) for i in range(2)]
        aw = sb("aw", [P, KC * 2 * AI + D])
        sg = [sb(f"sg{i}", [P, NJ + 1, CAP]) for i in range(2)]
        h = [sb(f"h{i}", [P, NJ + 1, CAP]) for i in range(2)]
        ye = [sb(f"ye{i}", [CAP, D]) for i in range(2)]
        gp = [ps(f"gp{i}", [P, NJ + 1, CAP]) for i in range(2)]
        up = [ps(f"up{i}", [P, NJ + 1, CAP]) for i in range(2)]
        y = [ps(f"y{i}", [CAP, D]) for i in range(2)]
        tp = [ps(f"tp{i}", [P, 4, CAP]) for i in range(2)]
        gathered, turned, taken, we_ready = sem("gathered"), sem("turned"), sem("taken"), sem("we_ready")
        w_loaded = [sem(f"w_loaded{i}") for i in range(2)]
        aw_loaded = sem("aw_loaded")
        g_ready, u_ready, silu_done, h_done = sem("g_ready"), sem("u_ready"), sem("silu_done"), sem("h_done")
        y_ready, ye_ready, added, back = sem("y_ready"), sem("ye_ready"), sem("added"), sem("back")
        block = ctx.enter_context(nc.Block())

        @block.sync
        def _(sp):
            with sp.Fori(0, E0 // 2) as i:
                for s in range(2):
                    sp.wait_ge(y_ready, 2 * i)
                    if s == 0:
                        sp.dma_start(aw[:, :], a["aw"][bass.ds(i, 1)].rearrange("o p n -> (o p) n")).then_inc(aw_loaded, 16)
                    sp.dma_start(w[s][:, :], a["we"][bass.ds(2 * i + s, 1)].rearrange("o p n -> (o p) n")).then_inc(w_loaded[s], 16)
            sp.wait_ge(added, 16 * E0)
            sp.dma_start(x_sb[:, :, :], a["acc"].rearrange("(t p) d -> p t d", p=P)).then_inc(back, 16)
            sp.wait_ge(back, 16)

        @block.gpsimd
        def _(pool):
            for e in range(E0):
                pool.indirect_dma_start(xe[:, e, :], None, a["table"],
                                        bass.IndirectOffsetOnAxis(slots[:CAP, e:e + 1], 0)).then_inc(gathered, 16)
            for e in range(E0):
                pool.wait_ge(ye_ready, e + 1)
                if e >= 1:
                    pool.wait_ge(added, 16 * e)
                pool.indirect_dma_start(a["acc"], bass.IndirectOffsetOnAxis(slots[:CAP, e:e + 1], 0), ye[e % 2][:, :], None,
                                        compute_op=ALU.add).then_inc(added, 16)

        @block.tensor
        def _(pe):
            pe.wait_ge(gathered, 16 * E0)
            n = 0
            for e0 in range(0, E0, 4):
                for k in range(KC):
                    if n >= 2:
                        pe.wait_ge(taken, n - 1)
                    for e in range(e0, e0 + 4):
                        last = pe.transpose(tp[n % 2][:, e - e0, :], xe[:, e, P * k:P * k + P], ident[:CAP, :CAP])
                    last.then_inc(turned, 1)
                    n += 1
            pe.wait_ge(taken, n)
            with pe.Fori(0, E0 // 2) as i:
                for s in range(2):
                    e = 2 * i + s
                    pe.wait_ge(w_loaded[s], 16 * i + 16)
                    pe.wait_ge(aw_loaded, 16 * i + 16)
                    pe.wait_ge(h_done, 2 * i)
                    for dst, off, aoff, ready in ((gp[s], 0, 0, g_ready), (up[s], INTER, AI, u_ready)):
                        for j in range(NJ + 1):
                            for k in range(KC):
                                if j < NJ:
                                    o = 2 * INTER * k + off + P * j
                                    lhs = w[s][:, o:o + P]
                                else:
                                    o = 2 * AI * k + aoff
                                    lhs = aw[:, o:o + AI]
                                last = pe.matmul(dst[:, j, :], lhs, xet[:, k, bass.ds(e, 1), :].rearrange("p o c -> p (o c)"),
                                                 start=(k == 0), stop=(k == KC - 1))
                        last.then_inc(ready, 1)
                for s in range(2):
                    pe.wait_ge(h_done, 2 * i + s + 1)
                    pe.wait_ge(ye_ready, 2 * i)
                    for j in range(NJ + 1):
                        rhs = w[s][:, UP + D * j:UP + D * j + D] if j < NJ else aw[:, KC * 2 * AI:]
                        last = pe.matmul(y[s][:, :], h[s][:, j, :], rhs, start=(j == 0), stop=(j == NJ))
                    last.then_inc(y_ready, 1)

        @block.scalar
        def _(act):
            with act.Fori(0, E0 // 2) as i:
                for s in range(2):
                    act.wait_ge(g_ready, 2 * i + s + 1)
                    act.wait_ge(h_done, 2 * i)
                    act.activation(sg[s][:, :, :], gp[s][:, :, :], ACT.Silu).then_inc(silu_done, 1)

        @block.vector
        def _(dve):
            n = 0
            for e0 in range(0, E0, 4):
                for k in range(KC):
                    dve.wait_ge(turned, n + 1)
                    dve.tensor_copy(xet[:, k, e0:e0 + 4, :], tp[n % 2][:, :, :]).then_inc(taken, 1)
                    n += 1
            flat = xe[:, :, :].rearrange("p e c -> p (e c)")
            dve.tensor_copy(we[:, :], flat[:, D:D + (ROW + 1) * (E0 - 1) + 1:ROW + 1]).then_inc(we_ready, 1)
            dve.wait_ge(we_ready, 1)
            with dve.Fori(0, E0 // 2) as i:
                for s in range(2):
                    dve.wait_ge(silu_done, 2 * i + s + 1)
                    dve.wait_ge(u_ready, 2 * i + s + 1)
                    dve.wait_ge(y_ready, 2 * i)
                    dve.tensor_tensor(h[s][:, :NJ, :], sg[s][:, :NJ, :], up[s][:, :NJ, :], ALU.mult)
                    dve.scalar_tensor_tensor(out=h[s][:, NJ, :], in0=sg[s][:, NJ, :], scalar=0.05, in1=up[s][:, NJ, :],
                                             op0=ALU.mult, op1=ALU.mult).then_inc(h_done, 1)
                for s in range(2):
                    dve.wait_ge(y_ready, 2 * i + s + 1)
                    dve.wait_ge(added, 32 * i)
                    dve.tensor_scalar(ye[s][:, :], y[s][:, :], we[:, bass.ds(2 * i + s, 1)], None, ALU.mult).then_inc(ye_ready, 1)


def gate1(nc, a, xt, gate_bias, cw):
    ctx, sb, ps, sem = phase(nc, "gate1")
    with ctx:
        gw = sb("gw", [P, KC, E1])
        lg = ps("lg", [P, NT, E1])
        sco = sb("sco", [P, NT, E1])
        sfc = sb("sfc", [P, NT, E1])
        hi = sb("hi", [P, NT * G1, 2])
        lo = sb("lo", [P, NT * G1, 2])
        t1 = sb("t1", [P, NT * G1])
        t2 = sb("t2", [P, NT * G1])
        gs = sb("gs", [P, NT, 8])
        top = sb("top", [P, NT, 8])
        at = sb("at", [P, NT, 8], U32)
        atf = sb("atf", [P, NT, 8])
        iota = sb("iota", [P, NT, E1])
        m4 = sb("m4", [P, NT, G1])
        m4b = sb("m4b", [P, NT, G1])
        m16 = [sb(f"m16{i}", [P, NT, E1]) for i in range(4)]
        tot = sb("tot", [P, NT])
        w_loaded, iota_ready, logits_ready, sig_ready, chain = sem("w_loaded"), sem("iota_ready"), sem("logits_ready"), sem("sig_ready"), sem("chain")
        block = ctx.enter_context(nc.Block())

        @block.sync
        def _(sp):
            sp.dma_start(gw[:, :, :], a["gw"]).then_inc(w_loaded, 16)

        @block.gpsimd
        def _(pool):
            pool.iota(iota[:, :, :], [[0, NT], [1, E1]], base=0, channel_multiplier=0,
                      allow_small_or_imprecise_dtypes=True).then_inc(iota_ready, 1)

        @block.tensor
        def _(pe):
            pe.wait_ge(w_loaded, 16)
            for t in range(NT):
                for k in range(KC):
                    last = pe.matmul(lg[:, t, :], xt[:, k, P * t:P * t + P], gw[:, k, :], start=(k == 0), stop=(k == KC - 1))
            last.then_inc(logits_ready, 1)

        @block.scalar
        def _(act):
            act.wait_ge(logits_ready, 1)
            act.activation(sco[:, :, :], lg[:, :, :], ACT.Sigmoid).then_inc(sig_ready, 1)

        @block.vector
        def _(dve):
            link = Chain(dve, chain)
            dve.memset(cw[:, :, E1:], 1.0)
            dve.memset(gs[:, :, :], -3e38)
            dve.wait_ge(sig_ready, 1)
            dve.wait_ge(iota_ready, 1)
            link(dve.tensor_tensor(sfc[:, :, :], sco[:, :, :], gate_bias.unsqueeze(1).to_broadcast([P, NT, E1]), ALU.add))
            four = sfc[:, :, :].rearrange("p t (g i) -> p (t g) i", i=E1 // G1)
            dve.tensor_tensor(hi[:, :, :], four[:, :, 0:2], four[:, :, 2:4], ALU.max)
            link(dve.tensor_tensor(lo[:, :, :], four[:, :, 0:2], four[:, :, 2:4], ALU.min))
            dve.tensor_tensor(t1[:, :], hi[:, :, 0], hi[:, :, 1], ALU.min)
            link(dve.tensor_tensor(t2[:, :], lo[:, :, 0], lo[:, :, 1], ALU.max))
            link(dve.tensor_tensor(t1[:, :], t1[:, :], t2[:, :], ALU.max))
            link(dve.tensor_tensor(t2[:, :], hi[:, :, 0], hi[:, :, 1], ALU.max))
            link(dve.tensor_tensor(gs[:, :, :G1], t1[:, :].rearrange("p (t g) -> p t g", g=G1),
                                   t2[:, :].rearrange("p (t g) -> p t g", g=G1), ALU.add))
            for t in range(NT):
                last = dve.max(top[:, t, :], gs[:, t, :])
            link(last)
            for t in range(NT):
                last = dve.max_index(at[:, t, :], top[:, t, :], gs[:, t, :])
            link(last)
            link(dve.tensor_copy(atf[:, :, :], at[:, :, :]))
            dve.tensor_tensor(m4[:, :, :], iota[:, :, :G1], over(atf[:, :, 0], G1), ALU.is_equal)
            link(dve.tensor_tensor(m4b[:, :, :], iota[:, :, :G1], over(atf[:, :, 1], G1), ALU.is_equal))
            link(dve.tensor_tensor(m4[:, :, :], m4[:, :, :], m4b[:, :, :], ALU.add))
            link(dve.tensor_tensor(four, four, over(m4[:, :, :].rearrange("p t g -> p (t g)"), E1 // G1), ALU.mult))
            link(dve.tensor_scalar(sfc[:, :, :], sfc[:, :, :], 0.0, None, ALU.add))
            for t in range(NT):
                last = dve.max(top[:, t, :], sfc[:, t, :])
            link(last)
            for t in range(NT):
                last = dve.max_index(at[:, t, :], top[:, t, :], sfc[:, t, :])
            link(last)
            link(dve.tensor_copy(atf[:, :, :], at[:, :, :]))
            for i in range(TOPK1):
                last = dve.tensor_tensor(m16[i][:, :, :], iota[:, :, :], over(atf[:, :, i], E1), ALU.is_equal)
            link(last)
            dve.tensor_tensor(m16[0][:, :, :], m16[0][:, :, :], m16[1][:, :, :], ALU.add)
            link(dve.tensor_tensor(m16[2][:, :, :], m16[2][:, :, :], m16[3][:, :, :], ALU.add))
            link(dve.tensor_tensor(m16[0][:, :, :], m16[0][:, :, :], m16[2][:, :, :], ALU.add))
            link(dve.tensor_tensor(sco[:, :, :], sco[:, :, :], m16[0][:, :, :], ALU.mult))
            link(dve.tensor_reduce(tot[:, :], sco[:, :, :], AX.X, ALU.add))
            link(dve.tensor_scalar(tot[:, :], tot[:, :], 1e-20, None, ALU.add))
            link(dve.reciprocal(tot[:, :], tot[:, :]))
            link(dve.tensor_tensor(cw[:, :, :E1], sco[:, :, :], over(tot[:, :], E1), ALU.mult))


def moe(nc, a, xt, cw, x_sb, out):
    ctx, sb, ps, sem = phase(nc, "moe")
    it_rows = tiles_of(EI)
    NI = len(it_rows)
    UP, DN = KC * EI, 2 * KC * EI
    NE = E1 + SH
    NU = 2 * NCH * NI
    NY = 2 * NT
    with ctx:
        w = [sb(f"w{i}", [P, DN + NI * D]) for i in range(2)]
        sg = sb("sg", [P, 2, CH])
        h = sb("h", [P, 2, NI, CH])
        gp = [ps(f"gp{i}", [P, CH]) for i in range(2)]
        up = [ps(f"up{i}", [P, CH]) for i in range(2)]
        y = [ps(f"y{i}", [P, D]) for i in range(4)]
        w_loaded = [sem(f"w_loaded{i}") for i in range(2)]
        gu_ready, silu_done, h_done, y_ready, summed, stored = (sem("gu_ready"), sem("silu_done"), sem("h_done"), sem("y_ready"),
                                                                sem("summed"), sem("stored"))
        block = ctx.enter_context(nc.Block())

        @block.sync
        def _(sp):
            with sp.Fori(0, NE // 2) as i:
                for s in range(2):
                    sp.wait_ge(y_ready, NY * i)
                    sp.dma_start(w[s][:, :], a["wm"][bass.ds(2 * i + s, 1)].rearrange("o p n -> (o p) n")).then_inc(w_loaded[s], 16)
            sp.wait_ge(summed, NY * (NE // 2))
            sp.dma_start(out.rearrange("o (t p) d -> p (o t) d", p=P), x_sb[:, :, :]).then_inc(stored, 16)
            sp.wait_ge(stored, 16)

        @block.tensor
        def _(pe):
            def hidden(i, s, c, it):
                n = NI * (NCH * s + c) + it
                r = it_rows[it]
                if n >= 2:
                    pe.wait_ge(h_done, NU * i + n - 1)
                else:
                    pe.wait_ge(h_done, NU * i)
                for dst, off in ((gp[n % 2], 0), (up[n % 2], UP)):
                    for k in range(KC):
                        o = off + EI * k + P * it
                        last = pe.matmul(dst[:r, :], w[s][:, o:o + r], xt[:, k, CH * c:CH * c + CH], start=(k == 0), stop=(k == KC - 1))
                last.then_inc(gu_ready, 1)

            def out_tile(i, s, t):
                n = NT * s + t
                c = NCH * s + t // TPC
                pe.wait_ge(h_done, NU * i + NI * (c + 1))
                if n >= 4:
                    pe.wait_ge(summed, NY * i + n - 3)
                else:
                    pe.wait_ge(summed, NY * i)
                q = P * (t % TPC)
                for it in range(NI):
                    r = it_rows[it]
                    last = pe.matmul(y[n % 4][:, :], h[:r, c % 2, it, q:q + P], w[s][:r, DN + D * it:DN + D * it + D],
                                     start=(it == 0), stop=(it == NI - 1))
                last.then_inc(y_ready, 1)

            with pe.Fori(0, NE // 2) as i:
                for c in range(2 * NCH + 1):
                    if c % NCH == 0 and c < 2 * NCH:
                        pe.wait_ge(w_loaded[c // NCH], 16 * i + 16)
                    done = 0
                    for it in range(NI):
                        if c < 2 * NCH:
                            hidden(i, c // NCH, c % NCH, it)
                        if c >= 1:
                            for q in range(TPC * it // NI, TPC * (it + 1) // NI):
                                out_tile(i, (c - 1) // NCH, TPC * ((c - 1) % NCH) + q)

        @block.scalar
        def _(act):
            with act.Fori(0, NE // 2) as i:
                for n in range(NU):
                    r = it_rows[n % NI]
                    act.wait_ge(gu_ready, NU * i + n + 1)
                    act.wait_ge(h_done, NU * i + max(n - 1, 0))
                    act.activation(sg[:r, n % 2, :], gp[n % 2][:r, :], ACT.Silu).then_inc(silu_done, 1)

        @block.vector
        def _(dve):
            def product(i, n):
                it, c = n % NI, n // NI
                r = it_rows[it]
                dve.wait_ge(silu_done, NU * i + n + 1)
                if it == 0:
                    dve.wait_ge(y_ready, NY * i + TPC * max(c - 1, 0))
                dve.tensor_tensor(h[:r, c % 2, it, :], sg[:r, n % 2, :], up[n % 2][:r, :], ALU.mult).then_inc(h_done, 1)

            def add(i, n):
                s, t = n // NT, n % NT
                dve.wait_ge(y_ready, NY * i + n + 1)
                dve.scalar_tensor_tensor(out=x_sb[:, t, :], in0=y[n % 4][:, :], scalar=cw[:, t, bass.ds(2 * i + s, 1)],
                                         in1=x_sb[:, t, :], op0=ALU.mult, op1=ALU.add).then_inc(summed, 1)

            with dve.Fori(0, NE // 2) as i:
                dve.wait_ge(summed, NY * i)
                for c in range(2 * NCH + 1):
                    for it in range(NI):
                        if c < 2 * NCH:
                            product(i, NI * c + it)
                        if c >= 1:
                            for q in range(TPC * it // NI, TPC * (it + 1) // NI):
                                if c - 1 == NCH and it == 0 and q == 0:
                                    dve.wait_ge(summed, NY * i + NT)
                                add(i, TPC * (c - 1) + q)


def program(nc, a, out, stop=99, dump=None):
    a = dict(a)
    a["table"] = nc.dram_tensor("token_rows", (T, ROW), F32, kind="Internal").ap()
    a["acc"] = nc.dram_tensor("token_sums", (T, D), F32, kind="Internal").ap()
    rows_t = [P] * NT
    rows_s = tiles_of(S)

    FREE_SEMS.clear()
    FREE_SEMS.extend(sorted(nc.free_semaphores))
    top = ExitStack()
    with top:
        def sb(n, shape, dt=F32):
            return top.enter_context(nc.sbuf_tensor(n, shape, dt))

        def finish(t):
            c, _, _, sem = phase(nc, "finish")
            with c:
                stored = sem("stored")
                block = c.enter_context(nc.Block())

                @block.sync
                def _(sp):
                    sp.dma_start(out.rearrange("o (t p) d -> p (o t) d", p=P), t[:, :, :]).then_inc(stored, 16)
                    sp.wait_ge(stored, 16)

        cols, rows = sb("cols", [P, NCOLS]), sb("rows", [P, NROWS])
        ident, ones = sb("ident", [P, P]), sb("ones", [P, P])
        x = sb("x", [P, NT, D])
        a["ident"] = ident
        load_constants(nc, a, cols, rows, ident, ones, x)

        def col(n):
            o, k = COLS[n]
            return cols[:, o:o + k]

        def row(n):
            o, k = ROWS[n]
            return rows[:, o:o + k]

        def scope():
            c = ExitStack()
            return c, lambda n, shape, dt=F32: c.enter_context(nc.sbuf_tensor(n, shape, dt))

        c, sb1 = scope()
        with c:
            ot = sb1("ot_0", [P, NG, T])
            c2, sb2 = scope()
            with c2:
                ct, xt = sb2("ct_0", [P, 1, S]), sb2("xt_0", [P, KC, T])
                c3, sb3 = scope()
                with c3:
                    ctx_block(nc, a, "ctx_t", ct)
                    xn = sb3("xn_0", [P, NT, D])
                    layernorm(nc, "ln_0", x, xn, rows_t, D, outs=[(xt, None, None)], ident=ident)
                attention(nc, a, "xa0", a["wq0"], a["wk0"], a["wv0"], xt, KC, ct, 1, S, (D // HEADS) ** -0.5, False, ot, ones,
                          bq=col("bq0"), bk=col("bk0"), bv=row("bv0").rearrange("p (g n) -> p g n", n=P))
            project_out(nc, "out0", ot, a["wo0"], row("bo0"), x, x)
        if stop == 0:
            return finish(x)

        c, sb1 = scope()
        with c:
            slots = sb1("slots", [P, E0], U32)
            c2, sb2 = scope()
            with c2:
                z, wc, picks = sb2("z", [P, NT, D]), sb2("wc", [P, NT, E0]), sb2("picks", [E0, T])
                zt, zst = sb2("zt", [P, KC, T]), sb2("zst", [NSTAT, T])
                layernorm(nc, "ln_z", x, z, rows_t, D, outs=[(zt, None, None)], ident=ident)
                router_stats(nc, z, zst, ident)
                router(nc, a, zt, zst, col("r1b"), wc, picks, ident)
                choose(nc, a, picks, z, wc, x, slots, ident)
            experts(nc, a, slots, x, ident)
        if stop == 1:
            return finish(x)

        c, sb1 = scope()
        with c:
            r = x
            layernorm(nc, "ln_xx", x, r, rows_t, D)
            layernorm(nc, "ln1", r, r, rows_t, D, affine=(row("ln1_g"), row("ln1_b")))
            for n, p in enumerate(("a1", "a2")):
                if n == 1:
                    layernorm(nc, "ln2", r, r, rows_t, D, affine=(row("ln2_g"), row("ln2_b")))
                c2, sb2 = scope()
                with c2:
                    ot = sb2(f"{p}_ot", [P, NG, T])
                    c3, sb3 = scope()
                    with c3:
                        xq = sb3(f"{p}_xq", [P, KC, T])
                        if n == 0:
                            xk, nkk, nkeys = sb3(f"{p}_xk", [P, KC, T]), KC, T
                        else:
                            xk, nkk, nkeys = sb3(f"{p}_xk", [P, 1, S]), 1, S
                        c4, sb4 = scope()
                        with c4:
                            xn = sb4(f"{p}_xn", [P, NT, D])
                            outs = [(xq, col(p + "_lnx_g"), col(p + "_lnx_b"))]
                            if n == 0:
                                outs.append((xk, col(p + "_lny_g"), col(p + "_lny_b")))
                            layernorm(nc, p + "_lnx", r, xn, rows_t, D, outs=outs, ident=ident)
                        if n == 1:
                            c4, sb4 = scope()
                            with c4:
                                cr = sb4("ctx_rows", [P, len(rows_s), C])
                                load_ctx_rows(nc, a, cr)
                                layernorm(nc, p + "_lny", cr, cr, rows_s, C,
                                          outs=[(xk, col(p + "_lny_g"), col(p + "_lny_b"))], ident=ident)
                        attention(nc, a, p, a[p + "_wq"], a[p + "_wk"], a[p + "_wv"], xq, KC, xk, nkk, nkeys, SLOT ** -0.5, n == 0,
                                  ot, ones, ering=2 if n == 0 else 4)
                    xo = sb2(f"{p}_xo", [P, NT, D])
                    project_out(nc, p + "_out", ot, a[p + "_wo"], row(p + "_li1_b"), r, xo)
                    xt = sb2(f"{p}_xt", [P, KC, T])
                    c3, sb3 = scope()
                    with c3:
                        xn = sb3(f"{p}_xn3", [P, NT, D])
                        layernorm(nc, p + "_ln3", xo, xn, rows_t, D, outs=[(xt, col(p + "_ln3_g"), col(p + "_ln3_b"))], ident=ident)
                    adds = [r]
                    if n == 1:
                        adds.append(sb2("x2", [P, NT, D]))
                        load_tokens(nc, a["acc"], adds[1])
                    gelu_ffn(nc, p + "_ffn", xt, a[p + "_li2"], a[p + "_li3"], col(p + "_li2_b"), row(p + "_li3_b"), xo, adds, r)
                if stop == 2 + n:
                    return finish(r if n == 0 else x)

        xt, cw = sb("m_xt", [P, KC, T]), sb("cw", [P, NT, E1 + SH])
        c, sb1 = scope()
        with c:
            xn = sb1("m_xn", [P, NT, D])
            layernorm(nc, "m_ln", x, xn, rows_t, D, outs=[(xt, None, None)], ident=ident)
        gate1(nc, a, xt, row("gate_bias"), cw)
        moe(nc, a, xt, cw, x, out)


def ctx_block(nc, a, name, ct):
    ctx, sb, ps, sem = phase(nc, name)
    with ctx:
        loaded = sem("loaded")
        block = ctx.enter_context(nc.Block())

        @block.sync
        def _(sp):
            sp.dma_start(ct[:, 0, :], a["ctx_t"]).then_inc(loaded, 16)
            sp.wait_ge(loaded, 16)


def load_tokens(nc, source, target):
    ctx, sb, ps, sem = phase(nc, "tokens_in")
    with ctx:
        loaded = sem("loaded")
        block = ctx.enter_context(nc.Block())

        @block.sync
        def _(sp):
            sp.dma_start(target[:, :, :], source.rearrange("(t p) d -> p t d", p=P)).then_inc(loaded, 16)
            sp.wait_ge(loaded, 16)


def load_ctx_rows(nc, a, cr):
    ctx, sb, ps, sem = phase(nc, "ctx_rows_in")
    full = S // P
    with ctx:
        loaded = sem("loaded")
        block = ctx.enter_context(nc.Block())

        @block.sync
        def _(sp):
            sp.dma_start(cr[:, :full, :], a["ctx"][:full * P, :].rearrange("(t p) c -> p t c", p=P)).then_inc(loaded, 16)
            sp.dma_start(cr[:S - full * P, full, :], a["ctx"][full * P:, :]).then_inc(loaded, 16)
            sp.wait_ge(loaded, 32)


def laid_out(i):
    i = {k: np.asarray(v) for k, v in i.items()}

    def blocks(w):
        k, n = w.shape
        return w.reshape(k // P, P, n).transpose(1, 0, 2)

    def slots(w, heads_width):
        k = w.shape[0]
        o = np.zeros((k, HEADS, SLOT), np.float32)
        o[:, :, :heads_width] = w.reshape(k, HEADS, heads_width)
        return o.reshape(k, HEADS * SLOT)

    def grouped(w):
        k = w.shape[0]
        return w.reshape(k // P, P, NG, P).transpose(2, 1, 0, 3)

    dk = D // HEADS
    o = {"x": i["x"], "ctx": i["ctx_512"][0], "ctx_t": i["ctx_512"][0].T}
    o["wq0"] = grouped(slots(i["L0_xattn_Wq"], dk))
    o["wk0"] = grouped(slots(i["L0_xattn_Wk"], dk))
    o["wv0"] = grouped(slots(i["L0_xattn_Wv"], dk))
    o["wo0"] = blocks(slots(i["L0_xattn_Wo"].T, dk).T)
    o["r1"] = blocks(i["L0_ffn_r1_w"][:, :D].T)
    o["r1s"] = i["L0_ffn_r1_w"][:, D:].T
    o["r2"] = i["L0_ffn_r2_w"].T
    up = i["L0_ffn_w_up"].transpose(0, 2, 1).reshape(E0, KC, P, 2 * INTER).transpose(0, 2, 1, 3).reshape(E0, P, -1)
    dn = i["L0_ffn_w_down"].transpose(0, 2, 1).reshape(E0, INTER // P, P, D).transpose(0, 2, 1, 3).reshape(E0, P, -1)
    o["we"] = np.concatenate([up, dn], 2)
    up = i["L0_ffn_a_up"].transpose(0, 2, 1).reshape(AG, KC, P, 2 * AI).transpose(0, 2, 1, 3).reshape(AG, P, -1)
    o["aw"] = np.concatenate([up, i["L0_ffn_a_down"].transpose(0, 2, 1)], 2)
    for p in ("a1", "a2"):
        for n in "qkv":
            w = i[f"L1_xattn_{p}_w{n}"]
            o[f"{p}_w{n}"] = grouped(w.transpose(1, 0, 2).reshape(w.shape[1], HEADS * SLOT))
        o[p + "_wo"] = blocks(i[f"L1_xattn_{p}_li1_w"])
        o[p + "_li2"] = blocks(i[f"L1_xattn_{p}_li2_w"])
        o[p + "_li3"] = blocks(i[f"L1_xattn_{p}_li3_w"])
    o["gw"] = blocks(i["L1_ffn_gate_w"].T)
    gate = np.concatenate([i["L1_ffn_gate_proj"], i["L1_ffn_shared_gate_w"].reshape(SH, EI, D)])
    upw = np.concatenate([i["L1_ffn_up_proj"], i["L1_ffn_shared_up_w"].reshape(SH, EI, D)])
    down = np.concatenate([i["L1_ffn_down_proj"], i["L1_ffn_shared_down_w"].reshape(D, SH, EI).transpose(1, 0, 2)])
    n = E1 + SH
    gu = [w.transpose(0, 2, 1).reshape(n, KC, P, EI).transpose(0, 2, 1, 3).reshape(n, P, -1) for w in (gate, upw)]
    ni = (EI + P - 1) // P
    dn = np.zeros((n, ni * P, D), np.float32)
    dn[:, :EI] = down.transpose(0, 2, 1)
    o["wm"] = np.concatenate([*gu, dn.reshape(n, ni, P, D).transpose(0, 2, 1, 3).reshape(n, P, -1)], 2)
    vec = {"bq0": slots(i["L0_xattn_bq"][None], dk)[0], "bk0": slots(i["L0_xattn_bk"][None], dk)[0], "r1b": i["L0_ffn_r1_b"],
           "bo0": i["L0_xattn_bo"], "bv0": slots(i["L0_xattn_bv"][None], dk)[0], "gate_bias": i["L1_ffn_gate_bias"]}
    for n in ("ln1_g", "ln1_b", "ln2_g", "ln2_b"):
        vec[n] = i["L1_xattn_" + n]
    for n in list(COLS) + list(ROWS):
        if n not in vec:
            vec[n] = i["L1_xattn_" + n]
    o["cols"] = np.concatenate([vec[n].reshape(-1, P).T for n in COLS], 1)
    o["rows"] = np.concatenate([vec[n] for n in ROWS])[None]
    return {k: np.ascontiguousarray(v) for k, v in o.items()}


def kernel(**inputs):
    import concourse.bacc as bacc
    from concourse.bass_utils import run_bass_kernel_spmd

    arrays = {f"in_{k}": v for k, v in laid_out(inputs).items()}
    nc = bacc.Bacc("TRN2", target_bir_lowering=False, num_devices=1)
    a = {k[3:]: nc.dram_tensor(k, v.shape, mybir.dt.from_np(v.dtype), kind="ExternalInput").ap() for k, v in arrays.items()}
    out = nc.dram_tensor("out_x", (1, T, D), F32, kind="ExternalOutput").ap()
    program(nc, a, out)
    r = run_bass_kernel_spmd(nc, [arrays], core_ids=[0])
    return r.results[0]["out_x"]
```

```python
from collections import deque
from contextlib import ExitStack

import numpy as np
import concourse.bass as bass
from concourse import mybir

F32 = mybir.dt.float32
F16 = mybir.dt.float16
U32 = mybir.dt.uint32
ALU = mybir.AluOpType
ACT = mybir.ActivationFunctionType
AX = mybir.AxisListType

P = 128
T = 2048
D = 256
S = 1601
C = 128
NT = T // P
KC = D // P
CH = 512
NCH = T // CH
TPC = CH // P
HEADS = 16
HG = 4
NG = HEADS // HG
SLOT = 32
STACK = 3 * SLOT
EPS = 1e-5

E0, CAP, INTER, AG, AI = 32, 80, 512, 16, 128
NSTAT = 6
ROW = D + E0
E1, EI, SH, TOPK1, G1, TG1 = 16, 352, 2, 4, 4, 2
FF = 1024

COLS, ROWS = {}, {}
_at = 0
for _n, _k in (("bq0", NG), ("bk0", NG), ("r1b", 1),
               ("a1_lnx_g", 2), ("a1_lnx_b", 2), ("a1_lny_g", 2), ("a1_lny_b", 2), ("a1_ln3_g", 2), ("a1_ln3_b", 2),
               ("a1_li2_b", 8),
               ("a2_lnx_g", 2), ("a2_lnx_b", 2), ("a2_lny_g", 1), ("a2_lny_b", 1), ("a2_ln3_g", 2), ("a2_ln3_b", 2),
               ("a2_li2_b", 8)):
    COLS[_n] = (_at, _k)
    _at += _k
NCOLS = _at
_at = 0
for _n, _k in (("bo0", D), ("ln1_g", D), ("ln1_b", D), ("ln2_g", D), ("ln2_b", D), ("a1_li1_b", D), ("a1_li3_b", D),
               ("a2_li1_b", D), ("a2_li3_b", D), ("gate_bias", E1), ("bv0", NG * P)):
    ROWS[_n] = (_at, _k)
    _at += _k
NROWS = _at


def tiles_of(n):
    return [min(P, n - P * t) for t in range((n + P - 1) // P)]


def chunks_of(n):
    return [(CH * c, min(CH, n - CH * c)) for c in range((n + CH - 1) // CH)]


FREE_SEMS = deque()


def phase(nc, name):
    ctx = ExitStack()
    sems = []

    def clear():
        nc.clear_and_free_semaphores(sems)
        FREE_SEMS.extend(s.num for s in sems)

    ctx.callback(clear)

    def sb(n, shape, dt=F32):
        return ctx.enter_context(nc.sbuf_tensor(f"{name}_{n}", shape, dt))

    def ps(n, shape, dt=F32):
        return ctx.enter_context(nc.psum_tensor(f"{name}_{n}", shape, dt))

    def sem(n):
        sems.append(nc.alloc_semaphore(f"{name}_{n}", FREE_SEMS.popleft()))
        return sems[-1]

    return ctx, sb, ps, sem


def load_constants(nc, a, cols, rows, ident, ones, x_sb):
    ctx, sb, ps, sem = phase(nc, "init")
    with ctx:
        loaded, zeroed, made = sem("loaded"), sem("zeroed"), sem("made")
        block = ctx.enter_context(nc.Block())

        @block.sync
        def _(sp):
            sp.dma_start(cols[:, :], a["cols"]).then_inc(loaded, 16)
            sp.dma_start(rows[:, :], a["rows"].partition_broadcast(P).rearrange("p o n -> p (o n)")).then_inc(loaded, 16)
            sp.dma_start(x_sb[:, :, :], a["x"].rearrange("o (t p) d -> p (o t) d", p=P)).then_inc(loaded, 16)
            sp.wait_ge(loaded, 48)

        @block.gpsimd
        def _(pool):
            pool.memset(ident[:, :], 0.0).then_inc(zeroed, 1)
            pool.memset(ones[:, :], 1.0)
            pool.wait_ge(zeroed, 1)
            pool.affine_select(out=ident[:, :], in_=ident[:, :], compare_op=ALU.not_equal, fill=1.0, base=0,
                               pattern=[[-1, P]], channel_multiplier=1).then_inc(made, 1)
            pool.wait_ge(made, 1)


def layernorm(nc, name, src, dst, rows, width, affine=None, outs=(), ident=None):
    ctx, sb, ps, sem = phase(nc, name)
    n = len(rows)
    nk = width // P
    with ctx:
        stats = sb("stats", [P, n, 6])
        mv = sb("mv", [P, n, 2])
        std = sb("std", [P, n])
        rstd = sb("rstd", [P, n])
        eps = sb("eps", [P, 1])
        tp = ps("tp", [P, 4, CH]) if outs else None
        eps_set, stats_done, var_ready = sem("eps_set"), sem("stats_done"), sem("var_ready")
        std_ready, rstd_ready, scaled = sem("std_ready"), sem("rstd_ready"), sem("scaled")
        ready, turned, taken = sem("ready"), sem("turned"), sem("taken")
        block = ctx.enter_context(nc.Block())
        full = [t for t in range(n) if rows[t] == P]
        spans = [(0, len(full), P)] + [(t, t + 1, rows[t]) for t in range(n) if rows[t] < P]
        groups = [(k, t0, min(t0 + TPC, n)) for t0 in range(0, n, TPC) for k in range(nk)]

        @block.vector
        def _(dve):
            dve.memset(eps[:, :], EPS).then_inc(eps_set, 1)
            for t in range(n):
                r = rows[t]
                dve.bn_stats(stats[:r, t, :], src[:r, t, :]).then_inc(stats_done, 1)
            for t in range(n):
                r = rows[t]
                dve.wait_ge(stats_done, t + 1)
                dve.bn_aggr(mv[:r, t, :], stats[:r, t, :]).then_inc(var_ready, 1)
            if affine is not None:
                dve.wait_ge(var_ready, n)
                for t in range(n):
                    dve.scalar_tensor_tensor(out=dst[:, t, :], in0=src[:, t, :], scalar=mv[:, t, 0:1], in1=affine[0],
                                             op0=ALU.subtract, op1=ALU.mult).then_inc(scaled, 1)
            for i, (t0, t1, r) in enumerate(spans):
                dve.wait_ge(std_ready, i + 1)
                dve.reciprocal(rstd[:r, t0:t1], std[:r, t0:t1]).then_inc(rstd_ready, 1)
            dve.wait_ge(rstd_ready, len(spans))
            for t in range(n):
                r = rows[t]
                if affine is None:
                    dve.tensor_scalar(dst[:r, t, :], src[:r, t, :], mv[:r, t, 0:1], rstd[:r, t:t + 1],
                                      ALU.subtract, ALU.mult).then_inc(ready, 1)
                else:
                    dve.wait_ge(scaled, t + 1)
                    dve.scalar_tensor_tensor(out=dst[:, t, :], in0=dst[:, t, :], scalar=rstd[:, t:t + 1], in1=affine[1],
                                             op0=ALU.mult, op1=ALU.add).then_inc(ready, 1)

        @block.scalar
        def _(act):
            act.wait_ge(eps_set, 1)
            act.wait_ge(var_ready, n)
            for t0, t1, r in spans:
                act.activation(std[:r, t0:t1], mv[:r, t0:t1, 1], ACT.Sqrt, bias=eps[:r, 0:1]).then_inc(std_ready, 1)
            for i, (k, t0, t1) in enumerate(groups if outs else ()):
                w = sum(rows[t0:t1])
                act.wait_ge(turned, i + 1)
                for target, g, b in outs:
                    o = target[:, k, P * t0:P * t0 + w]
                    if g is None:
                        last = act.activation(o, tp[:, i % 4, :w], ACT.Copy)
                    else:
                        last = act.activation(o, tp[:, i % 4, :w], ACT.Identity, bias=b[:, k:k + 1], scale=g[:, k:k + 1])
                last.then_inc(taken, 1)

        if outs:
            @block.tensor
            def _(pe):
                for i, (k, t0, t1) in enumerate(groups):
                    pe.wait_ge(ready, t1)
                    if i >= 4:
                        pe.wait_ge(taken, i - 3)
                    for t in range(t0, t1):
                        r = rows[t]
                        o = P * (t - t0)
                        last = pe.transpose(tp[:, i % 4, o:o + r], dst[:r, t, P * k:P * k + P], ident[:r, :r])
                    last.then_inc(turned, 1)


def attention(nc, a, name, wq, wk, wv, xq, nkq, xk, nkk, nkeys, scale, causal, ot, ones, bq=None, bk=None, bv=None, ering=4, ones_at=None):
    ctx, sb, ps, sem = phase(nc, name)
    kt_rows = tiles_of(nkeys)
    nkt = len(kt_rows)
    kch = chunks_of(nkeys)
    nmx = 4
    mxw = (nkeys + nmx - 1) // nmx
    mxs = [min(mxw * i, nkeys - mxw) for i in range(nmx)]
    nvb = (nkt + 3) // 4
    NC = NG * NCH
    NST = 3
    NQ = 3
    NWB = 3 if ones_at is None else 4
    NSC = 3
    PASSED_WORK, TILE_WORK = 5, 8
    LEAD = 2
    own_sum = ones_at is None
    NCOPY = 2 if own_sum else 1
    den_at = 0 if own_sum else ones_at
    MOVES = 16 * 3 * HG

    def maxima(n, spans=range(nmx)):
        return [("max", n, t, j, i) for i in spans for t in range(TPC) for j in range(HG)]

    def diagonal_of(n, kt):
        i = kt - TPC * (n % NCH)
        return i if causal and 0 <= i < TPC else None

    def passed(n, kt):
        return causal and kt < TPC * (n % NCH)

    summed = [0]
    for m in range(nkt * NC):
        summed.append(summed[-1] + (not passed(m // nkt, m % nkt)))

    shared = [[kt for kt in range(1, nkt - 2) if kt % 4 and own_sum and not causal]
              for n in range(NC)]
    nshared = [sum(len(x) for x in shared[:n]) for n in range(NC + 1)]

    before = [("k", 0, 0), ("q", 0), ("k", 0, 1)]
    for i in range(nmx):
        before += maxima(0, [i]) + ([("k", 0, i + 2)] if i + 2 < len(kch) else [])
        if i == 1:
            before += [("v", 0, b) for b in range(nvb)] + [("q", 1)]
    before.append(("turn", 0))
    during = []
    for n in range(NC):
        g, qc = n // NCH, n % NCH
        work = []
        if g + 1 < NG:
            work += {0: [("k", g + 1, c) for c in range(2)], 1: [("k", g + 1, c) for c in range(2, len(kch))],
                     2: [("v", g + 1, b) for b in range(nvb)]}.get(qc, [])
        if n + 1 < NC:
            work += maxima(n + 1) + [("turn", n + 1)]
        if n + 2 < NC:
            work.insert(16, ("q", n + 2))
        if 0 < n < NC - 1:
            work[26:26], work[32:32] = [("divisors", n - 1)], [("divide", n - 1)]
        during.append(work)
    after = [(u, n) for n in (NC - 2, NC - 1) for u in ("divisors", "divide")]
    order = before + [u for work in during for u in work] + after
    number = {u: i for i, u in enumerate(order)}
    staged = {u: i for i, u in enumerate(u for u in order if u[0] in "kq")}

    with ctx:
        wqs = sb("wqs", [P, NG, nkq, P])
        wks = sb("wks", [P, NG, nkk, P])
        wvs = sb("wvs", [P, NG, nkk, P])
        stage = sb("stage", [P, NST, 2, CH], F16)
        qs = sb("qs", [P, HG, NQ, CH], F16)
        ks = sb("ks", [P, 2, HG, nkeys + nkeys % 2], F16)
        v = sb("v", [P, 2, nkt, P])
        e = sb("e", [P, ering, HG, CH])
        em = sb("em", [P, 2, HG, P]) if causal else None
        later = sb("later", [P, P]) if causal else None
        part_sum = sb("part_sum", [P, HG, CH]) if own_sum and not causal else None
        part_max = sb("part_max", [P, HG, TPC, nmx])
        row_max = sb("row_max", [P, HG, TPC])
        neg_max = sb("neg_max", [HG * TPC, P], F16)
        span_sum = sb("span_sum", [P, 2, TPC, HG, NCH - 1]) if causal else None
        total = sb("total", [P, TPC, HG]) if causal else None
        inverse = sb("inverse", [P, TPC, HG])
        spread = sb("spread", [P, TPC, HG, SLOT])
        oc = sb("oc", [P, CH])
        dc = sb("dc", [P, CH]) if own_sum else oc
        wb = [ps(f"wb{i}", [P, CH]) for i in range(NWB)]
        sc = [ps(f"sc{i}", [P, CH]) for i in range(NSC)]
        po = ps("po", [P, CH])
        pd = ps("pd", [P, CH]) if own_sum else None

        w_loaded = {u: sem(f"w{u}_loaded") for u in "kqv"}
        ones_set, mask_filled = sem("ones_set"), sem("mask_filled")
        unit_ready, unit_taken, high_ready = sem("unit_ready"), sem("unit_taken"), sem("high_ready")
        split_ready = sem("split_ready")
        stacked = [sem(f"stacked{i}") for i in range(NST)]
        rowmax_ready, negmax_ready, negmax_loaded = sem("rowmax_ready"), sem("negmax_ready"), sem("negmax_loaded")
        sc_ready, exp_done, masked, pv_done = sem("sc_ready"), sem("exp_done"), sem("masked"), sem("pv_done")
        total_step = sem("total_step")
        o_taken, inverse_spread, part_added, part_cleared = sem("o_taken"), sem("inverse_spread"), sem("part_added"), sem("part_cleared")
        block = ctx.enter_context(nc.Block())

        def wait_stacked(eng, unit):
            i = staged[unit]
            eng.wait_ge(stacked[i % NST], MOVES * (i // NST + 1))

        @block.sync
        def _(sp):
            sp.dma_start(wks[:, :, :, :], wk.rearrange("g p k n -> p g k n")).then_inc(w_loaded["k"], 16)
            sp.dma_start(wqs[:, :, :, :], wq.rearrange("g p k n -> p g k n")).then_inc(w_loaded["q"], 16)
            sp.dma_start(wvs[:, :, :, :], wv.rearrange("g p k n -> p g k n")).then_inc(w_loaded["v"], 16)
            for u in order:
                if u[0] in "kq":
                    i = staged[u]
                    sp.wait_ge(split_ready, i + 1)
                    if u[0] == "k":
                        g, (o, w) = u[1], kch[u[2]]
                        if g >= 2:
                            sp.wait_ge(sc_ready, HG * nkt * NCH * (g - 1))
                        dst = [ks[SLOT * s:SLOT * s + SLOT, g % 2, j, o:o + w] for s in range(3) for j in range(HG)]
                        parts = (0, 1, 0)
                    else:
                        n, w = u[1], CH
                        if n >= NQ:
                            sp.wait_ge(sc_ready, HG * nkt * (n - NQ + 1))
                        dst = [qs[SLOT * s:SLOT * s + SLOT, j, n % NQ, :] for s in range(3) for j in range(HG)]
                        parts = (0, 0, 1)
                    for m, d in enumerate(dst):
                        h = SLOT * (m % HG)
                        sp.dma_start(d, stage[h:h + SLOT, i % NST, parts[m // HG], :w]).then_inc(stacked[i % NST], 16)
                if u[0] == "turn":
                    n = u[1]
                    sp.wait_ge(negmax_ready, n + 1)
                    for j in range(HG):
                        sp.dma_start(qs[STACK:STACK + 1, j, n % NQ, :].rearrange("o (t q) -> o t q", t=TPC),
                                     neg_max[TPC * j:TPC * j + TPC, :]).then_inc(negmax_loaded, 16)

        @block.gpsimd
        def _(pool):
            pool.memset(ks[STACK:STACK + 1, :, :, :], 1.0).then_inc(ones_set, 1)
            pool.wait_ge(ones_set, 1)
            if causal:
                pool.memset(later[:, :], 1.0).then_inc(mask_filled, 1)
                pool.wait_ge(mask_filled, 1)
                pool.affine_select(out=later[:, :], in_=later[:, :], compare_op=ALU.is_gt, fill=0.0, base=0,
                                   pattern=[[-1, P]], channel_multiplier=1).then_inc(mask_filled, 1)
                pool.wait_ge(mask_filled, 2)
            for n in range(NC if causal or own_sum else 0):
                if n:
                    pool.wait_ge(pv_done, summed[nkt * n])
                if not causal:
                    pool.memset(part_sum[:, :, :], 0.0).then_inc(part_cleared, 1)
                    pool.wait_ge(part_cleared, n + 1)
                for kt in range(nkt):
                    i = diagonal_of(n, kt)
                    if i is not None:
                        pool.wait_ge(exp_done, HG * (nkt * n + kt + 1))
                        if TPC * n + i >= 2:
                            before_n, before_kt = (n, kt - 2) if i >= 2 else (n - 1, TPC * ((n - 1) % NCH) + i + 2)
                            pool.wait_ge(pv_done, summed[nkt * before_n + before_kt + 1])
                        pool.tensor_tensor(em[:, kt % 2, :, :], e[:, (nkt * n + kt) % ering, :, P * i:P * i + P],
                                           later[:, :].unsqueeze(1).to_broadcast([P, HG, P]), ALU.mult).then_inc(masked, 1)
                    if kt in shared[n]:
                        m = nshared[n] + shared[n].index(kt)
                        pool.wait_ge(exp_done, HG * (nkt * n + kt + 1))
                        if m:
                            pool.wait_ge(part_added, m)
                        pool.tensor_tensor(part_sum[:, :, :], part_sum[:, :, :], e[:, (nkt * n + kt) % ering, :, :],
                                           ALU.add).then_inc(part_added, 1)

        @block.scalar
        def _(act):
            def copy_sums(n):
                act.wait_ge(pv_done, summed[nkt * (n + 1)])
                if n:
                    act.wait_ge(unit_taken, number[("divide", n - 1)] + 1)
                act.activation(oc[:, :], po[:, :], ACT.Copy).then_inc(o_taken, 1)
                if own_sum:
                    act.activation(dc[:, :], pd[:, :], ACT.Copy).then_inc(o_taken, 1)

            for m in range(nkt * NC):
                r = kt_rows[m % nkt]
                for j in range(HG):
                    act.wait_ge(sc_ready, HG * m + j + 1)
                    if m >= ering:
                        act.wait_ge(pv_done, summed[m - ering + 1])
                        act.wait_ge(exp_done, HG * (m - ering + 1))
                        n, kt = (m - ering) // nkt, (m - ering) % nkt
                        if kt in shared[n]:
                            act.wait_ge(part_added, nshared[n] + shared[n].index(kt) + 1)
                    n, kt = m // nkt, m % nkt
                    if passed(n, kt):
                        if kt == 0 and n >= 2:
                            act.wait_ge(unit_taken, number[("divisors", n - 2)] + 1)
                        c, t = kt // TPC, kt % TPC
                        act.activation(e[:, m % ering, j, :], sc[(HG * m + j) % NSC][:, :], ACT.Exp, scale=scale,
                                       accum_out=span_sum[:, n % 2, t, j, c:c + 1]).then_inc(exp_done, 1)
                        continue
                    act.activation(e[:r, m % ering, j, :], sc[(HG * m + j) % NSC][:r, :], ACT.Exp,
                                   scale=scale).then_inc(exp_done, 1)
                if m and m % nkt == 0:
                    copy_sums(m // nkt - 1)
            copy_sums(NC - 1)

        @block.vector
        def _(dve):
            def take(u):
                i = number[u]
                src = wb[i % NWB]
                if u[0] in "kq":
                    m = staged[u]
                    g = u[1] if u[0] == "k" else u[1] // NCH
                    w = kch[u[2]][1] if u[0] == "k" else CH
                    bias = bk if u[0] == "k" else bq
                    bias = bias[:, g:g + 1] if bias is not None else 0.0
                    high, low = (stage[:, m % NST, k, :w] for k in range(2))
                    dve.wait_ge(unit_ready, i + 1)
                    if m >= NST:
                        dve.wait_ge(stacked[m % NST], MOVES * (m // NST))
                    dve.tensor_scalar(high, src[:, :w], bias, None, ALU.add).then_inc(high_ready, 1)
                    dve.wait_ge(high_ready, m + 1)
                    last = dve.scalar_tensor_tensor(out=low, in0=src[:, :w], scalar=bias, in1=high, op0=ALU.add, op1=ALU.subtract)
                    last.then_inc(split_ready, 1)
                    dve.wait_ge(split_ready, m + 1)
                    dve.sem_inc(unit_taken, 1)
                elif u[0] == "v":
                    g, b = u[1:]
                    dve.wait_ge(unit_ready, i + 1)
                    if g >= 2:
                        dve.wait_ge(pv_done, summed[nkt * NCH * (g - 1)])
                    ts = range(4 * b, min(4 * b + 4, nkt))
                    whole = [t for t in ts if kt_rows[t] == P]
                    src = src[:, :].rearrange("p (t n) -> p t n", n=P)
                    if whole:
                        last = dve.tensor_copy(v[:, g % 2, whole[0]:whole[-1] + 1, :], src[:, :len(whole), :])
                    for t in ts:
                        r = kt_rows[t]
                        if r < P:
                            last = dve.tensor_copy(v[:r, g % 2, t, :], src[:r, t - 4 * b, :])
                    last.then_inc(unit_taken, 1)
                elif u[0] == "max":
                    n, t, j, k = u[1:]
                    dve.wait_ge(unit_ready, i + 1)
                    dve.tensor_reduce(part_max[:, j, t, k:k + 1], src[:, :mxw], AX.X, ALU.max).then_inc(unit_taken, 1)
                elif u[0] == "divisors":
                    dve.wait_ge(unit_ready, i + 1)
                    n, den = u[1], src[:, :TPC * HG].rearrange("p (t j) -> p t j", j=HG)
                    if passed(n, 0):
                        steps = sum(2 for k in range(n) if passed(k, 0))
                        dve.wait_ge(exp_done, HG * (nkt * n + TPC * (n % NCH)))
                        dve.tensor_reduce(total[:, :, :], span_sum[:, n % 2, :, :, :n % NCH], AX.X, ALU.add).then_inc(total_step, 1)
                        dve.wait_ge(total_step, steps + 1)
                        dve.tensor_tensor(total[:, :, :], total[:, :, :], den, ALU.add).then_inc(total_step, 1)
                        dve.wait_ge(total_step, steps + 2)
                        den = total[:, :, :]
                    dve.reciprocal(inverse[:, :, :], den).then_inc(unit_taken, 1)
                    dve.wait_ge(unit_taken, i + 1)
                    dve.tensor_copy(spread[:, :, :, :], inverse[:, :, :].unsqueeze(3).to_broadcast([P, TPC, HG, SLOT])).then_inc(
                        inverse_spread, 1)
                elif u[0] == "divide":
                    g, o = u[1] // NCH, CH * (u[1] % NCH)
                    dve.wait_ge(unit_ready, i + 1)
                    dve.tensor_tensor(ot[:, g, o:o + CH], oc[:, :], src[:, :], ALU.mult).then_inc(unit_taken, 1)
                else:
                    n = u[1]
                    dve.wait_ge(unit_taken, i)
                    dve.tensor_reduce(row_max[:, :, :], part_max[:, :, :, :], AX.X, ALU.max).then_inc(rowmax_ready, 1)
                    dve.wait_ge(unit_ready, i + 1)
                    if n:
                        dve.wait_ge(negmax_loaded, 16 * HG * n)
                    dve.tensor_scalar(neg_max[:, :], src[:HG * TPC, :P], -1.0, None, ALU.mult).then_inc(negmax_ready, 1)
                    dve.wait_ge(negmax_ready, n + 1)
                    dve.sem_inc(unit_taken, 1)

            for u in order:
                take(u)

        @block.tensor
        def _(pe):
            def unit(u):
                i = number[u]
                dst = wb[i % NWB]
                if i >= NWB:
                    pe.wait_ge(unit_taken, i - NWB + 1)
                if u[0] == "k":
                    g, (o, w) = u[1], kch[u[2]]
                    for k in range(nkk):
                        last = pe.matmul(dst[:, :w], wks[:, g, k, :], xk[:, k, o:o + w], start=(k == 0), stop=(k == nkk - 1))
                elif u[0] == "q":
                    g, o = u[1] // NCH, CH * (u[1] % NCH)
                    for k in range(nkq):
                        last = pe.matmul(dst[:, :], wqs[:, g, k, :], xq[:, k, o:o + CH], start=(k == 0), stop=(k == nkq - 1))
                elif u[0] == "v":
                    g, b = u[1:]
                    for t in range(4 * b, min(4 * b + 4, nkt)):
                        r = kt_rows[t]
                        o = dst[:r, P * (t - 4 * b):P * (t - 4 * b) + P]
                        for k in range(nkk):
                            last = pe.matmul(o, xk[:, k, P * t:P * t + r], wvs[:, g, k, :], start=(k == 0),
                                             stop=(k == nkk - 1 and bv is None))
                        if bv is not None:
                            last = pe.matmul(o, ones[0:1, :r], bv[0:1, g, :], start=False, stop=True)
                elif u[0] == "max":
                    n, t, j, k = u[1:]
                    g = n // NCH
                    if (t, j) == (0, 0):
                        wait_stacked(pe, ("q", n))
                        if n % NCH == 0:
                            for c, (o, w) in enumerate(kch):
                                if o < mxs[k] + mxw:
                                    wait_stacked(pe, ("k", g, c))
                    last = pe.matmul(dst[:, :mxw], qs[:STACK, j, n % NQ, P * t:P * t + P],
                                     ks[:STACK, g % 2, j, mxs[k]:mxs[k] + mxw], start=True, stop=True)
                elif u[0] == "divisors":
                    pe.wait_ge(o_taken, NCOPY * (u[1] + 1))
                    pick = a["ident"][:, :].rearrange("p (j d) -> p j d", d=SLOT)[:, :, den_at]
                    for t in range(TPC):
                        last = pe.matmul(dst[:, HG * t:HG * t + HG], dc[:, P * t:P * t + P], pick, start=True, stop=True)
                elif u[0] == "divide":
                    pe.wait_ge(inverse_spread, u[1] + 1)
                    for t in range(TPC):
                        last = pe.matmul(dst[:, P * t:P * t + P], spread[:, t, :, :].rearrange("p j d -> p (j d)"),
                                         a["ident"][:, :], start=True, stop=True)
                else:
                    pe.wait_ge(rowmax_ready, u[1] + 1)
                    last = pe.transpose(dst[:HG * TPC, :P], row_max[:, :, :].rearrange("p j t -> p (j t)"), a["ident"][:, :])
                last.then_inc(unit_ready, 1)

            def score(n, kt, j):
                i = HG * (nkt * n + kt) + j
                r = kt_rows[kt]
                if i >= NSC:
                    pe.wait_ge(exp_done, i - NSC + 1)
                if passed(n, kt):
                    c, t = kt // TPC, kt % TPC
                    pe.matmul(sc[i % NSC][:, :], qs[:STACK + 1, j, n % NQ, P * t:P * t + P],
                              ks[:STACK + 1, n // NCH % 2, j, CH * c:CH * c + CH], start=True, stop=True).then_inc(sc_ready, 1)
                    return
                pe.matmul(sc[i % NSC][:r, :], ks[:STACK + 1, n // NCH % 2, j, P * kt:P * kt + r],
                          qs[:STACK + 1, j, n % NQ, :], start=True, stop=True).then_inc(sc_ready, 1)

            def sum_values(n, kt):
                m = nkt * n + kt
                r = kt_rows[kt]
                first = TPC * (n % NCH) if causal else 0
                if passed(n, kt):
                    return
                pe.wait_ge(exp_done, HG * (m + 1))
                if kt == first and n:
                    pe.wait_ge(o_taken, NCOPY * n)
                i = kt - first
                diagonal = causal and i < TPC
                if diagonal:
                    pe.wait_ge(masked, TPC * n + i + 1)
                for j in range(HG):
                    h = SLOT * j
                    w = v[:r, n // NCH % 2, kt, h:h + SLOT]
                    stop = kt == nkt - 1
                    if not diagonal:
                        last = pe.matmul(po[h:h + SLOT, :], w, e[:r, m % ering, j, :], start=(kt == first), stop=stop)
                        continue
                    if i:
                        pe.matmul(po[h:h + SLOT, :P * i], w, e[:r, m % ering, j, :P * i], start=False, stop=False)
                    pe.matmul(po[h:h + SLOT, P * i:P * i + P], w, em[:r, kt % 2, j, :], start=(i == 0), stop=stop)
                if not own_sum or kt in shared[n]:
                    last.then_inc(pv_done, 1)

            def sum_weights(n, kt):
                m = nkt * n + kt
                r = kt_rows[kt]
                if not own_sum or passed(n, kt) or kt in shared[n]:
                    return
                first = TPC * (n % NCH) if causal else 0
                if kt == nkt - 1 and not causal:
                    pe.wait_ge(part_added, nshared[n + 1])
                    for j in range(HG):
                        h = SLOT * j
                        pe.matmul(pd[h:h + SLOT, :], ones[:, :SLOT], part_sum[:, j, :], start=False, stop=False)
                for j in range(HG):
                    h = SLOT * j
                    last = pe.matmul(pd[h:h + SLOT, :], ones[:r, :SLOT], e[:r, m % ering, j, :],
                                     start=(kt == first), stop=(kt == nkt - 1))
                last.then_inc(pv_done, 1)

            for u in before:
                if u in (("k", 0, 0), ("q", 0), ("v", 0, 0)):
                    pe.wait_ge(w_loaded[u[0]], 16)
                unit(u)
            pe.wait_ge(ones_set, 1)
            shares = [1, 1, 1, 1, 1, 1 if own_sum else 0]
            tile_work = [PASSED_WORK if passed(m // nkt, m % nkt) else TILE_WORK for m in range(nkt * NC + 1)]
            for m in range(nkt * NC + 1):
                n, kt = m // nkt, m % nkt
                ahead = (m + LEAD) // nkt
                window = range(max(nkt * ahead - LEAD, 0), min(nkt * (ahead + 1) - LEAD, nkt * NC + 1))
                work = during[ahead] if ahead < NC else []
                in_all = sum(shares) * sum(tile_work[k] for k in window)

                def some_work(step):
                    before_tile = sum(shares) * sum(tile_work[k] for k in range(window.start, m))
                    lo, hi = (-(-len(work) * (before_tile + tile_work[m] * sum(shares[:i])) // in_all) for i in (step, step + 1))
                    for u in work[lo:hi]:
                        unit(u)

                if kt == 0 and n < NC:
                    pe.wait_ge(negmax_loaded, 16 * HG * (n + 1))
                for half in range(2):
                    if n < NC:
                        score(n, kt, 2 * half)
                    some_work(3 * half)
                    if n < NC:
                        score(n, kt, 2 * half + 1)
                    some_work(3 * half + 1)
                    if m and half == 0:
                        sum_values((m - 1) // nkt, (m - 1) % nkt)
                    elif m:
                        sum_weights((m - 1) // nkt, (m - 1) % nkt)
                    some_work(3 * half + 2)
            for u in after:
                unit(u)


def project_out(nc, name, ot, wo_dram, bias, res, dst):
    ctx, sb, ps, sem = phase(nc, name)
    with ctx:
        wo = sb("wo", [P, NG, D])
        y = [ps(f"y{i}", [P, D]) for i in range(4)]
        w_loaded, y_ready, summed, biased = sem("w_loaded"), sem("y_ready"), sem("summed"), sem("biased")
        block = ctx.enter_context(nc.Block())

        @block.sync
        def _(sp):
            sp.dma_start(wo[:, :, :], wo_dram).then_inc(w_loaded, 16)

        @block.tensor
        def _(pe):
            pe.wait_ge(w_loaded, 16)
            for t in range(NT):
                if t >= 4:
                    pe.wait_ge(summed, t - 3)
                for g in range(NG):
                    last = pe.matmul(y[t % 4][:, :], ot[:, g, P * t:P * t + P], wo[:, g, :], start=(g == 0), stop=(g == NG - 1))
                last.then_inc(y_ready, 1)

        @block.vector
        def _(dve):
            for t in range(NT):
                dve.wait_ge(y_ready, t + 1)
                dve.tensor_tensor(dst[:, t, :], y[t % 4][:, :], res[:, t, :], ALU.add).then_inc(summed, 1)

        @block.gpsimd
        def _(pool):
            for t in range(NT):
                pool.wait_ge(summed, t + 1)
                pool.tensor_tensor(dst[:, t, :], dst[:, t, :], bias, ALU.add).then_inc(biased, 1)


def gelu_ffn(nc, name, xt, w2_dram, w3_dram, b2, b3, xo, adds, dst):
    ctx, sb, ps, sem = phase(nc, name)
    nj = FF // P
    PRODUCTS = ((0, 0), (0, 1), (1, 0))
    NU = nj * NCH
    with ctx:
        w2 = sb("w2", [P, KC, FF])
        w3 = sb("w3", [P, nj, D])
        w2p = sb("w2p", [P, 2, KC, FF], F16)
        w3p = sb("w3p", [P, 2, nj, D], F16)
        xp = sb("xp", [P, 2, KC, T], F16)
        hf = sb("hf", [P, 2, CH])
        h = sb("h", [P, 2, 2, nj, CH], F16)
        hp = [ps(f"hp{i}", [P, CH]) for i in range(4)]
        y = [ps(f"y{i}", [P, D]) for i in range(4)]
        w2_loaded, w3_loaded, based = sem("w2_loaded"), sem("w3_loaded"), sem("based")
        w_high, w_split, x_high, x_split = sem("w_high"), sem("w_split"), sem("x_high"), sem("x_split")
        h_ready, hf_ready, h_high, h_done, y_ready, summed = (
            sem("h_ready"), sem("hf_ready"), sem("h_high"), sem("h_done"), sem("y_ready"), sem("summed"))
        block = ctx.enter_context(nc.Block())

        @block.sync
        def _(sp):
            sp.dma_start(w2[:, :, :], w2_dram).then_inc(w2_loaded, 16)
            sp.dma_start(w3[:, :, :], w3_dram).then_inc(w3_loaded, 16)

        @block.gpsimd
        def _(pool):
            for i, add in enumerate(adds):
                if i:
                    pool.wait_ge(based, i)
                pool.tensor_tensor(xo[:, :, :], xo[:, :, :], add[:, :, :], ALU.add).then_inc(based, 1)
            pool.wait_ge(based, len(adds))
            for t in range(NT):
                pool.tensor_tensor(xo[:, t, :], xo[:, t, :], b3, ALU.add).then_inc(based, 1)

        @block.tensor
        def _(pe):
            def hidden(c, j):
                n = nj * c + j
                if j == 0:
                    pe.wait_ge(x_split, c + 1)
                if n >= 4:
                    pe.wait_ge(hf_ready, n - 3)
                for k in range(KC):
                    for m, (pw, px) in enumerate(PRODUCTS):
                        last = pe.matmul(hp[n % 4][:, :], w2p[:, pw, k, P * j:P * j + P], xp[:, px, k, CH * c:CH * c + CH],
                                         start=(k == 0 and m == 0), stop=(k == KC - 1 and m == 2))
                last.then_inc(h_ready, 1)

            def out(t):
                c = t // TPC
                pe.wait_ge(h_done, nj * (c + 1))
                if t >= 4:
                    pe.wait_ge(summed, t - 3)
                q = P * (t % TPC)
                for j in range(nj):
                    for m, (ph, pw) in enumerate(PRODUCTS):
                        last = pe.matmul(y[t % 4][:, :], h[:, c % 2, ph, j, q:q + P], w3p[:, pw, j, :],
                                         start=(j == 0 and m == 0), stop=(j == nj - 1 and m == 2))
                last.then_inc(y_ready, 1)

            pe.wait_ge(w_split, 1)
            for c in range(NCH + 1):
                if c == 1:
                    pe.wait_ge(w_split, 2)
                for i in range(nj):
                    if c < NCH:
                        hidden(c, i)
                    if c >= 1 and i % 2 == 1:
                        out(TPC * (c - 1) + i // 2)

        @block.scalar
        def _(act):
            act.wait_ge(w2_loaded, 16)
            act.activation(w2p[:, 0, :, :], w2[:, :, :], ACT.Copy).then_inc(w_high, 1)
            act.wait_ge(w3_loaded, 16)
            act.activation(w3p[:, 0, :, :], w3[:, :, :], ACT.Copy).then_inc(w_high, 1)
            for n in range(NU):
                c, j = n // nj, n % nj
                act.wait_ge(h_ready, n + 1)
                if n >= 2:
                    act.wait_ge(h_done, n - 1)
                act.activation(hf[:, n % 2, :], hp[n % 4][:, :], ACT.Gelu, bias=b2[:, j:j + 1]).then_inc(hf_ready, 1)
                act.wait_ge(hf_ready, n + 1)
                if c >= 2 and j == 0:
                    act.wait_ge(y_ready, TPC * (c - 1))
                act.activation(h[:, c % 2, 0, j, :], hf[:, n % 2, :], ACT.Copy).then_inc(h_high, 1)

        @block.vector
        def _(dve):
            def split_tokens(c):
                x = slice(CH * c, CH * c + CH)
                dve.tensor_copy(xp[:, 0, :, x], xt[:, :, x]).then_inc(x_high, 1)
                dve.wait_ge(x_high, c + 1)
                dve.tensor_tensor(xp[:, 1, :, x], xt[:, :, x], xp[:, 0, :, x], ALU.subtract).then_inc(x_split, 1)

            def low(n):
                c, j = n // nj, n % nj
                dve.wait_ge(h_high, n + 1)
                dve.tensor_tensor(h[:, c % 2, 1, j, :], hf[:, n % 2, :], h[:, c % 2, 0, j, :], ALU.subtract).then_inc(h_done, 1)

            def add(t):
                dve.wait_ge(y_ready, t + 1)
                dve.wait_ge(based, len(adds) + t + 1)
                dve.tensor_tensor(dst[:, t, :], y[t % 4][:, :], xo[:, t, :], ALU.add).then_inc(summed, 1)

            split_tokens(0)
            for i, (w, wp) in enumerate(((w2, w2p), (w3, w3p))):
                dve.wait_ge(w_high, i + 1)
                dve.tensor_tensor(wp[:, 1, :, :], w[:, :, :], wp[:, 0, :, :], ALU.subtract).then_inc(w_split, 1)
            for c in range(1, NCH):
                split_tokens(c)
            for c in range(NCH + 1):
                for j in range(nj):
                    if c < NCH:
                        low(nj * c + j)
                    if c >= 1 and j % 2 == 1:
                        add(TPC * (c - 1) + j // 2)


class Chain:

    def __init__(self, engine, sem):
        self.engine, self.sem, self.n = engine, sem, 0

    def __call__(self, instruction):
        self.n += 1
        instruction.then_inc(self.sem, 1)
        self.engine.wait_ge(self.sem, self.n)


def over(ap, n):
    return ap.unsqueeze(2).to_broadcast([ap.shape[0], ap.shape[1], n])


def router_stats(nc, z, zst, ident):
    ctx, sb, ps, sem = phase(nc, "stats")
    with ctx:
        st = sb("st", [P, NT, 6])
        mv = sb("mv", [P, NT, 2])
        sq = sb("sq", [P, NT])
        f = sb("f", [P, NT, NSTAT])
        small = sb("small", [P, NT, D])
        tp = [ps(f"tp{i}", [NSTAT, CH]) for i in range(NCH)]
        chain, sums_ready, roots_ready, turned, taken = sem("chain"), sem("sums_ready"), sem("roots_ready"), sem("turned"), sem("taken")
        block = ctx.enter_context(nc.Block())

        @block.vector
        def _(dve):
            link = Chain(dve, chain)
            for t in range(NT):
                last = dve.bn_stats(st[:, t, :], z[:, t, :])
            link(last)
            for t in range(NT):
                last = dve.bn_aggr(mv[:, t, :], st[:, t, :])
            link(last)
            dve.tensor_copy(f[:, :, 0], mv[:, :, 0])
            link(dve.tensor_tensor(sq[:, :], mv[:, :, 0], mv[:, :, 0], ALU.mult))
            dve.tensor_tensor(sq[:, :], sq[:, :], mv[:, :, 1], ALU.add).then_inc(sums_ready, 1)
            dve.tensor_reduce(f[:, :, 2], z[:, :, :], AX.X, ALU.min)
            dve.tensor_reduce(f[:, :, 3], z[:, :, :], AX.X, ALU.max)
            link(dve.tensor_scalar(small[:, :, :], z[:, :, :], 1e-6, None, ALU.is_lt))
            flat_z, flat_small = (v[:, :, :].rearrange("p t d -> p (t d)") for v in (z, small))
            link(dve.scalar_tensor_tensor(out=flat_small, in0=flat_z, scalar=-1e-6, in1=flat_small, op0=ALU.is_gt, op1=ALU.mult))
            link(dve.tensor_reduce(f[:, :, 5], small[:, :, :], AX.X, ALU.add))
            link(dve.tensor_scalar(f[:, :, 5], f[:, :, 5], 1.0 / D, None, ALU.mult))
            for c in range(NCH):
                dve.wait_ge(turned, c + 1)
                dve.tensor_copy(zst[:NSTAT, CH * c:CH * c + CH], tp[c][:, :]).then_inc(taken, 1)

        @block.scalar
        def _(act):
            act.wait_ge(sums_ready, 1)
            act.activation(f[:, :, 4], sq[:, :], ACT.Sqrt, scale=float(D)).then_inc(roots_ready, 1)
            act.activation(f[:, :, 1], mv[:, :, 1], ACT.Sqrt, scale=D / (D - 1.0)).then_inc(roots_ready, 1)

        @block.tensor
        def _(pe):
            pe.wait_ge(roots_ready, 2)
            pe.wait_ge(chain, 7)
            for c in range(NCH):
                for i in range(TPC):
                    last = pe.transpose(tp[c][:, P * i:P * i + P], f[:, TPC * c + i, :], ident[:, :])
                last.then_inc(turned, 1)


def router(nc, a, zt, zst, r1b, wc, picks, ident):
    ctx, sb, ps, sem = phase(nc, "router")
    with ctx:
        r1 = sb("r1", [P, KC, P])
        r1s = sb("r1s", [NSTAT, P])
        r2 = sb("r2", [P, E0])
        h = sb("h", [P, T])
        hp = [ps(f"hp{i}", [P, CH]) for i in range(2)]
        lg = ps("lg", [P, NT, E0])
        tp = [ps(f"tp{i}", [E0, CH]) for i in range(NCH)]
        pr = sb("pr", [P, NT, E0])
        top = sb("top", [P, NT, 8])
        at = sb("at", [P, NT, 8], U32)
        atf = sb("atf", [P, NT, 8])
        iota = sb("iota", [P, NT, E0])
        mask = sb("mask", [P, NT, E0])
        one = sb("one", [P, NT, E0])
        m = sb("m", [P, NT])
        w_loaded, iota_ready, chain = sem("w_loaded"), sem("iota_ready"), sem("chain")
        h_ready, h_done, logits_ready, shifted, exped = sem("h_ready"), sem("h_done"), sem("logits_ready"), sem("shifted"), sem("exped")
        picked, turned, taken = sem("picked"), sem("turned"), sem("taken")
        block = ctx.enter_context(nc.Block())

        @block.sync
        def _(sp):
            sp.dma_start(r1[:, :, :], a["r1"]).then_inc(w_loaded, 16)
            sp.dma_start(r1s[:, :], a["r1s"]).then_inc(w_loaded, 16)
            sp.dma_start(r2[:, :], a["r2"]).then_inc(w_loaded, 16)

        @block.gpsimd
        def _(pool):
            pool.iota(iota[:, :, :], [[0, NT], [1, E0]], base=0, channel_multiplier=0,
                      allow_small_or_imprecise_dtypes=True).then_inc(iota_ready, 1)

        @block.tensor
        def _(pe):
            pe.wait_ge(w_loaded, 48)
            for c in range(NCH):
                if c >= 2:
                    pe.wait_ge(h_done, c - 1)
                o = hp[c % 2][:, :]
                x = slice(CH * c, CH * c + CH)
                for k in range(KC):
                    pe.matmul(o, r1[:, k, :], zt[:, k, x], start=(k == 0), stop=False)
                pe.matmul(o, r1s[:, :], zst[:NSTAT, x], start=False, stop=True).then_inc(h_ready, 1)
            for t in range(NT):
                pe.wait_ge(h_done, t // TPC + 1)
                last = pe.matmul(lg[:, t, :], h[:, P * t:P * t + P], r2[:, :], start=True, stop=True)
            last.then_inc(logits_ready, 1)
            pe.wait_ge(picked, 1)
            for c in range(NCH):
                for i in range(TPC):
                    last = pe.transpose(tp[c][:, P * i:P * i + P], one[:, TPC * c + i, :], ident[:, :])
                last.then_inc(turned, 1)

        @block.scalar
        def _(act):
            for c in range(NCH):
                act.wait_ge(h_ready, c + 1)
                act.activation(h[:, CH * c:CH * c + CH], hp[c % 2][:, :], ACT.Gelu, bias=r1b).then_inc(h_done, 1)
            act.wait_ge(shifted, 1)
            act.activation(pr[:, :, :], pr[:, :, :], ACT.Exp).then_inc(exped, 1)

        @block.vector
        def _(dve):
            link = Chain(dve, chain)
            dve.wait_ge(logits_ready, 1)
            link(dve.tensor_reduce(m[:, :], lg[:, :, :], AX.X, ALU.max))
            dve.tensor_tensor(pr[:, :, :], lg[:, :, :], over(m[:, :], E0), ALU.subtract).then_inc(shifted, 1)
            dve.wait_ge(exped, 1)
            link(dve.tensor_reduce(m[:, :], pr[:, :, :], AX.X, ALU.add))
            link(dve.reciprocal(m[:, :], m[:, :]))
            link(dve.tensor_tensor(pr[:, :, :], pr[:, :, :], over(m[:, :], E0), ALU.mult))
            for t in range(NT):
                last = dve.max(top[:, t, :], pr[:, t, :])
            link(last)
            for t in range(NT):
                last = dve.max_index(at[:, t, :], top[:, t, :], pr[:, t, :])
            link(last)
            link(dve.tensor_copy(atf[:, :, :], at[:, :, :]))
            dve.wait_ge(iota_ready, 1)
            dve.tensor_tensor(mask[:, :, :], iota[:, :, :], over(atf[:, :, 0], E0), ALU.is_equal)
            link(dve.tensor_tensor(one[:, :, :], iota[:, :, :], over(atf[:, :, 1], E0), ALU.is_equal))
            dve.tensor_tensor(m[:, :], top[:, :, 0], top[:, :, 1], ALU.add)
            link(dve.tensor_tensor(mask[:, :, :], mask[:, :, :], one[:, :, :], ALU.add))
            link(dve.reciprocal(m[:, :], m[:, :]))
            link(dve.tensor_tensor(pr[:, :, :], pr[:, :, :], mask[:, :, :], ALU.mult))
            dve.tensor_tensor(wc[:, :, :], pr[:, :, :], over(m[:, :], E0), ALU.mult)
            link(dve.tensor_scalar(mask[:, :, :], mask[:, :, :], 1.0, None, ALU.subtract))
            dve.tensor_tensor(one[:, :, :], pr[:, :, :], mask[:, :, :], ALU.add).then_inc(picked, 1)
            for c in range(NCH):
                dve.wait_ge(turned, c + 1)
                dve.tensor_copy(picks[:, CH * c:CH * c + CH], tp[c][:, :]).then_inc(taken, 1)


def choose(nc, a, picks, z, wc, x_sb, slots, ident):
    ctx, sb, ps, sem = phase(nc, "choose")
    with ctx:
        other = sb("other", [E0, T])
        val = sb("val", [E0, CAP])
        at = sb("at", [E0, CAP], U32)
        atf = sb("atf", [E0, CAP])
        tp = ps("tp", [CAP, E0])
        chain, at_ready, turned, stored = sem("chain"), sem("at_ready"), sem("turned"), sem("stored")
        block = ctx.enter_context(nc.Block())

        @block.sync
        def _(sp):
            rows = a["table"].rearrange("(t p) c -> p t c", p=P)
            sp.dma_start(rows[:, :, :D], z[:, :, :]).then_inc(stored, 16)
            sp.dma_start(rows[:, :, D:], wc[:, :, :]).then_inc(stored, 16)
            sp.dma_start(a["acc"].rearrange("(t p) d -> p t d", p=P), x_sb[:, :, :]).then_inc(stored, 16)
            sp.wait_ge(stored, 48)

        @block.vector
        def _(dve):
            link = Chain(dve, chain)
            buf = [picks, other]
            for r in range(CAP // 8):
                src, dst = buf[r % 2], buf[(r + 1) % 2]
                o = slice(8 * r, 8 * r + 8)
                link(dve.max(val[:, o], src[:, :]))
                link(dve.max_index(at[:, o], val[:, o], src[:, :]))
                if r < CAP // 8 - 1:
                    link(dve.match_replace(dst[:, :], val[:, o], src[:, :], -2.0))
            dve.tensor_copy(atf[:, :], at[:, :]).then_inc(at_ready, 1)
            dve.wait_ge(turned, 1)
            link(dve.tensor_copy(slots[:CAP, :], tp[:, :]))

        @block.tensor
        def _(pe):
            pe.wait_ge(at_ready, 1)
            pe.transpose(tp[:, :], atf[:, :], ident[:E0, :E0]).then_inc(turned, 1)


def experts(nc, a, slots, x_sb, ident):
    ctx, sb, ps, sem = phase(nc, "experts")
    NJ = INTER // P
    UP = KC * 2 * INTER
    NP = E0 // 2
    with ctx:
        xe = [sb(f"xe{i}", [CAP, ROW]) for i in range(2)]
        xet = [sb(f"xet{i}", [P, KC, CAP]) for i in range(2)]
        we = sb("we", [CAP, 2])
        w_up = [sb(f"w_up{i}", [P, UP]) for i in range(2)]
        w_down = [sb(f"w_down{i}", [P, NJ * D]) for i in range(2)]
        aw = sb("aw", [P, KC * 2 * AI + D])
        sg = [sb(f"sg{i}", [P, NJ + 1, CAP]) for i in range(2)]
        h = [sb(f"h{i}", [P, NJ + 1, CAP]) for i in range(2)]
        ye = [sb(f"ye{i}", [CAP, D]) for i in range(2)]
        gp = [ps(f"gp{i}", [P, NJ + 1, CAP]) for i in range(2)]
        up = [ps(f"up{i}", [P, NJ + 1, CAP]) for i in range(2)]
        y = [ps(f"y{i}", [CAP, D]) for i in range(2)]
        tp = [ps(f"tp{i}", [P, KC, CAP]) for i in range(2)]
        gathered = [sem(f"gathered{i}") for i in range(2)]
        up_loaded = [sem(f"up_loaded{i}") for i in range(2)]
        down_loaded = [sem(f"down_loaded{i}") for i in range(2)]
        turned, xet_ready, taken, aw_loaded = sem("turned"), sem("xet_ready"), sem("taken"), sem("aw_loaded")
        gu_ready, silu_done, h_done = sem("gu_ready"), sem("silu_done"), sem("h_done")
        y_ready, ye_ready, added, back = sem("y_ready"), sem("ye_ready"), sem("added"), sem("back")
        block = ctx.enter_context(nc.Block())

        @block.sync
        def _(sp):
            def of_expert(e):
                return a["we"][bass.ds(e, 1)].rearrange("o p n -> (o p) n")

            def load(i, s, down):
                if down:
                    sp.dma_start(w_down[s][:, :], of_expert(2 * i + s)[:, UP:]).then_inc(down_loaded[s], 16)
                else:
                    sp.dma_start(w_up[s][:, :], of_expert(2 * i + s)[:, :UP]).then_inc(up_loaded[s], 16)

            def load_adapter(i):
                sp.dma_start(aw[:, :], a["aw"][bass.ds(i, 1)].rearrange("o p n -> (o p) n")).then_inc(aw_loaded, 16)

            load(0, 0, False)
            load_adapter(0)
            load(0, 1, False)
            load(0, 0, True)
            load(0, 1, True)
            with sp.Fori(1, NP) as i:
                for s in range(2):
                    sp.wait_ge(gu_ready, 2 * i - 1 + s)
                    load(i, s, False)
                sp.wait_ge(y_ready, 2 * i)
                load_adapter(i)
                load(i, 0, True)
                load(i, 1, True)
            sp.wait_ge(added, 16 * E0)
            sp.dma_start(x_sb[:, :, :], a["acc"].rearrange("(t p) d -> p t d", p=P)).then_inc(back, 16)
            sp.wait_ge(back, 16)

        @block.gpsimd
        def _(pool):
            def gather(e):
                if e >= 2:
                    pool.wait_ge(taken, e - 1)
                pool.indirect_dma_start(xe[e % 2][:, :], None, a["table"],
                                        bass.IndirectOffsetOnAxis(slots[:CAP, e:e + 1], 0)).then_inc(gathered[e % 2], 16)

            for e in range(4):
                gather(e)
            for e in range(E0):
                pool.wait_ge(ye_ready, e + 1)
                if e >= 1:
                    pool.wait_ge(added, 16 * e)
                pool.indirect_dma_start(a["acc"], bass.IndirectOffsetOnAxis(slots[:CAP, e:e + 1], 0), ye[e % 2][:, :], None,
                                        compute_op=ALU.add).then_inc(added, 16)
                if e + 4 < E0:
                    gather(e + 4)

        @block.tensor
        def _(pe):
            def turn(i, s):
                pe.wait_ge(gathered[s], 16 * i + 16)
                for k in range(KC):
                    last = pe.transpose(tp[s][:, k, :], xe[s][:, P * k:P * k + P], ident[:CAP, :CAP])
                last.then_inc(turned, 1)

            def hidden(i, s):
                pe.wait_ge(up_loaded[s], 16 * i + 16)
                pe.wait_ge(xet_ready, 2 * i + s + 1)
                for dst, off in ((gp[s], 0), (up[s], INTER)):
                    for j in range(NJ):
                        for k in range(KC):
                            o = 2 * INTER * k + off + P * j
                            pe.matmul(dst[:, j, :], w_up[s][:, o:o + P], xet[s][:, k, :], start=(k == 0), stop=(k == KC - 1))
                if s == 0:
                    pe.wait_ge(aw_loaded, 16 * i + 16)
                for dst, off in ((gp[s], 0), (up[s], AI)):
                    for k in range(KC):
                        o = 2 * AI * k + off
                        last = pe.matmul(dst[:, NJ, :], aw[:, o:o + AI], xet[s][:, k, :], start=(k == 0), stop=(k == KC - 1))
                last.then_inc(gu_ready, 1)

            def output(i, s):
                pe.wait_ge(down_loaded[s], 16 * i + 16)
                pe.wait_ge(h_done, 2 * i + s + 1)
                pe.wait_ge(ye_ready, 2 * i)
                for j in range(NJ + 1):
                    rhs = w_down[s][:, D * j:D * j + D] if j < NJ else aw[:, KC * 2 * AI:]
                    last = pe.matmul(y[s][:, :], h[s][:, j, :], rhs, start=(j == 0), stop=(j == NJ))
                last.then_inc(y_ready, 1)

            def pair(i, last):
                for s in range(2):
                    hidden(i, s)
                for s in range(0 if last else 2):
                    turn(i + 1, s)
                for s in range(2):
                    output(i, s)

            for s in range(2):
                turn(0, s)
            with pe.Fori(0, NP - 1) as i:
                pair(i, False)
            pair(NP - 1, True)

        @block.scalar
        def _(act):
            with act.Fori(0, NP) as i:
                for s in range(2):
                    act.wait_ge(gu_ready, 2 * i + s + 1)
                    act.wait_ge(h_done, 2 * i)
                    act.activation(sg[s][:, :, :], gp[s][:, :, :], ACT.Silu).then_inc(silu_done, 1)

        @block.vector
        def _(dve):
            def take_turned(i, s):
                dve.wait_ge(turned, 2 * i + s + 1)
                dve.tensor_copy(xet[s][:, :, :], tp[s][:, :, :]).then_inc(xet_ready, 1)

            def take_weights(i, s):
                dve.tensor_copy(we[:, s:s + 1], xe[s][:, bass.ds(2 * i + (D + s), 1)]).then_inc(taken, 1)

            def pair(i, first=False, last=False):
                for s in range(2):
                    dve.wait_ge(silu_done, 2 * i + s + 1)
                    dve.wait_ge(y_ready, 2 * i)
                    dve.tensor_tensor(h[s][:, :NJ, :], sg[s][:, :NJ, :], up[s][:, :NJ, :], ALU.mult)
                    dve.scalar_tensor_tensor(out=h[s][:, NJ, :], in0=sg[s][:, NJ, :], scalar=0.05, in1=up[s][:, NJ, :],
                                             op0=ALU.mult, op1=ALU.mult).then_inc(h_done, 1)
                for s in range(0 if last else 2):
                    take_turned(i + 1, s)
                for s in range(2):
                    dve.wait_ge(y_ready, 2 * i + s + 1)
                    dve.wait_ge(taken, 2 * i + s + 1)
                    if not first:
                        dve.wait_ge(added, 32 * i + 16 * (s - 1))
                    dve.tensor_scalar(ye[s][:, :], y[s][:, :], we[:, s:s + 1], None, ALU.mult).then_inc(ye_ready, 1)
                for s in range(0 if last else 2):
                    dve.wait_ge(ye_ready, 2 * i + s + 1)
                    take_weights(i + 1, s)

            for s in range(2):
                take_turned(0, s)
                take_weights(0, s)
            pair(0, first=True)
            with dve.Fori(1, NP - 1) as i:
                pair(i)
            pair(NP - 1, last=True)


def gate1(nc, a, xt, gate_bias, cw):
    ctx, sb, ps, sem = phase(nc, "gate1")
    with ctx:
        gw = sb("gw", [P, KC, E1])
        lg = ps("lg", [P, NT, E1])
        sco = sb("sco", [P, NT, E1])
        sfc = sb("sfc", [P, NT, E1])
        hi = sb("hi", [P, NT * G1, 2])
        lo = sb("lo", [P, NT * G1, 2])
        t1 = sb("t1", [P, NT * G1])
        t2 = sb("t2", [P, NT * G1])
        gs = sb("gs", [P, NT, 8])
        top = sb("top", [P, NT, 8])
        at = sb("at", [P, NT, 8], U32)
        atf = sb("atf", [P, NT, 8])
        iota = sb("iota", [P, NT, E1])
        m4 = sb("m4", [P, NT, G1])
        m4b = sb("m4b", [P, NT, G1])
        m16 = [sb(f"m16{i}", [P, NT, E1]) for i in range(4)]
        tot = sb("tot", [P, NT])
        w_loaded, iota_ready, logits_ready, sig_ready, chain = sem("w_loaded"), sem("iota_ready"), sem("logits_ready"), sem("sig_ready"), sem("chain")
        block = ctx.enter_context(nc.Block())

        @block.sync
        def _(sp):
            sp.dma_start(gw[:, :, :], a["gw"]).then_inc(w_loaded, 16)

        @block.gpsimd
        def _(pool):
            pool.iota(iota[:, :, :], [[0, NT], [1, E1]], base=0, channel_multiplier=0,
                      allow_small_or_imprecise_dtypes=True).then_inc(iota_ready, 1)

        @block.tensor
        def _(pe):
            pe.wait_ge(w_loaded, 16)
            for t in range(NT):
                for k in range(KC):
                    last = pe.matmul(lg[:, t, :], xt[:, k, P * t:P * t + P], gw[:, k, :], start=(k == 0), stop=(k == KC - 1))
            last.then_inc(logits_ready, 1)

        @block.scalar
        def _(act):
            act.wait_ge(logits_ready, 1)
            act.activation(sco[:, :, :], lg[:, :, :], ACT.Sigmoid).then_inc(sig_ready, 1)

        @block.vector
        def _(dve):
            link = Chain(dve, chain)
            dve.memset(cw[:, :, E1:], 1.0)
            dve.memset(gs[:, :, :], -3e38)
            dve.wait_ge(sig_ready, 1)
            dve.wait_ge(iota_ready, 1)
            link(dve.tensor_tensor(sfc[:, :, :], sco[:, :, :], gate_bias.unsqueeze(1).to_broadcast([P, NT, E1]), ALU.add))
            four = sfc[:, :, :].rearrange("p t (g i) -> p (t g) i", i=E1 // G1)
            dve.tensor_tensor(hi[:, :, :], four[:, :, 0:2], four[:, :, 2:4], ALU.max)
            link(dve.tensor_tensor(lo[:, :, :], four[:, :, 0:2], four[:, :, 2:4], ALU.min))
            dve.tensor_tensor(t1[:, :], hi[:, :, 0], hi[:, :, 1], ALU.min)
            link(dve.tensor_tensor(t2[:, :], lo[:, :, 0], lo[:, :, 1], ALU.max))
            link(dve.tensor_tensor(t1[:, :], t1[:, :], t2[:, :], ALU.max))
            link(dve.tensor_tensor(t2[:, :], hi[:, :, 0], hi[:, :, 1], ALU.max))
            link(dve.tensor_tensor(gs[:, :, :G1], t1[:, :].rearrange("p (t g) -> p t g", g=G1),
                                   t2[:, :].rearrange("p (t g) -> p t g", g=G1), ALU.add))
            for t in range(NT):
                last = dve.max(top[:, t, :], gs[:, t, :])
            link(last)
            for t in range(NT):
                last = dve.max_index(at[:, t, :], top[:, t, :], gs[:, t, :])
            link(last)
            link(dve.tensor_copy(atf[:, :, :], at[:, :, :]))
            dve.tensor_tensor(m4[:, :, :], iota[:, :, :G1], over(atf[:, :, 0], G1), ALU.is_equal)
            link(dve.tensor_tensor(m4b[:, :, :], iota[:, :, :G1], over(atf[:, :, 1], G1), ALU.is_equal))
            link(dve.tensor_tensor(m4[:, :, :], m4[:, :, :], m4b[:, :, :], ALU.add))
            link(dve.tensor_tensor(four, four, over(m4[:, :, :].rearrange("p t g -> p (t g)"), E1 // G1), ALU.mult))
            link(dve.tensor_scalar(sfc[:, :, :], sfc[:, :, :], 0.0, None, ALU.add))
            for t in range(NT):
                last = dve.max(top[:, t, :], sfc[:, t, :])
            link(last)
            for t in range(NT):
                last = dve.max_index(at[:, t, :], top[:, t, :], sfc[:, t, :])
            link(last)
            link(dve.tensor_copy(atf[:, :, :], at[:, :, :]))
            for i in range(TOPK1):
                last = dve.tensor_tensor(m16[i][:, :, :], iota[:, :, :], over(atf[:, :, i], E1), ALU.is_equal)
            link(last)
            dve.tensor_tensor(m16[0][:, :, :], m16[0][:, :, :], m16[1][:, :, :], ALU.add)
            link(dve.tensor_tensor(m16[2][:, :, :], m16[2][:, :, :], m16[3][:, :, :], ALU.add))
            link(dve.tensor_tensor(m16[0][:, :, :], m16[0][:, :, :], m16[2][:, :, :], ALU.add))
            link(dve.tensor_tensor(sco[:, :, :], sco[:, :, :], m16[0][:, :, :], ALU.mult))
            link(dve.tensor_reduce(tot[:, :], sco[:, :, :], AX.X, ALU.add))
            link(dve.tensor_scalar(tot[:, :], tot[:, :], 1e-20, None, ALU.add))
            link(dve.reciprocal(tot[:, :], tot[:, :]))
            link(dve.tensor_tensor(cw[:, :, :E1], sco[:, :, :], over(tot[:, :], E1), ALU.mult))


def moe(nc, a, xt, cw, x_sb, out):
    ctx, sb, ps, sem = phase(nc, "moe")
    it_rows = tiles_of(EI)
    NI = len(it_rows)
    UP, DN = KC * EI, 2 * KC * EI
    WN = DN + NI * D
    NE = E1 + SH
    NPAIR = NE // 2
    NU = 2 * NCH * NI
    NY = 2 * NT
    PIECES = 4
    PRODUCTS = ((0, 0), (0, 1), (1, 0))

    def out_tiles(it):
        return range(TPC * max(it - 1, 0) // (NI - 1), TPC * it // (NI - 1))

    with ctx:
        w = [sb(f"w{i}", [P, WN]) for i in range(2)]
        wp = [sb(f"wp{i}", [P, 2, WN], F16) for i in range(2)]
        xp = sb("xp", [P, 2, KC, T], F16)
        sg = sb("sg", [P, 2, CH])
        hf = sb("hf", [P, 2, CH])
        h = sb("h", [P, 2, 2, NI, CH], F16)
        gp = [ps(f"gp{i}", [P, CH]) for i in range(2)]
        up = [ps(f"up{i}", [P, CH]) for i in range(2)]
        y = [ps(f"y{i}", [P, D]) for i in range(4)]
        w_loaded = [sem(f"w_loaded{i}") for i in range(2)]
        x_high, x_split, w_high, w_split = sem("x_high"), sem("x_split"), sem("w_high"), sem("w_split")
        gu_ready, silu_done, hf_ready, h_high, h_done = sem("gu_ready"), sem("silu_done"), sem("hf_ready"), sem("h_high"), sem("h_done")
        y_ready, summed, stored = sem("y_ready"), sem("summed"), sem("stored")
        block = ctx.enter_context(nc.Block())

        @block.sync
        def _(sp):
            for s in range(2):
                sp.dma_start(w[s][:, :], a["wm"][s]).then_inc(w_loaded[s], 16)
            with sp.Fori(0, NPAIR - 1) as i:
                for s in range(2):
                    sp.wait_ge(w_split, PIECES * (2 * i + s + 1))
                    sp.dma_start(w[s][:, :], a["wm"][bass.ds(2 * i + (2 + s), 1)].rearrange("o p n -> (o p) n")).then_inc(w_loaded[s], 16)
            sp.wait_ge(summed, NY * NPAIR)
            sp.dma_start(out.rearrange("o (t p) d -> p (o t) d", p=P), x_sb[:, :, :]).then_inc(stored, 16)
            sp.wait_ge(stored, 16)

        @block.tensor
        def _(pe):
            def hidden(i, c, it, first):
                s, n = c // NCH, NI * c + it
                c, r = c % NCH, it_rows[it]
                if n >= 2 or not first:
                    pe.wait_ge(hf_ready, NU * i + (n - 1))
                for dst, off in ((gp[n % 2], 0), (up[n % 2], UP)):
                    for k in range(KC):
                        o = off + EI * k + P * it
                        for m, (pw, px) in enumerate(PRODUCTS):
                            last = pe.matmul(dst[:r, :], wp[s][:, pw, o:o + r], xp[:, px, k, CH * c:CH * c + CH],
                                             start=(k == 0 and m == 0), stop=(k == KC - 1 and m == 2))
                last.then_inc(gu_ready, 1)

            def out_tile(i, n, first):
                s, t, c = n // NT, n % NT, n // TPC
                pe.wait_ge(h_done, NU * i + NI * (c + 1))
                if n >= 4 or not first:
                    pe.wait_ge(summed, NY * i + (n - 3))
                q = P * (t % TPC)
                for it in range(NI):
                    r = it_rows[it]
                    o = DN + D * it
                    for m, (ph, pw) in enumerate(PRODUCTS):
                        last = pe.matmul(y[n % 4][:, :], h[:r, c % 2, ph, it, q:q + P], wp[s][:r, pw, o:o + D],
                                         start=(it == 0 and m == 0), stop=(it == NI - 1 and m == 2))
                last.then_inc(y_ready, 1)

            def pair(i, first=False):
                for c in range(2 * NCH):
                    if c % NCH == 0:
                        pe.wait_ge(w_split, PIECES * (2 * i + c // NCH + 1))
                    for it in range(NI):
                        hidden(i, c, it, first)
                        for q in out_tiles(it):
                            if c:
                                out_tile(i, TPC * (c - 1) + q, first)
                            elif not first:
                                out_tile(i - 1, TPC * (2 * NCH - 1) + q, False)

            pe.wait_ge(x_split, 1)
            pair(0, first=True)
            with pe.Fori(1, NPAIR) as i:
                pair(i)
            for q in range(TPC):
                out_tile(NPAIR - 1, TPC * (2 * NCH - 1) + q, False)

        @block.scalar
        def _(act):
            def silu(i, n):
                r = it_rows[n % NI]
                act.wait_ge(gu_ready, NU * i + n + 1)
                act.wait_ge(hf_ready, NU * i + max(n - 1, 0))
                act.activation(sg[:r, n % 2, :], gp[n % 2][:r, :], ACT.Silu).then_inc(silu_done, 1)

            def high(i, n, first):
                it, c = n % NI, n // NI
                r = it_rows[it]
                act.wait_ge(hf_ready, NU * i + n + 1)
                if it == 0 and (c >= 2 or not first):
                    act.wait_ge(y_ready, NY * i + TPC * (c - 1))
                act.activation(h[:r, c % 2, 0, it, :], hf[:r, n % 2, :], ACT.Copy).then_inc(h_high, 1)

            def pair(i, first=False):
                for n in range(NU + 1):
                    if n < NU:
                        silu(i, n)
                    if n >= 1:
                        high(i, n - 1, first)

            pair(0, first=True)
            with act.Fori(1, NPAIR) as i:
                pair(i)

        @block.vector
        def _(dve):
            def product(i, n):
                r = it_rows[n % NI]
                dve.wait_ge(silu_done, NU * i + n + 1)
                dve.wait_ge(h_done, NU * i + max(n - 1, 0))
                dve.tensor_tensor(hf[:r, n % 2, :], sg[:r, n % 2, :], up[n % 2][:r, :], ALU.mult).then_inc(hf_ready, 1)

            def low(i, n):
                it, c = n % NI, n // NI
                r = it_rows[it]
                dve.wait_ge(h_high, NU * i + n + 1)
                dve.tensor_tensor(h[:r, c % 2, 1, it, :], hf[:r, n % 2, :], h[:r, c % 2, 0, it, :], ALU.subtract).then_inc(h_done, 1)

            def add(i, n):
                s, t = n // NT, n % NT
                dve.wait_ge(y_ready, NY * i + n + 1)
                if n % NT == 0:
                    dve.wait_ge(summed, NY * i + n)
                dve.scalar_tensor_tensor(out=x_sb[:, t, :], in0=y[n % 4][:, :], scalar=cw[:, t, bass.ds(2 * i + s, 1)],
                                         in1=x_sb[:, t, :], op0=ALU.mult, op1=ALU.add).then_inc(summed, 1)

            def split(i, s, k):
                if k == 0:
                    dve.wait_ge(w_loaded[s], 16 * i + 16)
                    dve.wait_ge(y_ready, NY * i - NT * (1 - s))
                parts(s, k, PIECES * (2 * i + s))

            def parts(s, k, before):
                x = slice(WN * k // PIECES, WN * (k + 1) // PIECES)
                dve.tensor_copy(wp[s][:, 0, x], w[s][:, x]).then_inc(w_high, 1)
                dve.wait_ge(w_high, before + (k + 1))
                dve.tensor_tensor(wp[s][:, 1, x], w[s][:, x], wp[s][:, 0, x], ALU.subtract).then_inc(w_split, 1)

            def pair(i, first=False, last=False):
                for c in range(2 * NCH):
                    for it in range(NI):
                        n = NI * c + it
                        product(i, n)
                        if n:
                            low(i, n - 1)
                        for q in out_tiles(it):
                            if c:
                                add(i, TPC * (c - 1) + q)
                            elif not first:
                                add(i - 1, TPC * (2 * NCH - 1) + q)
                        k = NI * (c % NCH - 1) + it
                        if 0 <= k < PIECES:
                            if c < NCH:
                                split(i, 1, k)
                            elif not last:
                                split(i + 1, 0, k)
                low(i, NU - 1)

            dve.tensor_copy(xp[:, 0, :, :], xt[:, :, :]).then_inc(x_high, 1)
            dve.wait_ge(x_high, 1)
            dve.tensor_tensor(xp[:, 1, :, :], xt[:, :, :], xp[:, 0, :, :], ALU.subtract).then_inc(x_split, 1)
            dve.wait_ge(w_loaded[0], 16)
            for k in range(PIECES):
                parts(0, k, 0)
            pair(0, first=True)
            with dve.Fori(1, NPAIR - 1) as i:
                pair(i)
            pair(NPAIR - 1, last=True)
            for q in range(TPC):
                add(NPAIR - 1, TPC * (2 * NCH - 1) + q)


def program(nc, a, out, stop=99, dump=None):
    a = dict(a)
    a["table"] = nc.dram_tensor("token_rows", (T, ROW), F32, kind="Internal").ap()
    a["acc"] = nc.dram_tensor("token_sums", (T, D), F32, kind="Internal").ap()
    rows_t = [P] * NT
    rows_s = tiles_of(S)

    FREE_SEMS.clear()
    FREE_SEMS.extend(sorted(nc.free_semaphores))
    top = ExitStack()
    with top:
        def sb(n, shape, dt=F32):
            return top.enter_context(nc.sbuf_tensor(n, shape, dt))

        def finish(t):
            c, _, _, sem = phase(nc, "finish")
            with c:
                stored = sem("stored")
                block = c.enter_context(nc.Block())

                @block.sync
                def _(sp):
                    sp.dma_start(out.rearrange("o (t p) d -> p (o t) d", p=P), t[:, :, :]).then_inc(stored, 16)
                    sp.wait_ge(stored, 16)

        cols, rows = sb("cols", [P, NCOLS]), sb("rows", [P, NROWS])
        ident, ones = sb("ident", [P, P]), sb("ones", [P, P])
        x = sb("x", [P, NT, D])
        a["ident"] = ident
        load_constants(nc, a, cols, rows, ident, ones, x)

        def col(n):
            o, k = COLS[n]
            return cols[:, o:o + k]

        def row(n):
            o, k = ROWS[n]
            return rows[:, o:o + k]

        def scope():
            c = ExitStack()
            return c, lambda n, shape, dt=F32: c.enter_context(nc.sbuf_tensor(n, shape, dt))

        c, sb1 = scope()
        with c:
            ot = sb1("ot_0", [P, NG, T])
            c2, sb2 = scope()
            with c2:
                ct, xt = sb2("ct_0", [P, 1, S]), sb2("xt_0", [P, KC, T])
                c3, sb3 = scope()
                with c3:
                    ctx_block(nc, a, "ctx_t", ct)
                    xn = sb3("xn_0", [P, NT, D])
                    layernorm(nc, "ln_0", x, xn, rows_t, D, outs=[(xt, None, None)], ident=ident)
                attention(nc, a, "xa0", a["wq0"], a["wk0"], a["wv0"], xt, KC, ct, 1, S, (D // HEADS) ** -0.5, False, ot, ones,
                          bq=col("bq0"), bk=col("bk0"), bv=row("bv0").rearrange("p (g n) -> p g n", n=P), ones_at=D // HEADS)
            project_out(nc, "out0", ot, a["wo0"], row("bo0"), x, x)
        if stop == 0:
            return finish(x)

        c, sb1 = scope()
        with c:
            slots = sb1("slots", [P, E0], U32)
            c2, sb2 = scope()
            with c2:
                z, wc, picks = sb2("z", [P, NT, D]), sb2("wc", [P, NT, E0]), sb2("picks", [E0, T])
                zt, zst = sb2("zt", [P, KC, T]), sb2("zst", [NSTAT, T])
                layernorm(nc, "ln_z", x, z, rows_t, D, outs=[(zt, None, None)], ident=ident)
                router_stats(nc, z, zst, ident)
                router(nc, a, zt, zst, col("r1b"), wc, picks, ident)
                choose(nc, a, picks, z, wc, x, slots, ident)
            experts(nc, a, slots, x, ident)
        if stop == 1:
            return finish(x)

        c, sb1 = scope()
        with c:
            r = x
            layernorm(nc, "ln_xx", x, r, rows_t, D)
            layernorm(nc, "ln1", r, r, rows_t, D, affine=(row("ln1_g"), row("ln1_b")))
            for n, p in enumerate(("a1", "a2")):
                if n == 1:
                    layernorm(nc, "ln2", r, r, rows_t, D, affine=(row("ln2_g"), row("ln2_b")))
                c2, sb2 = scope()
                with c2:
                    ot = sb2(f"{p}_ot", [P, NG, T])
                    c3, sb3 = scope()
                    with c3:
                        xq = sb3(f"{p}_xq", [P, KC, T])
                        if n == 0:
                            xk, nkk, nkeys = sb3(f"{p}_xk", [P, KC, T]), KC, T
                        else:
                            xk, nkk, nkeys = sb3(f"{p}_xk", [P, 1, S]), 1, S
                        c4, sb4 = scope()
                        with c4:
                            xn = sb4(f"{p}_xn", [P, NT, D])
                            outs = [(xq, col(p + "_lnx_g"), col(p + "_lnx_b"))]
                            if n == 0:
                                outs.append((xk, col(p + "_lny_g"), col(p + "_lny_b")))
                            layernorm(nc, p + "_lnx", r, xn, rows_t, D, outs=outs, ident=ident)
                        if n == 1:
                            c4, sb4 = scope()
                            with c4:
                                cr = sb4("ctx_rows", [P, len(rows_s), C])
                                load_ctx_rows(nc, a, cr)
                                layernorm(nc, p + "_lny", cr, cr, rows_s, C,
                                          outs=[(xk, col(p + "_lny_g"), col(p + "_lny_b"))], ident=ident)
                        attention(nc, a, p, a[p + "_wq"], a[p + "_wk"], a[p + "_wv"], xq, KC, xk, nkk, nkeys, SLOT ** -0.5, n == 0,
                                  ot, ones, ering=3 if n == 0 else 4)
                    xo = sb2(f"{p}_xo", [P, NT, D])
                    project_out(nc, p + "_out", ot, a[p + "_wo"], row(p + "_li1_b"), r, xo)
                    xt = sb2(f"{p}_xt", [P, KC, T])
                    c3, sb3 = scope()
                    with c3:
                        xn = sb3(f"{p}_xn3", [P, NT, D])
                        layernorm(nc, p + "_ln3", xo, xn, rows_t, D, outs=[(xt, col(p + "_ln3_g"), col(p + "_ln3_b"))], ident=ident)
                    adds = [r]
                    if n == 1:
                        adds.append(sb2("x2", [P, NT, D]))
                        load_tokens(nc, a["acc"], adds[1])
                    gelu_ffn(nc, p + "_ffn", xt, a[p + "_li2"], a[p + "_li3"], col(p + "_li2_b"), row(p + "_li3_b"), xo, adds, r)
                if stop == 2 + n:
                    return finish(r if n == 0 else x)

        xt, cw = sb("m_xt", [P, KC, T]), sb("cw", [P, NT, E1 + SH])
        c, sb1 = scope()
        with c:
            xn = sb1("m_xn", [P, NT, D])
            layernorm(nc, "m_ln", x, xn, rows_t, D, outs=[(xt, None, None)], ident=ident)
        gate1(nc, a, xt, row("gate_bias"), cw)
        moe(nc, a, xt, cw, x, out)


def ctx_block(nc, a, name, ct):
    ctx, sb, ps, sem = phase(nc, name)
    with ctx:
        loaded = sem("loaded")
        block = ctx.enter_context(nc.Block())

        @block.sync
        def _(sp):
            sp.dma_start(ct[:, 0, :], a["ctx_t"]).then_inc(loaded, 16)
            sp.wait_ge(loaded, 16)


def load_tokens(nc, source, target):
    ctx, sb, ps, sem = phase(nc, "tokens_in")
    with ctx:
        loaded = sem("loaded")
        block = ctx.enter_context(nc.Block())

        @block.sync
        def _(sp):
            sp.dma_start(target[:, :, :], source.rearrange("(t p) d -> p t d", p=P)).then_inc(loaded, 16)
            sp.wait_ge(loaded, 16)


def load_ctx_rows(nc, a, cr):
    ctx, sb, ps, sem = phase(nc, "ctx_rows_in")
    full = S // P
    with ctx:
        loaded = sem("loaded")
        block = ctx.enter_context(nc.Block())

        @block.sync
        def _(sp):
            sp.dma_start(cr[:, :full, :], a["ctx"][:full * P, :].rearrange("(t p) c -> p t c", p=P)).then_inc(loaded, 16)
            sp.dma_start(cr[:S - full * P, full, :], a["ctx"][full * P:, :]).then_inc(loaded, 16)
            sp.wait_ge(loaded, 32)


def laid_out(i):
    i = {k: np.asarray(v) for k, v in i.items()}

    def blocks(w):
        k, n = w.shape
        return w.reshape(k // P, P, n).transpose(1, 0, 2)

    def slots(w, heads_width):
        k = w.shape[0]
        o = np.zeros((k, HEADS, SLOT), np.float32)
        o[:, :, :heads_width] = w.reshape(k, HEADS, heads_width)
        return o.reshape(k, HEADS * SLOT)

    def grouped(w):
        k = w.shape[0]
        return w.reshape(k // P, P, NG, P).transpose(2, 1, 0, 3)

    dk = D // HEADS
    o = {"x": i["x"], "ctx": i["ctx_512"][0], "ctx_t": i["ctx_512"][0].T}
    o["wq0"] = grouped(slots(i["L0_xattn_Wq"], dk))
    o["wk0"] = grouped(slots(i["L0_xattn_Wk"], dk))
    o["wv0"] = grouped(slots(i["L0_xattn_Wv"], dk))
    o["wo0"] = blocks(slots(i["L0_xattn_Wo"].T, dk).T)
    o["r1"] = blocks(i["L0_ffn_r1_w"][:, :D].T)
    o["r1s"] = i["L0_ffn_r1_w"][:, D:].T
    o["r2"] = i["L0_ffn_r2_w"].T
    up = i["L0_ffn_w_up"].transpose(0, 2, 1).reshape(E0, KC, P, 2 * INTER).transpose(0, 2, 1, 3).reshape(E0, P, -1)
    dn = i["L0_ffn_w_down"].transpose(0, 2, 1).reshape(E0, INTER // P, P, D).transpose(0, 2, 1, 3).reshape(E0, P, -1)
    o["we"] = np.concatenate([up, dn], 2)
    up = i["L0_ffn_a_up"].transpose(0, 2, 1).reshape(AG, KC, P, 2 * AI).transpose(0, 2, 1, 3).reshape(AG, P, -1)
    o["aw"] = np.concatenate([up, i["L0_ffn_a_down"].transpose(0, 2, 1)], 2)
    for p in ("a1", "a2"):
        for n in "qkv":
            w = i[f"L1_xattn_{p}_w{n}"]
            o[f"{p}_w{n}"] = grouped(w.transpose(1, 0, 2).reshape(w.shape[1], HEADS * SLOT))
        o[p + "_wo"] = blocks(i[f"L1_xattn_{p}_li1_w"])
        o[p + "_li2"] = blocks(i[f"L1_xattn_{p}_li2_w"])
        o[p + "_li3"] = blocks(i[f"L1_xattn_{p}_li3_w"])
    o["gw"] = blocks(i["L1_ffn_gate_w"].T)
    gate = np.concatenate([i["L1_ffn_gate_proj"], i["L1_ffn_shared_gate_w"].reshape(SH, EI, D)])
    upw = np.concatenate([i["L1_ffn_up_proj"], i["L1_ffn_shared_up_w"].reshape(SH, EI, D)])
    down = np.concatenate([i["L1_ffn_down_proj"], i["L1_ffn_shared_down_w"].reshape(D, SH, EI).transpose(1, 0, 2)])
    n = E1 + SH
    gu = [w.transpose(0, 2, 1).reshape(n, KC, P, EI).transpose(0, 2, 1, 3).reshape(n, P, -1) for w in (gate, upw)]
    ni = (EI + P - 1) // P
    dn = np.zeros((n, ni * P, D), np.float32)
    dn[:, :EI] = down.transpose(0, 2, 1)
    o["wm"] = np.concatenate([*gu, dn.reshape(n, ni, P, D).transpose(0, 2, 1, 3).reshape(n, P, -1)], 2)
    vec = {"bq0": slots(i["L0_xattn_bq"][None], dk)[0], "bk0": slots(i["L0_xattn_bk"][None], dk)[0], "r1b": i["L0_ffn_r1_b"],
           "bo0": i["L0_xattn_bo"], "bv0": slots(i["L0_xattn_bv"][None], dk)[0], "gate_bias": i["L1_ffn_gate_bias"]}
    vec["bv0"][dk::SLOT] = 1.0
    for n in ("ln1_g", "ln1_b", "ln2_g", "ln2_b"):
        vec[n] = i["L1_xattn_" + n]
    for n in list(COLS) + list(ROWS):
        if n not in vec:
            vec[n] = i["L1_xattn_" + n]
    o["cols"] = np.concatenate([vec[n].reshape(-1, P).T for n in COLS], 1)
    o["rows"] = np.concatenate([vec[n] for n in ROWS])[None]
    return {k: np.ascontiguousarray(v) for k, v in o.items()}


def kernel(**inputs):
    import concourse.bacc as bacc
    from concourse.bass_utils import run_bass_kernel_spmd

    arrays = {f"in_{k}": v for k, v in laid_out(inputs).items()}
    nc = bacc.Bacc("TRN2", target_bir_lowering=False, num_devices=1)
    a = {k[3:]: nc.dram_tensor(k, v.shape, mybir.dt.from_np(v.dtype), kind="ExternalInput").ap() for k, v in arrays.items()}
    out = nc.dram_tensor("out_x", (1, T, D), F32, kind="ExternalOutput").ap()
    program(nc, a, out)
    r = run_bass_kernel_spmd(nc, [arrays], core_ids=[0])
    return r.results[0]["out_x"]
```
